# Optimizing a Trainium2 kernel written in Bass

```python
import numpy as np
import jax
import jax.numpy as jnp

def _softmax(x, axis=-1):
    return jax.nn.softmax(x, axis=axis)

def _gelu(x):
    return jax.nn.gelu(x, approximate=True)

def _silu(x):
    return jax.nn.silu(x)

def _sigmoid(x):
    return jax.nn.sigmoid(x)

def _layernorm(x, axis=-1, eps=1e-05):
    m = jnp.mean(x, axis=axis, keepdims=True)
    v = jnp.var(x, axis=axis, keepdims=True)
    return (x - m) / jnp.sqrt(v + eps)

def _scatter_add(tgt, idx, src, axis=0):
    return tgt.at[idx].add(src)

def _segment_sum(src, seg, n):
    return jax.ops.segment_sum(src, seg, n)
kernel_name = 'mk_xattn_ffn_d2_seqx_r4_9e0bf3'

def setup_inputs(seed: int=0):
    np.random.seed(seed)
    _w = jnp.asarray

    def _rec_inputs():
        import jax
        import jax.numpy as jnp
        _rk = jax.random.key(seed)
        x = -0.0003929 + 0.9999 * jax.random.normal(jax.random.fold_in(_rk, 1), (8, 256, 512), jnp.float32)
        _lenS = 256 - jax.random.randint(jax.random.fold_in(_rk, 7), (8,), 0, max(1, 256 // 4) + 1, jnp.int32)
        _lenS2 = 256 - jax.random.randint(jax.random.fold_in(_rk, 8), (8,), 0, max(1, 256 // 4) + 1, jnp.int32)
        _ctx_1024P = jax.random.normal(jax.random.fold_in(_rk, 11), (8, 16, 256), jnp.float32)
        _ctx_1024c = jax.random.dirichlet(jax.random.fold_in(_rk, 511), 0.3 * jnp.ones((16,), jnp.float32), (8, 256))
        _ctx_1024t = jnp.einsum('bsk,bkd->bsd', _ctx_1024c, _ctx_1024P)
        _ctx_1024t = _ctx_1024t * jax.lax.rsqrt(jnp.mean(jnp.square(_ctx_1024t)) + 1e-12) * 0.953939
        ctx_1024 = -0.000494167 + 1.00018 * (_ctx_1024t + 0.3 * jax.random.normal(jax.random.fold_in(_rk, 611), (8, 256, 256), jnp.float32))
        _validS = jnp.arange(256)[None, :] < _lenS[:, None]
        _validS2 = jnp.arange(256)[None, :] < _lenS2[:, None]
        _causal = jnp.tril(jnp.ones((256, 256), dtype=bool))
        mask_BxS2_bf1 = jnp.ones((8, 256), dtype=bool)
        return (x, ctx_1024, mask_BxS2_bf1)
    x, ctx_1024, mask_BxS2_bf1 = _rec_inputs()

    def _L0_xattn_setup():
        import jax, jax.numpy as jnp
        import numpy as np
        N_HEADS = 16
        N_KV_HEADS = 8
        HEAD_DIM = 128
        D_TEXT = 512
        D_VISION = 256
        GROUPS = N_HEADS // N_KV_HEADS
        key = jax.random.key(seed)
        ks = jax.random.split(key, 6)
        B, T_text, T_vis = (4, 512, 144)
        text_hidden = jax.random.normal(ks[0], (B, T_text, D_TEXT), dtype=jnp.float32)
        vision_tokens = jax.random.normal(ks[1], (B, T_vis, D_VISION), dtype=jnp.float32)
        vision_mask = jnp.ones((B, T_vis), dtype=bool)
        s = 0.02
        Wq = jax.random.normal(ks[2], (D_TEXT, N_HEADS * HEAD_DIM), dtype=jnp.float32) * s
        Wk = jax.random.normal(ks[3], (D_VISION, N_KV_HEADS * HEAD_DIM), dtype=jnp.float32) * s
        Wv = jax.random.normal(ks[4], (D_VISION, N_KV_HEADS * HEAD_DIM), dtype=jnp.float32) * s
        Wo = jax.random.normal(ks[5], (N_HEADS * HEAD_DIM, D_TEXT), dtype=jnp.float32) * s
        return {'text_hidden': text_hidden, 'vision_tokens': vision_tokens, 'vision_mask': vision_mask, 'Wq': Wq, 'Wk': Wk, 'Wv': Wv, 'Wo': Wo}
    _L0_xattn_all = _L0_xattn_setup()
    _L0_xattn_in = {k: v for k, v in _L0_xattn_all.items() if k in ('Wq', 'Wk', 'Wv', 'Wo')}
    del _L0_xattn_all

    def _L0_ffn_setup():
        import jax, jax.numpy as jnp
        import numpy as np
        B, S, H, I = (1, 64, 512, 1536)

        def _quantized_matmul(x, w, scale):
            wq = w.astype(jnp.float8_e4m3fn).astype(x.dtype)
            y = jnp.einsum('bsi,io->bso', x, wq)
            return y * scale
        key = jax.random.key(seed)
        ks = jax.random.split(key, 7)
        return {'x': jax.random.normal(ks[0], (B, S, H), dtype=jnp.float32), 'gate_w': jax.random.normal(ks[1], (H, I), dtype=jnp.float32) * 0.02, 'up_w': jax.random.normal(ks[2], (H, I), dtype=jnp.float32) * 0.02, 'down_w': jax.random.normal(ks[3], (I, H), dtype=jnp.float32) * 0.02, 'gate_scale': jax.random.uniform(ks[4], (I,), dtype=jnp.float32, minval=0.5, maxval=1.5), 'up_scale': jax.random.uniform(ks[5], (I,), dtype=jnp.float32, minval=0.5, maxval=1.5), 'down_scale': jax.random.uniform(ks[6], (H,), dtype=jnp.float32, minval=0.5, maxval=1.5)}
    _L0_ffn_all = _L0_ffn_setup()
    _L0_ffn_in = {k: v for k, v in _L0_ffn_all.items() if k in ('gate_w', 'up_w', 'down_w', 'gate_scale', 'up_scale', 'down_scale')}
    del _L0_ffn_all

    def _L1_xattn_setup():
        import jax, jax.numpy as jnp
        import numpy as np
        EPS = 1e-05

        def rmsnorm(x, g, eps=EPS):
            var = jnp.mean(jnp.square(x), axis=-1, keepdims=True)
            return x * jax.lax.rsqrt(var + eps) * g
        key = jax.random.key(seed)
        ks = jax.random.split(key, 8)
        B, Sq, Skv = (2, 1024, 128)
        dim, cdim, H, D = (512, 256, 16, 128)
        inner = H * D
        s = lambda f: 1.0 / np.sqrt(f)
        return {'hidden_states': jax.random.normal(ks[0], (B, Sq, dim), jnp.float32), 'encoder_hidden_states': jax.random.normal(ks[1], (B, Skv, cdim), jnp.float32), 'Wq': jax.random.normal(ks[2], (dim, inner), jnp.float32) * s(dim), 'Wk': jax.random.normal(ks[3], (cdim, inner), jnp.float32) * s(cdim), 'Wv': jax.random.normal(ks[4], (cdim, inner), jnp.float32) * s(cdim), 'Wo': jax.random.normal(ks[5], (inner, dim), jnp.float32) * s(inner), 'gq': jnp.ones((D,), jnp.float32), 'gk': jnp.ones((D,), jnp.float32)}
    _L1_xattn_all = _L1_xattn_setup()
    _L1_xattn_in = {k: v for k, v in _L1_xattn_all.items() if k in ('Wq', 'Wk', 'Wv', 'Wo', 'gq', 'gk')}
    del _L1_xattn_all

    def _L1_ffn_setup():
        import jax, jax.numpy as jnp
        import numpy as np
        B, S, H, E, I, TOPK = (1, 256, 512, 16, 256, 2)
        SCALE = 1.0
        key = jax.random.key(seed)
        k0, k1, k2, k3 = jax.random.split(key, 4)
        hidden_states = jax.random.normal(k0, (B, S, H), dtype=jnp.float32)
        gate_w = jax.random.normal(k1, (E, H), dtype=jnp.float32) * 0.02
        gate_up_proj = jax.random.normal(k2, (E, H, 2 * I), dtype=jnp.float32) / np.sqrt(H)
        down_proj = jax.random.normal(k3, (E, I, H), dtype=jnp.float32) / np.sqrt(I)
        return {'hidden_states': hidden_states, 'gate_w': gate_w, 'gate_up_proj': gate_up_proj, 'down_proj': down_proj}
    _L1_ffn_all = _L1_ffn_setup()
    _L1_ffn_in = {k: v for k, v in _L1_ffn_all.items() if k in ('gate_w', 'gate_up_proj', 'down_proj')}
    del _L1_ffn_all
    return {'x': x, 'ctx_1024': ctx_1024, 'mask_BxS2_bf1': mask_BxS2_bf1, 'L0_xattn_Wq': _L0_xattn_in['Wq'], 'L0_xattn_Wk': _L0_xattn_in['Wk'], 'L0_xattn_Wv': _L0_xattn_in['Wv'], 'L0_xattn_Wo': _L0_xattn_in['Wo'], 'L0_ffn_gate_w': _L0_ffn_in['gate_w'], 'L0_ffn_up_w': _L0_ffn_in['up_w'], 'L0_ffn_down_w': _L0_ffn_in['down_w'], 'L0_ffn_gate_scale': _L0_ffn_in['gate_scale'], 'L0_ffn_up_scale': _L0_ffn_in['up_scale'], 'L0_ffn_down_scale': _L0_ffn_in['down_scale'], 'L1_xattn_Wq': _L1_xattn_in['Wq'], 'L1_xattn_Wk': _L1_xattn_in['Wk'], 'L1_xattn_Wv': _L1_xattn_in['Wv'], 'L1_xattn_Wo': _L1_xattn_in['Wo'], 'L1_xattn_gq': _L1_xattn_in['gq'], 'L1_xattn_gk': _L1_xattn_in['gk'], 'L1_ffn_gate_w': _L1_ffn_in['gate_w'], 'L1_ffn_gate_up_proj': _L1_ffn_in['gate_up_proj'], 'L1_ffn_down_proj': _L1_ffn_in['down_proj']}

def reference(x, ctx_1024, mask_BxS2_bf1, L0_xattn_Wq, L0_xattn_Wk, L0_xattn_Wv, L0_xattn_Wo, L0_ffn_gate_w, L0_ffn_up_w, L0_ffn_down_w, L0_ffn_gate_scale, L0_ffn_up_scale, L0_ffn_down_scale, L1_xattn_Wq, L1_xattn_Wk, L1_xattn_Wv, L1_xattn_Wo, L1_xattn_gq, L1_xattn_gk, L1_ffn_gate_w, L1_ffn_gate_up_proj, L1_ffn_down_proj):
    import jax
    import jax.numpy as jnp

    def _L0_xattn_ref(text_hidden, vision_tokens, vision_mask, Wq, Wk, Wv, Wo):
        import jax, jax.numpy as jnp
        import numpy as np
        N_HEADS = 16
        N_KV_HEADS = 8
        HEAD_DIM = 128
        D_TEXT = 512
        D_VISION = 256
        GROUPS = N_HEADS // N_KV_HEADS
        B, T_text, _ = text_hidden.shape
        T_vis = vision_tokens.shape[1]
        scale = jnp.float32(np.sqrt(HEAD_DIM))
        q = (text_hidden @ Wq).reshape(B, T_text, N_HEADS, HEAD_DIM).transpose(0, 2, 1, 3)
        k = (vision_tokens @ Wk).reshape(B, T_vis, N_KV_HEADS, HEAD_DIM).transpose(0, 2, 1, 3)
        v = (vision_tokens @ Wv).reshape(B, T_vis, N_KV_HEADS, HEAD_DIM).transpose(0, 2, 1, 3)
        k = jnp.repeat(k, GROUPS, axis=1)
        v = jnp.repeat(v, GROUPS, axis=1)
        scores = jnp.einsum('bhtd,bhsd->bhts', q, k) / scale
        mask = vision_mask[:, None, None, :]
        scores = jnp.where(mask, scores, -jnp.inf)
        attn = jax.nn.softmax(scores, axis=-1)
        attn = jnp.nan_to_num(attn, nan=0.0)
        out = jnp.einsum('bhts,bhsd->bhtd', attn, v)
        out = out.transpose(0, 2, 1, 3).reshape(B, T_text, N_HEADS * HEAD_DIM)
        return out @ Wo

    def _L0_ffn_ref(x, gate_w, up_w, down_w, gate_scale, up_scale, down_scale):
        import jax, jax.numpy as jnp
        import numpy as np
        B, S, H, I = (1, 64, 512, 1536)

        def _quantized_matmul(x, w, scale):
            wq = w.astype(jnp.float8_e4m3fn).astype(x.dtype)
            y = jnp.einsum('bsi,io->bso', x, wq)
            return y * scale
        gate = jax.nn.silu(_quantized_matmul(x, gate_w, gate_scale))
        up = _quantized_matmul(x, up_w, up_scale)
        fuse = gate * up
        return _quantized_matmul(fuse, down_w, down_scale)

    def _L1_xattn_ref(hidden_states, encoder_hidden_states, Wq, Wk, Wv, Wo, gq, gk):
        import jax, jax.numpy as jnp
        import numpy as np
        EPS = 1e-05

        def rmsnorm(x, g, eps=EPS):
            var = jnp.mean(jnp.square(x), axis=-1, keepdims=True)
            return x * jax.lax.rsqrt(var + eps) * g
        B, Sq, _ = hidden_states.shape
        Skv = encoder_hidden_states.shape[1]
        D = gq.shape[0]
        H = Wq.shape[1] // D
        scale = 1.0 / np.sqrt(D)
        q = (hidden_states @ Wq).reshape(B, Sq, H, D)
        k = (encoder_hidden_states @ Wk).reshape(B, Skv, H, D)
        v = (encoder_hidden_states @ Wv).reshape(B, Skv, H, D)
        q = rmsnorm(q, gq)
        k = rmsnorm(k, gk)
        scores = jnp.einsum('bqhd,bkhd->bhqk', q, k) * scale
        attn = jax.nn.softmax(scores, axis=-1)
        out = jnp.einsum('bhqk,bkhd->bqhd', attn, v)
        out = out.reshape(B, Sq, H * D)
        return out @ Wo

    def _L1_ffn_ref(hidden_states, gate_w, gate_up_proj, down_proj):
        import jax, jax.numpy as jnp
        import numpy as np
        B, S, H, E, I, TOPK = (1, 256, 512, 16, 256, 2)
        SCALE = 1.0
        b, s, h = hidden_states.shape
        e = gate_w.shape[0]
        x = hidden_states.reshape(-1, h)
        logits = jnp.matmul(x.astype(jnp.float32), gate_w.T.astype(jnp.float32))
        p = jax.nn.sigmoid(logits)
        p = p / jnp.sum(p, axis=-1, keepdims=True)
        w, idx = jax.lax.top_k(p, TOPK)
        w = w / jnp.sum(w, axis=-1, keepdims=True)
        w = w * SCALE
        combine = jnp.sum(jax.nn.one_hot(idx, e, dtype=w.dtype) * w[..., None], axis=1)
        gu = jnp.einsum('th,ehf->etf', x, gate_up_proj)
        gate, up = jnp.split(gu, 2, axis=-1)
        inter = jax.nn.silu(gate) * up
        y = jnp.einsum('eti,eih->eth', inter, down_proj)
        out = jnp.einsum('eth,te->th', y, combine.astype(y.dtype))
        return out.reshape(b, s, h)
    x = x + _L0_xattn_ref(_layernorm(x, axis=-1), ctx_1024, mask_BxS2_bf1, L0_xattn_Wq, L0_xattn_Wk, L0_xattn_Wv, L0_xattn_Wo)
    x = x + _L0_ffn_ref(_layernorm(x, axis=-1), L0_ffn_gate_w, L0_ffn_up_w, L0_ffn_down_w, L0_ffn_gate_scale, L0_ffn_up_scale, L0_ffn_down_scale)
    x = x + _L1_xattn_ref(_layernorm(x, axis=-1), ctx_1024, L1_xattn_Wq, L1_xattn_Wk, L1_xattn_Wv, L1_xattn_Wo, L1_xattn_gq, L1_xattn_gk)
    x = x + _L1_ffn_ref(_layernorm(x, axis=-1), L1_ffn_gate_w, L1_ffn_gate_up_proj, L1_ffn_down_proj)
    return x

_drawn_inputs = setup_inputs


def setup_inputs(seed=0):
    import zlib

    import numpy as np

    out = dict(_drawn_inputs(seed))
    spreads = {'L1_xattn_gq': (1.0, 0.2), 'L1_xattn_gk': (1.0, 0.2)}
    factors = {}
    for name, (base, spread) in spreads.items():
        noise = np.random.default_rng([zlib.crc32(name.encode()), seed]).standard_normal(out[name].shape)
        drawn = base * np.exp(spread * noise) if base else spread * noise
        out[name] = jnp.asarray(drawn.astype(out[name].dtype))
    for name, factor in factors.items():
        out[name] = (out[name] * factor).astype(out[name].dtype)
    return out
```

```python
from contextlib import ExitStack

import concourse.bass as bass
from concourse import mybir

ALU = mybir.AluOpType
ACT = mybir.ActivationFunctionType
AX = mybir.AxisListType
F32 = mybir.dt.float32
F32R = mybir.dt.float32r
BF16 = mybir.dt.bfloat16
I32 = mybir.dt.int32
U32 = mybir.dt.uint32
U8 = mybir.dt.uint8

P = 128
B, S, D = 8, 256, 512
C = 256
T = B * S
NT = T // P
KD, KC = D // P, C // P
GT = 512
NG = T // GT
TG = GT // P
NH, HD = 16, 128
HB = 2
NHG = NH // HB
UN = HB * 2
F = 1536
NF = F // P
E, I = 16, 256
EPS = 1e-5
SM_SCALE = float(HD) ** -0.5
MASKED = -1e30
MAX_FLOOR = -1e29
RSQRT_SEED = float(0x5F3759DF)


def rsqrt_steps(eng, y, tmp, v, step, apart=lambda: None):
    apart()
    step(eng.tensor_scalar(y.bitcast(I32), v.bitcast(I32), -0.5, RSQRT_SEED, ALU.mult, ALU.add))
    for _ in range(3):
        step(eng.tensor_tensor(tmp, y, y, ALU.mult))
        step(eng.tensor_tensor(tmp, tmp, v, ALU.mult))
        apart()
        step(eng.tensor_scalar(tmp, tmp, -0.5, 1.5, ALU.mult, ALU.add))
        step(eng.tensor_tensor(y, y, tmp, ALU.mult))


RSQRT_STEPS = 13


def apart(k, eng):
    eng.sem_inc(k.wait_over, 1)


class Parts:
    pass


def load_stage(k, x, ctx_in):
    nc, banks = k.nc, k.banks
    with ExitStack() as st:
        c_sb = st.enter_context(nc.sbuf_tensor("c_sb", [P, NT, C], F32))
        ct = [st.enter_context(nc.sbuf_tensor(f"ct{i}", [P, 2, KC, GT], F32R)) for i in range(2)]
        zero = st.enter_context(nc.sbuf_tensor("zero", [P, P], F32))
        block = st.enter_context(nc.Block())
        ident_made = k.ident_made
        x_in, c_loaded, c_turned, c_hi, c_lo = (k.sem(n) for n in ("x_in", "c_loaded", "c_turned", "c_hi", "c_lo"))
        c_stored = [k.sem(f"c_stored{i}") for i in range(2)]

        @block.sync
        def _(sp):
            sp.dma_start(c_sb[:, :, :], ctx_in.rearrange("b (t p) d -> p (b t) d", p=P)).then_inc(c_loaded, 16)
            xv = x.rearrange("b (t p) d -> p (b t) d", p=P)
            for g in range(NG):
                sp.dma_start(k.x_sb[:, TG * g:TG * (g + 1), :], xv[:, TG * g:TG * (g + 1), :]).then_inc(x_in, 16)
            for g in range(NG):
                sp.wait_ge(c_lo, KC * (g + 1))
                sp.dma_start(k.ctx_split[g], ct[g % 2][:, :, :, :].rearrange("p a k t -> p (a k t)").bitcast(F32)).then_inc(c_stored[g % 2], 16)
            sp.wait_ge(x_in, 16 * NG)
            for stored in c_stored:
                sp.wait_ge(stored, 16 * NG // 2)

        @block.gpsimd
        def _(pool):
            nc.gpsimd.memset(zero[:, :], 0.0).then_inc(ident_made, 1)
            pool.wait_ge(ident_made, 1)
            nc.gpsimd.affine_select(out=k.ident[:, :], in_=zero[:, :], compare_op=ALU.not_equal, fill=1.0, base=0,
                                    pattern=[[-1, P]], channel_multiplier=1).then_inc(ident_made, 1)

        @block.tensor
        def _(pe):
            pe.wait_ge(ident_made, 2)
            pe.wait_ge(c_loaded, 16)
            for g in range(NG):
                for c in range(KC):
                    if g >= 2:
                        pe.wait_ge(c_lo, KC * (g - 2) + c + 1)
                    for j in range(TG):
                        mm = nc.tensor.transpose(banks[KC * (g % 2) + c][:, P * j:P * (j + 1)],
                                                 c_sb[:, TG * g + j, P * c:P * (c + 1)], k.ident[:, :])
                    mm.then_inc(c_turned, 1)

        @block.scalar
        def _(act):
            for g in range(NG):
                if g >= 2:
                    act.wait_ge(c_stored[g % 2], 16 * (g // 2))
                for c in range(KC):
                    act.wait_ge(c_turned, KC * g + c + 1)
                    nc.scalar.copy(ct[g % 2][:, 0, c, :], banks[KC * (g % 2) + c][:, :]).then_inc(c_hi, 1)

        @block.vector
        def _(dve):
            for g in range(NG):
                for c in range(KC):
                    dve.wait_ge(c_hi, KC * g + c + 1)
                    nc.vector.tensor_tensor(ct[g % 2][:, 1, c, :], banks[KC * (g % 2) + c][:, :],
                                            ct[g % 2][:, 0, c, :].bitcast(F32), ALU.subtract).then_inc(c_lo, 1)


def layernorm_stage(k):
    nc, banks = k.nc, k.banks
    turn = k.ln_calls
    k.ln_calls += 1
    steps = 2 * TG + 1 + RSQRT_STEPS
    with ExitStack() as st:
        xn = [st.enter_context(nc.sbuf_tensor(f"xn{turn}_{j}", [P, D], F32)) for j in range(TG)]
        stats = st.enter_context(nc.sbuf_tensor(f"ln_stats{turn}", [P, TG, 6], F32))
        mv = st.enter_context(nc.sbuf_tensor(f"ln_mv{turn}", [P, TG, 2], F32))
        var = st.enter_context(nc.sbuf_tensor(f"ln_var{turn}", [P, TG], F32))
        rstd = st.enter_context(nc.sbuf_tensor(f"ln_rstd{turn}", [P, TG], F32))
        tmp = st.enter_context(nc.sbuf_tensor(f"ln_tmp{turn}", [P, TG], F32))
        block = st.enter_context(nc.Block())
        chain, normed, turned, hi_done, lo_done = k.ln_sems

        @block.vector
        def _(dve):
            with dve.Fori(0, NG) as g:
                done = [0]

                def step(ins, wait=True):
                    ins.then_inc(chain, 1)
                    done[0] += 1
                    if wait:
                        dve.wait_ge(chain, g * steps + (turn * NG * steps + done[0]))

                for j in range(TG):
                    step(nc.vector.bn_stats(stats[:, j, :], k.x_sb[:, bass.ds(g * TG + j, 1), :]), j == TG - 1)
                apart(k, dve)
                for j in range(TG):
                    step(nc.vector.bn_aggr(mv[:, j, :], stats[:, j, :]), j == TG - 1)
                step(nc.vector.tensor_scalar(var[:, :], mv[:, :, 1], EPS, None, ALU.add))
                rsqrt_steps(nc.vector, rstd[:, :], tmp[:, :], var[:, :], step)
                for j in range(TG):
                    nc.vector.tensor_scalar(xn[j][:, :], k.x_sb[:, bass.ds(g * TG + j, 1), :], mv[:, j, 0:1],
                                            rstd[:, j:j + 1], ALU.subtract, ALU.mult).then_inc(normed, 1)
                for j in range(TG):
                    at = bass.ds(g * GT + P * j, P)
                    dve.wait_ge(hi_done, g * TG + (turn * NT + j + 1))
                    nc.vector.tensor_tensor(k.xnT_lo[:, :, at], banks[j][:, :].rearrange("p (k t) -> p k t", k=KD),
                                            k.xnT_hi[:, :, at].bitcast(F32), ALU.subtract).then_inc(lo_done, 1)

        @block.tensor
        def _(pe):
            with pe.Fori(0, NG) as g:
                for j in range(TG):
                    pe.wait_ge(normed, g * TG + (turn * NT + j + 1))
                    for c in range(KD):
                        mm = nc.tensor.transpose(banks[j][:, P * c:P * (c + 1)], xn[j][:, P * c:P * (c + 1)], k.ident[:, :])
                    mm.then_inc(turned, 1)

        @block.scalar
        def _(act):
            with act.Fori(0, NG) as g:
                for j in range(TG):
                    act.wait_ge(turned, g * TG + (turn * NT + j + 1))
                    nc.scalar.copy(k.xnT_hi[:, :, bass.ds(g * GT + P * j, P)],
                                   banks[j][:, :].rearrange("p (k t) -> p k t", k=KD)).then_inc(hi_done, 1)


def attention_stage(k, name, Wq, Wk, Wv, Wo, mask=None, gq=None, gk=None):
    nc, banks = k.nc, k.banks
    rms = gq is not None
    nkv = HB if rms else 1
    kvw = nkv * HD
    b_q, b_kv, b_s, b_pt, b_o = banks[0:2], banks[2:4], banks[4:6], banks[6], banks[7]
    wq_v = Wq.rearrange("(k p) n -> p k n", p=P)
    wk_v = Wk.rearrange("(k p) n -> p k n", p=P)
    wv_v = Wv.rearrange("(k p) n -> p k n", p=P)
    wo_v = Wo.rearrange("(h p) n -> p h n", p=P)

    with ExitStack() as st:
        def sb(n, shape, dt=F32):
            return st.enter_context(nc.sbuf_tensor(f"{name}_{n}", shape, dt))

        def pair(n, shape):
            return [sb(f"{n}_hi", shape, F32R), sb(f"{n}_lo", shape, F32R)]

        def sem(n):
            return k.sem(f"{name}_{n}")

        wq, wkv, wo = pair("wq", [P, KD, HB * HD]), pair("wkv", [P, KC, 2 * kvw]), pair("wo", [P, HB, D])
        raw_a = sb("raw_a", [P, KD * HB * HD])
        raw_b = sb("raw_b", [P, KC, 2 * kvw])
        ctxT = [sb(f"ctxT{i}", [P, 2, KC, GT], F32R) for i in range(2)]
        qT = [pair(f"qT{h}", [P, GT]) for h in range(HB)]
        kT = [pair(f"kT{h}", [P, GT]) for h in range(nkv)]
        v = [pair(f"v{i}", [P, TG, kvw]) for i in range(2)]
        kn = sb("kn", [P, TG, kvw])
        probs = [sb(f"probs{i}", [P, 2, S]) for i in range(2)]
        pT = pair("pT", [P, 2, S])
        oT = [pair(f"oT{h}", [P, GT]) for h in range(HB)]
        mx, nbias, rsum, rden = (sb(n, [P, 2 * UN]) for n in ("mx", "nbias", "rsum", "rden"))
        if rms:
            q2 = [sb(f"q2_{h}", [P, GT]) for h in range(HB)]
            k2 = sb("k2", [P, TG, kvw])
            nk, nq = TG * nkv, TG * HB
            sums, var, rr, tmp = (sb(n, [P, nk + nq]) for n in ("sums", "var", "rr", "tmp"))
            gain_in = sb("gain_in", [P, 2])
            gain = sb("gain", [P, 1])
            ones = sb("ones", [P, 1])
        else:
            mask_u8 = sb("mask_u8", [P, T // 2], U8)
            mask_bias = sb("mask_bias", [P, T], BF16)
            scored = [sb(f"scored{i}", [P, 2, S]) for i in range(2)]
        block = st.enter_context(nc.Block())

        wq_in, wkv_in, wo_in, const_in = (sem(n) for n in ("wq_in", "wkv_in", "wo_in", "const_in"))
        ctx_in = [sem(f"ctx_in{i}") for i in range(2)]
        wq_split, wkv_split, wo_split, p_normed, k_ready = (sem(n) for n in ("wq_split", "wkv_split", "wo_split", "p_normed", "k_ready"))
        pool_chain, pool_w = sem("pool_chain"), sem("pool_w")
        q_made, kv_made, k_turned, s_made, p_turned, pv_made, y_made, qsum_made = (
            sem(n) for n in ("q_made", "kv_made", "k_turned", "s_made", "p_turned", "pv_made", "y_made", "qsum_made"))
        q_hi, q_sq, kv_hi, kT_hi, exp_done, pT_hi, o_hi = (sem(n) for n in ("q_hi", "q_sq", "kv_hi", "kT_hi", "exp_done", "pT_hi", "o_hi"))
        q_split, kv_split, kT_split, pT_split, o_split, bias_done, rden_done, y_added, sums_done, dve_chain = (
            sem(n) for n in ("q_split", "kv_split", "kT_split", "pT_split", "o_split", "bias_done", "rden_done", "y_added",
                             "sums_done", "dve_chain"))
        if rms:
            k_squared = sem("k_squared")
        else:
            den_chain = sem("den_chain")

        def count(per_body, extra, hg, g):
            return hg * (NG * per_body) + (g * per_body + extra)

        PROLOGUE = (0, -1)

        @block.sync
        def _(sp):
            def load_wq(hg):
                sp.dma_start(raw_a[:, :].rearrange("p (k n) -> p k n", k=KD), wq_v[:, :, bass.ds(hg * (HB * HD), HB * HD)]).then_inc(wq_in, 16)

            def load_wkv(hg):
                at = bass.ds(hg * kvw, kvw)
                sp.dma_start(raw_b[:, :, 0:kvw], wk_v[:, :, at]).then_inc(wkv_in, 16)
                sp.dma_start(raw_b[:, :, kvw:2 * kvw], wv_v[:, :, at]).then_inc(wkv_in, 16)

            def load_ctx(m):
                sp.dma_start(ctxT[m % 2][:, :, :, :].rearrange("p a k t -> p (a k t)").bitcast(F32), k.ctx_split[m % NG]).then_inc(ctx_in[m % 2], 16)

            load_wq(0)
            load_wkv(0)
            load_ctx(0)
            load_ctx(1)
            if rms:
                sp.dma_start(gain_in[:, 0:1], gq.rearrange("(p a) -> p a", a=1)).then_inc(const_in, 16)
                sp.dma_start(gain_in[:, 1:2], gk.rearrange("(p a) -> p a", a=1)).then_inc(const_in, 16)
            else:
                flat = mask.rearrange("(a b) s -> a (b s)", a=2)
                sp.dma_start(mask_u8[:, :], flat[0:1, :].broadcast_to([P, T // 2])).then_inc(const_in, 16)
                sp.wait_ge(dve_chain, 1)
                sp.dma_start(mask_u8[:, :], flat[1:2, :].broadcast_to([P, T // 2])).then_inc(const_in, 16)
            with sp.Fori(0, NHG) as hg:
                sp.wait_ge(wq_split, hg + 1)
                sp.dma_start(raw_a[:, :].rearrange("p (h n) -> p h n", h=HB), wo_v[:, bass.ds(hg * HB, HB), :]).then_inc(wo_in, 16)
                sp.wait_ge(wkv_split, hg + 1)
                load_wkv((hg + 1) % NHG)
                for g in range(NG):
                    sp.wait_ge(kv_made, count(TG, TG, hg, g))
                    load_ctx(g + 2)
                    if g == 0:
                        sp.wait_ge(wo_split, hg + 1)
                        load_wq((hg + 1) % NHG)
            for loaded in ctx_in:
                sp.wait_ge(loaded, 16 * (NHG * NG + 2) // 2)
            sp.wait_ge(wkv_in, 32 * (NHG + 1))
            sp.wait_ge(wq_in, 16 * (NHG + 1))

        @block.gpsimd
        def _(pool):
            gp = nc.gpsimd

            def split(w, raw, arrived, level, w_count, free=None):
                pool.wait_ge(arrived, level)
                if free is not None:
                    pool.wait_ge(*free)
                apart(k, pool)
                gp.tensor_copy(w[0], raw).then_inc(pool_w, 1)
                return lambda done: (pool.wait_ge(pool_w, w_count),
                                     gp.tensor_tensor(w[1], raw, w[0].bitcast(F32), ALU.subtract).then_inc(done, 1))

            wq_p = [t[:, :, :].rearrange("p k n -> p (k n)") for t in wq]
            wkv_p = [t[:, :, :] for t in wkv]
            wo_p = [t[:, :, :].rearrange("p h n -> p (h n)") for t in wo]
            norm_steps = 1 + RSQRT_STEPS

            def norm_keys(hg, g):
                done = [0]

                def step(ins):
                    ins.then_inc(pool_chain, 1)
                    done[0] += 1
                    pool.wait_ge(pool_chain, count(norm_steps, norm_steps + done[0], hg, g))

                pool.wait_ge(kv_hi, count(TG, 2 * TG, hg, g))
                gp.tensor_tensor(k2[:, :, :], kn[:, :, :], kn[:, :, :], ALU.mult).then_inc(k_squared, 1)
                pool.wait_ge(sums_done, count(2, 4, hg, g))
                apart(k, pool)
                step(gp.tensor_scalar(var[:, :], sums[:, :], 1.0 / HD, EPS, ALU.mult, ALU.add))
                rsqrt_steps(gp, rr[:, :], tmp[:, :], var[:, :], step, lambda: apart(k, pool))
                kn3 = kn[:, :, :].rearrange("p t (h d) -> p (t h) d", d=HD)
                scale = rr[:, 0:nk].rearrange("p (a b) -> p a b", b=1).broadcast_to([P, nk, HD])
                gp.tensor_tensor(kn3, kn3, scale, ALU.mult).then_inc(k_ready, 1)

            if rms:
                gp.memset(ones[:, :], 1.0).then_inc(const_in, 1)
            split(wq_p, raw_a[:, :], wq_in, 16, 1)(wq_split)
            split(wkv_p, raw_b[:, :, :], wkv_in, 32, 2)(wkv_split)
            if rms:
                norm_keys(*PROLOGUE)
            with pool.Fori(0, NHG) as hg:
                for g in range(NG):
                    lo = None
                    for u in range(UN):
                        pool.wait_ge(rden_done, count(UN, u + 1, hg, g))
                        scale = rden[:, 2 * u:2 * u + 2].rearrange("p (a b) -> p a b", b=1).broadcast_to([P, 2, S])
                        gp.tensor_tensor(probs[u % 2][:, :, :], probs[u % 2][:, :, :], scale, ALU.mult).then_inc(p_normed, 1)
                        if g == 0 and u == 2:
                            lo = split(wo_p, raw_a[:, :], wo_in, hg * 16 + 16, hg * 3 + 3)
                        if g == 0 and u == 3:
                            lo(wo_split)
                        if g == 2 and u == 2:
                            lo = split(wq_p, raw_a[:, :], wq_in, hg * 16 + 32, hg * 3 + 4, (q_made, count(HB, 2 * HB, hg, g)))
                        if g == 2 and u == 3:
                            lo(wq_split)
                    if rms:
                        norm_keys(hg, g)
                    if g == 2:
                        split(wkv_p, raw_b[:, :, :], wkv_in, hg * 32 + 64, hg * 3 + 5, (kv_made, count(TG, 2 * TG, hg, g)))(wkv_split)

        @block.tensor
        def _(pe):
            def products(out, terms):
                n = 3 * len(terms)
                i = 0
                for a, b in terms:
                    for x, y in ((0, 0), (0, 1), (1, 0)):
                        mm = nc.tensor.matmul(out, a[x], b[y], start=(i == 0), stop=(i == n - 1))
                        i += 1
                return mm

            def project_q(hg, g, h):
                ng = (g + 1) % NG
                if h == 0:
                    pe.wait_ge(wq_split, hg + (2 if g == NG - 1 else 1))
                    if g >= 0:
                        pe.wait_ge(y_added, count(TG, 1, hg, g))
                at = slice(GT * ng, GT * (ng + 1))
                products(b_q[h][:, :], [([w[:, c, HD * h:HD * (h + 1)] for w in wq], [k.xnT_hi[:, c, at], k.xnT_lo[:, c, at]])
                                        for c in range(KD)]).then_inc(q_made, 1)

            def project_kv(hg, g, t):
                m = (g + 1) % 2
                if t == 0:
                    pe.wait_ge(wkv_split, hg + (2 if g == NG - 1 else 1))
                    pe.wait_ge(ctx_in[m], hg * (16 * NG // 2) + 16 * ((g + 1) // 2 + 1))
                if t >= 2:
                    pe.wait_ge(kv_split, count(TG, TG + t - 1, hg, g))
                products(b_kv[t % 2][:, 0:2 * kvw], [([ctxT[m][:, a, c, P * t:P * (t + 1)] for a in range(2)], [w[:, c, :] for w in wkv])
                                                     for c in range(KC)]).then_inc(kv_made, 1)

            def sum_q(hg, g):
                pe.wait_ge(q_sq, count(HB, 2 * HB, hg, g))
                pe.wait_ge(q_split, count(HB, HB + 1, hg, g))
                for h in range(HB):
                    for t in range(TG):
                        i = TG * h + t
                        mm = nc.tensor.matmul(b_q[0][:, i:i + 1], q2[h][:, P * t:P * (t + 1)], ones[:, :], start=True, stop=True)
                mm.then_inc(qsum_made, 1)

            def turn_k(hg, g):
                if rms:
                    pe.wait_ge(k_ready, count(1, 2, hg, g))
                pe.wait_ge(kv_split, count(TG, 2 * TG, hg, g))
                for h in range(nkv):
                    for t in range(TG):
                        mm = nc.tensor.transpose(b_kv[h][:, P * t:P * (t + 1)], kn[:, t, HD * h:HD * (h + 1)], k.ident[:, :])
                    mm.then_inc(k_turned, 1)

            def scores(hg, g, u):
                h, b = u // 2, u % 2
                if b == 0:
                    pe.wait_ge(q_split, count(HB, h + 1, hg, g))
                    pe.wait_ge(kT_split, count(nkv, min(h, nkv - 1) + 1, hg, g))
                kk = kT[min(h, nkv - 1)]
                for t in range(2):
                    at = slice(S * b + P * t, S * b + P * (t + 1))
                    mm = products(b_s[u % 2][:, S * t:S * (t + 1)], [([w[:, at] for w in qT[h]], [w[:, S * b:S * (b + 1)] for w in kk])])
                mm.then_inc(s_made, 1)

            def turn_p(hg, g, u):
                pe.wait_ge(p_normed, count(UN, u + 1, hg, g))
                for t in range(2):
                    for s in range(2):
                        mm = nc.tensor.transpose(b_pt[:, S * s + P * t:S * s + P * (t + 1)], probs[u % 2][:, t, P * s:P * (s + 1)], k.ident[:, :])
                mm.then_inc(p_turned, 1)

            def weigh_v(hg, g, u):
                h, b = u // 2, u % 2
                if u == 0:
                    pe.wait_ge(kv_split, count(TG, TG, hg, g))
                if u == 2:
                    pe.wait_ge(o_split, count(HB, 1, hg, g))
                pe.wait_ge(pT_split, count(UN, u + 1, hg, g))
                vh = min(h, nkv - 1)
                products(b_o[:, S * b:S * (b + 1)], [([w[:, 2 * b + s, HD * vh:HD * (vh + 1)] for w in v[g % 2]], [w[:, s, :] for w in pT])
                                                     for s in range(2)]).then_inc(pv_made, 1)

            def project_out(hg, g, t):
                if t == 0:
                    pe.wait_ge(wo_split, hg + 1)
                    pe.wait_ge(o_split, count(HB, HB, hg, g))
                    pe.wait_ge(q_split, count(HB, 2 * HB, hg, g))
                if t == 1 and rms:
                    pe.wait_ge(sums_done, count(2, 3, hg, g))
                if t >= 2:
                    pe.wait_ge(y_added, count(TG, t, hg, g))
                products(b_q[(t + 1) % 2][:, :], [([w[:, P * t:P * (t + 1)] for w in oT[h]], [w[:, h, :] for w in wo])
                                                  for h in range(HB)]).then_inc(y_made, 1)

            if rms:
                pe.wait_ge(const_in, 33)
            project_q(*PROLOGUE, 0)
            project_q(*PROLOGUE, 1)
            for t in range(TG):
                project_kv(*PROLOGUE, t)
            if rms:
                sum_q(*PROLOGUE)
            turn_k(*PROLOGUE)
            with pe.Fori(0, NHG) as hg:
                for g in range(NG):
                    scores(hg, g, 0)
                    scores(hg, g, 1)
                    project_q(hg, g, 0)
                    turn_p(hg, g, 0)
                    scores(hg, g, 2)
                    project_q(hg, g, 1)
                    weigh_v(hg, g, 0)
                    turn_p(hg, g, 1)
                    scores(hg, g, 3)
                    project_kv(hg, g, 0)
                    project_kv(hg, g, 1)
                    weigh_v(hg, g, 1)
                    turn_p(hg, g, 2)
                    if rms:
                        sum_q(hg, g)
                    project_kv(hg, g, 2)
                    project_kv(hg, g, 3)
                    weigh_v(hg, g, 2)
                    turn_p(hg, g, 3)
                    weigh_v(hg, g, 3)
                    project_out(hg, g, 0)
                    project_out(hg, g, 1)
                    turn_k(hg, g)
                    project_out(hg, g, 2)
                    project_out(hg, g, 3)

        @block.scalar
        def _(act):
            def copy_q(hg, g, h):
                act.wait_ge(q_made, count(HB, HB + h + 1, hg, g))
                nc.scalar.copy(qT[h][0][:, :], b_q[h][:, :]).then_inc(q_hi, 1)
                if rms:
                    nc.scalar.activation(q2[h][:, :], b_q[h][:, :], ACT.Square).then_inc(q_sq, 1)

            def copy_kv(hg, g, t):
                act.wait_ge(kv_made, count(TG, TG + t + 1, hg, g))
                nc.scalar.copy(kn[:, t, :], b_kv[t % 2][:, 0:kvw])
                nc.scalar.copy(v[(g + 1) % 2][0][:, t, :], b_kv[t % 2][:, kvw:2 * kvw]).then_inc(kv_hi, 1)

            def copy_k(hg, g, h):
                act.wait_ge(k_turned, count(nkv, nkv + h + 1, hg, g))
                if rms:
                    nc.scalar.activation(kT[h][0][:, :], b_kv[h][:, :], ACT.Identity, scale=gain[:, 0:1]).then_inc(kT_hi, 1)
                else:
                    nc.scalar.copy(kT[h][0][:, :], b_kv[h][:, :]).then_inc(kT_hi, 1)

            def exponentials(hg, g, u):
                act.wait_ge(bias_done, count(UN, u + 1, hg, g))
                for t in range(2):
                    i = 2 * u + t
                    src = b_s[u % 2][:, S * t:S * (t + 1)] if rms else scored[u % 2][:, t, :]
                    scale = rr[:, nk + i:nk + i + 1] if rms else SM_SCALE
                    ins = nc.scalar.activation(probs[u % 2][:, t, :], src, ACT.Exp, bias=nbias[:, i:i + 1], scale=scale,
                                               accum_out=rsum[:, i:i + 1])
                ins.then_inc(exp_done, 1)

            def copy_p(hg, g, u):
                act.wait_ge(p_turned, count(UN, u + 1, hg, g))
                nc.scalar.copy(pT[0][:, :, :].rearrange("p s q -> p (s q)"), b_pt[:, :]).then_inc(pT_hi, 1)

            def copy_o(hg, g, h):
                act.wait_ge(pv_made, count(UN, 2 * h + 2, hg, g))
                nc.scalar.copy(oT[h][0][:, :], b_o[:, :]).then_inc(o_hi, 1)

            for h in range(HB):
                copy_q(*PROLOGUE, h)
            for t in range(TG):
                copy_kv(*PROLOGUE, t)
            if rms:
                act.wait_ge(dve_chain, 1)
            for h in range(nkv):
                copy_k(*PROLOGUE, h)
            with act.Fori(0, NHG) as hg:
                for g in range(NG):
                    exponentials(hg, g, 0)
                    exponentials(hg, g, 1)
                    copy_q(hg, g, 0)
                    copy_p(hg, g, 0)
                    exponentials(hg, g, 2)
                    copy_p(hg, g, 1)
                    exponentials(hg, g, 3)
                    copy_q(hg, g, 1)
                    copy_kv(hg, g, 0)
                    copy_kv(hg, g, 1)
                    copy_o(hg, g, 0)
                    copy_p(hg, g, 2)
                    copy_kv(hg, g, 2)
                    copy_kv(hg, g, 3)
                    copy_p(hg, g, 3)
                    copy_o(hg, g, 1)
                    for h in range(nkv):
                        copy_k(hg, g, h)

        @block.vector
        def _(dve):
            def lo(pair, src, done):
                nc.vector.tensor_tensor(pair[1], src, pair[0].bitcast(F32), ALU.subtract).then_inc(done, 1)

            def split_q(hg, g, h):
                dve.wait_ge(q_sq if rms else q_hi, count(HB, HB + h + 1, hg, g))
                lo([w[:, :] for w in qT[h]], b_q[h][:, :], q_split)

            def split_kv(hg, g, t):
                dve.wait_ge(kv_hi, count(TG, TG + t + 1, hg, g))
                lo([w[:, t, :] for w in v[(g + 1) % 2]], b_kv[t % 2][:, kvw:2 * kvw], kv_split)

            def split_k(hg, g, h):
                dve.wait_ge(kT_hi, count(nkv, nkv + h + 1, hg, g))
                if rms:
                    nc.vector.scalar_tensor_tensor(kT[h][1][:, :], b_kv[h][:, :], gain[:, 0:1], kT[h][0][:, :].bitcast(F32),
                                                   ALU.mult, ALU.subtract).then_inc(kT_split, 1)
                else:
                    lo([w[:, :] for w in kT[h]], b_kv[h][:, :], kT_split)

            def split_p(hg, g, u):
                dve.wait_ge(pT_hi, count(UN, u + 1, hg, g))
                lo([w[:, :, :].rearrange("p s q -> p (s q)") for w in pT], b_pt[:, :], pT_split)

            def split_o(hg, g, h):
                dve.wait_ge(o_hi, count(HB, h + 1, hg, g))
                lo([w[:, :] for w in oT[h]], b_o[:, :], o_split)

            before_loop = 1 if rms else 2

            def biases(hg, g, u):
                i = slice(2 * u, 2 * u + 2)
                dve.wait_ge(s_made, count(UN, u + 1, hg, g))
                if rms:
                    nc.vector.tensor_reduce(mx[:, i], b_s[u % 2][:, :].rearrange("p (t s) -> p t s", t=2), AX.X, ALU.max).then_inc(dve_chain, 1)
                    dve.wait_ge(dve_chain, count(UN, before_loop + u + 1, hg, g))
                    nc.vector.scalar_tensor_tensor(nbias[:, i], mx[:, i], -1.0, rr[:, nk + 2 * u:nk + 2 * u + 2],
                                                   ALU.mult, ALU.mult).then_inc(bias_done, 1)
                else:
                    at = S * (2 * g + u % 2)
                    apart(k, dve)
                    for t in range(2):
                        ins = nc.vector.tensor_tensor_reduce(scored[u % 2][:, t, :], b_s[u % 2][:, S * t:S * (t + 1)], mask_bias[:, at:at + S],
                                                             1.0, MAX_FLOOR, ALU.add, ALU.max, mx[:, 2 * u + t:2 * u + t + 1])
                    ins.then_inc(dve_chain, 1)
                    dve.wait_ge(dve_chain, count(UN, before_loop + u + 1, hg, g))
                    nc.vector.tensor_scalar(nbias[:, i], mx[:, i], -SM_SCALE, None, ALU.mult).then_inc(bias_done, 1)

            def denominators(hg, g, u):
                i = slice(2 * u, 2 * u + 2)
                dve.wait_ge(exp_done, count(UN, u + 1, hg, g))
                if not rms:
                    nc.vector.tensor_scalar(rsum[:, i], rsum[:, i], 1e-30, None, ALU.max).then_inc(den_chain, 1)
                    dve.wait_ge(den_chain, count(UN, u + 1, hg, g))
                nc.vector.reciprocal(rden[:, i], rsum[:, i]).then_inc(rden_done, 1)

            def take_sums(hg, g):
                dve.wait_ge(qsum_made, count(1, 2, hg, g))
                nc.vector.tensor_copy(sums[:, nk:nk + nq], b_q[0][:, 0:nq]).then_inc(sums_done, 1)
                dve.wait_ge(k_squared, count(1, 2, hg, g))
                nc.vector.tensor_reduce(sums[:, 0:nk], k2[:, :, :].rearrange("p t (h d) -> p (t h) d", d=HD), AX.X,
                                        ALU.add).then_inc(sums_done, 1)

            def add_y(hg, g, t):
                dve.wait_ge(y_made, count(TG, t + 1, hg, g))
                row = k.x_sb[:, TG * g + t, :]
                nc.vector.tensor_tensor(row, b_q[(t + 1) % 2][:, :], row, ALU.add).then_inc(y_added, 1)

            if rms:
                dve.wait_ge(const_in, 33)
                nc.vector.scalar_tensor_tensor(gain[:, :], gain_in[:, 0:1], SM_SCALE, gain_in[:, 1:2], ALU.mult, ALU.mult).then_inc(dve_chain, 1)
            else:
                half = T // 2
                for i in range(2):
                    dve.wait_ge(const_in, 16 * (i + 1))
                    nc.vector.tensor_scalar(mask_bias[:, half * i:half * (i + 1)], mask_u8[:, :], -MASKED, MASKED, ALU.mult, ALU.add).then_inc(dve_chain, 1)
                dve.wait_ge(dve_chain, 2)
            dve.sem_inc(y_added, 1)
            for h in range(HB):
                split_q(*PROLOGUE, h)
            for t in range(TG):
                split_kv(*PROLOGUE, t)
            if rms:
                take_sums(*PROLOGUE)
            for h in range(nkv):
                split_k(*PROLOGUE, h)
            with dve.Fori(0, NHG) as hg:
                for g in range(NG):
                    biases(hg, g, 0)
                    biases(hg, g, 1)
                    denominators(hg, g, 0)
                    denominators(hg, g, 1)
                    split_q(hg, g, 0)
                    split_p(hg, g, 0)
                    biases(hg, g, 2)
                    denominators(hg, g, 2)
                    split_p(hg, g, 1)
                    biases(hg, g, 3)
                    denominators(hg, g, 3)
                    split_q(hg, g, 1)
                    split_kv(hg, g, 0)
                    split_kv(hg, g, 1)
                    split_o(hg, g, 0)
                    split_p(hg, g, 2)
                    split_kv(hg, g, 2)
                    split_kv(hg, g, 3)
                    if rms:
                        take_sums(hg, g)
                    split_p(hg, g, 3)
                    split_o(hg, g, 1)
                    add_y(hg, g, 0)
                    add_y(hg, g, 1)
                    for h in range(nkv):
                        split_k(hg, g, h)
                    add_y(hg, g, 2)
                    add_y(hg, g, 3)


def ffn_stage(k, gate_w, up_w, down_w, gate_scale, up_scale, down_scale):
    nc, banks = k.nc, k.banks
    half = 3 * D // 2
    gate_v = gate_w.rearrange("(k p) f -> p k f", p=P)
    up_v = up_w.rearrange("(k p) f -> p k f", p=P)
    down_v = down_w.rearrange("(f p) n -> p f n", p=P)
    b_gate, b_up, b_y = banks[0:2], banks[2:4], banks[4:8]
    with ExitStack() as st:
        def sb(n, shape, dt=F32):
            return st.enter_context(nc.sbuf_tensor(f"ffn_{n}", shape, dt))

        def sem(n):
            return k.sem(f"ffn_{n}")

        w = sb("w", [P, NF, 3 * D], F32R)
        raw = [sb(f"raw{i}", [P, half]) for i in range(2)]
        magic = [sb(f"magic{i}", [P, half]) for i in range(2)]
        silu = [sb(f"silu{i}", [P, GT]) for i in range(2)]
        fuse = [sb(f"fuse{i}", [P, GT]) for i in range(2)]
        fz = [[sb(f"fz{i}_{p}", [P, GT], F32R) for p in ("hi", "lo")] for i in range(2)]
        scale_rows = sb("scale_rows", [2 * NF, P])
        scales, dsc = sb("scales", [P, 2 * NF]), sb("dsc", [P, D])
        ysc = [sb(f"ysc{i}", [P, D]) for i in range(2)]
        block = st.enter_context(nc.Block())
        raw_in = [sem(f"raw_in{i}") for i in range(2)]
        scales_turned, scales_ready = sem("scales_turned"), sem("scales_ready")
        scales_in, magic_chain, magic_made, round_chain, w_ready = (
            sem(n) for n in ("scales_in", "magic_chain", "magic_made", "round_chain", "w_ready"))
        gate_made, up_made, silu_done, fuse_done, fz_hi, fz_split, y_made, y_chain, y_added = (
            sem(n) for n in ("gate_made", "up_made", "silu_done", "fuse_done", "fz_hi", "fz_split", "y_made", "y_chain", "y_added"))

        @block.sync
        def _(sp):
            def load(f):
                at = bass.ds(f * P, P)
                r0 = raw[0][:, :].rearrange("p (k f) -> p k f", f=P)
                sp.dma_start(r0[:, 0:KD, :], gate_v[:, :, at]).then_inc(raw_in[0], 16)
                sp.dma_start(r0[:, KD:half // P, :], up_v[:, 0:2, at]).then_inc(raw_in[0], 16)
                yield
                r1 = raw[1][:, 0:2 * P].rearrange("p (k f) -> p k f", f=P)
                sp.dma_start(r1, up_v[:, 2:4, at]).then_inc(raw_in[1], 16)
                sp.dma_start(raw[1][:, 2 * P:half], down_v[:, bass.ds(f, 1), :]).then_inc(raw_in[1], 16)
                yield

            for _ in load(0):
                pass
            sp.dma_start(scale_rows[0:NF, :], gate_scale.rearrange("(f p) -> f p", p=P)).then_inc(scales_in, 16)
            sp.dma_start(scale_rows[NF:2 * NF, :], up_scale.rearrange("(f p) -> f p", p=P)).then_inc(scales_in, 16)
            sp.dma_start(dsc[:, :], down_scale.rearrange("(a n) -> a n", a=1).broadcast_to([P, D])).then_inc(scales_in, 16)
            with sp.Fori(0, NF - 1) as f:
                steps = load(f + 1)
                for c in range(2):
                    sp.wait_ge(w_ready, f * 2 + (c + 1))
                    next(steps)

        @block.gpsimd
        def _(pool):
            with pool.Fori(0, NF) as f:
                for c in range(2):
                    pool.wait_ge(magic_made, f * 2 + (c + 1))
                    nc.gpsimd.tensor_tensor(raw[c][:, :], raw[c][:, :], magic[c][:, :], ALU.add).then_inc(round_chain, 1)
                    pool.wait_ge(round_chain, f * 2 + (c + 1))
                    nc.gpsimd.tensor_tensor(w[:, bass.ds(f, 1), half * c:half * (c + 1)], raw[c][:, :], magic[c][:, :],
                                            ALU.subtract).then_inc(w_ready, 1)
            with pool.Fori(0, NG) as g:
                for f in range(NF):
                    pool.wait_ge(fuse_done, g * NF + (f + 1))
                    apart(k, pool)
                    nc.gpsimd.tensor_copy(fz[f % 2][0][:, :], fuse[f % 2][:, :]).then_inc(fz_hi, 1)
                    pool.wait_ge(fz_hi, g * NF + (f + 1))
                    nc.gpsimd.tensor_tensor(fz[f % 2][1][:, :], fuse[f % 2][:, :], fz[f % 2][0][:, :].bitcast(F32),
                                            ALU.subtract).then_inc(fz_split, 1)

        @block.vector
        def _(dve):
            with dve.Fori(0, NF) as f:
                for c in range(2):
                    dve.wait_ge(raw_in[c], f * 32 + 32)
                    nc.vector.tensor_scalar(magic[c][:, :].bitcast(U32), raw[c][:, :].bitcast(U32), 0x7F800000, None,
                                            ALU.bitwise_and).then_inc(magic_chain, 1)
                    dve.wait_ge(magic_chain, f * 2 + (c + 1))
                    nc.vector.tensor_scalar(magic[c][:, :], magic[c][:, :], 2.0 ** -6, 1.5 * 2.0 ** 20, ALU.max, ALU.mult).then_inc(magic_made, 1)
            dve.wait_ge(scales_turned, 1)
            nc.vector.tensor_copy(scales[:, :], b_gate[0][:, 0:2 * NF]).then_inc(scales_ready, 1)
            dve.wait_ge(scales_ready, 1)
            with dve.Fori(0, NG) as g:
                for f in range(NF):
                    dve.wait_ge(silu_done, g * NF + (f + 1))
                    dve.wait_ge(up_made, g * NF + (f + 1))
                    nc.vector.scalar_tensor_tensor(fuse[f % 2][:, :], b_up[f % 2][:, :], scales[:, NF + f:NF + f + 1], silu[f % 2][:, :],
                                                   ALU.mult, ALU.mult).then_inc(fuse_done, 1)
                for t in range(TG):
                    dve.wait_ge(y_made, g * TG + (t + 1))
                    nc.vector.tensor_tensor(ysc[t % 2][:, :], b_y[t][:, :], dsc[:, :], ALU.mult).then_inc(y_chain, 1)
                    dve.wait_ge(y_chain, g * TG + (t + 1))
                    row = k.x_sb[:, bass.ds(g * TG + t, 1), :]
                    nc.vector.tensor_tensor(row, ysc[t % 2][:, :], row, ALU.add).then_inc(y_added, 1)

        @block.scalar
        def _(act):
            act.wait_ge(scales_ready, 1)
            with act.Fori(0, NG) as g:
                for f in range(NF):
                    act.wait_ge(gate_made, g * NF + (f + 1))
                    nc.scalar.activation(silu[f % 2][:, :], b_gate[f % 2][:, :], ACT.Silu, scale=scales[:, f:f + 1]).then_inc(silu_done, 1)

        @block.tensor
        def _(pe):
            pe.wait_ge(scales_in, 48)
            nc.tensor.transpose(b_gate[0][:, 0:2 * NF], scale_rows[:, :], k.ident[0:2 * NF, 0:2 * NF]).then_inc(scales_turned, 1)
            pe.wait_ge(scales_ready, 1)
            pe.wait_ge(w_ready, 2 * NF)
            with pe.Fori(0, NG) as g:
                def down(f):
                    pe.wait_ge(fz_split, g * NF + (f + 1))
                    for t in range(TG):
                        for part in fz[f % 2]:
                            mm = nc.tensor.matmul(b_y[t][:, :], part[:, P * t:P * (t + 1)], w[:, f, 2 * D:3 * D],
                                                  start=(f == 0 and part is fz[f % 2][0]), stop=(f == NF - 1 and part is fz[f % 2][1]))
                        if f == NF - 1:
                            mm.then_inc(y_made, 1)

                at = bass.ds(g * GT, GT)
                for f in range(NF):
                    for out, first, done in ((b_gate, 0, gate_made), (b_up, D, up_made)):
                        for c in range(KD):
                            for part in (k.xnT_hi, k.xnT_lo):
                                mm = nc.tensor.matmul(out[f % 2][:, :], w[:, f, first + P * c:first + P * (c + 1)], part[:, c, at],
                                                      start=(c == 0 and part is k.xnT_hi), stop=(c == KD - 1 and part is k.xnT_lo))
                        mm.then_inc(done, 1)
                    if f >= 1:
                        down(f - 1)
                down(NF - 1)


def moe_stage(k, gate_w, gate_up, down_proj, out):
    nc, banks = k.nc, k.banks
    gu_v = gate_up.rearrange("e (k p) f -> p e k f", p=P)
    dn_v = down_proj.rearrange("e (k p) n -> p e k n", p=P)
    KI = I // P
    WC = KD * 2 * I + KI * D
    with ExitStack() as st:
        def sb(n, shape, dt=F32):
            return st.enter_context(nc.sbuf_tensor(f"moe_{n}", shape, dt))

        def sem(n):
            return k.sem(f"moe_{n}")

        raw = [sb(f"raw{i}", [P, WC]) for i in range(2)]
        w = [[sb(f"w{i}_{p}", [P, WC], F32R) for p in ("hi", "lo")] for i in range(2)]
        silu = [sb(f"silu{i}", [P, GT]) for i in range(KI)]
        fuse = [[sb(f"fuse{i}_{f}", [P, GT]) for f in range(KI)] for i in range(2)]
        fz = [[sb(f"fz{i}_{p}", [P, KI, GT], F32R) for p in ("hi", "lo")] for i in range(2)]
        gw = sb("gw", [E, D])
        gwT = [sb(f"gwT_{p}", [P, KD, E], F32R) for p in ("hi", "lo")]
        prob, eq, pick1, pick2, comb = (sb(n, [P, NT, E]) for n in ("prob", "eq", "pick1", "pick2", "comb"))
        rank_int, rank = sb("rank_int", [P, E], I32), sb("rank", [P, E])
        m1, m2, ms, key = (sb(n, [P, NT]) for n in ("m1", "m2", "ms", "key"))
        block = st.enter_context(nc.Block())
        gw_in, gw_turned, gw_hi, gw_split, logits_made, prob_made, rank_made, route_chain, routed = (
            sem(n) for n in ("gw_in", "gw_turned", "gw_hi", "gw_split", "logits_made", "prob_made", "rank_made", "route_chain", "routed"))
        raw_in = [sem(f"raw_in{i}") for i in range(2)]
        w_hi, w_split, gu_made, silu_done, fuse_done, fz_hi, fz_split, y_made, y_added, stored = (
            sem(n) for n in ("w_hi", "w_split", "gu_made", "silu_done", "fuse_done", "fz_hi", "fz_split", "y_made", "y_added", "stored"))
        b_gu, b_y = banks[0:4], banks[4:8]
        UB = 2 * NG

        @block.sync
        def _(sp):
            sp.dma_start(gw[:, :], gate_w).then_inc(gw_in, 16)

            def load(e, i):
                sp.dma_start(raw[i][:, 0:KD * 2 * I].rearrange("p (k f) -> p k f", k=KD), gu_v[:, bass.ds(e, 1), :, :]).then_inc(raw_in[i], 16)
                sp.dma_start(raw[i][:, KD * 2 * I:WC].rearrange("p (k n) -> p k n", k=KI), dn_v[:, bass.ds(e, 1), :, :]).then_inc(raw_in[i], 16)

            for i in range(2):
                load(i, i)
            with sp.Fori(0, E // 2) as ep:
                for i in range(2):
                    sp.wait_ge(w_split, ep * 2 + (i + 1))
                    load((ep * 2 + (i + 2)) % E, i)
            for loaded in raw_in:
                sp.wait_ge(loaded, 32 * (E // 2 + 1))
            ov = out.rearrange("b (t p) d -> p (b t) d", p=P)
            for g in range(NG):
                sp.wait_ge(y_added, TG * (1 + (E - 1) * NG + g + 1))
                sp.dma_start(ov[:, TG * g:TG * (g + 1), :], k.x_sb[:, TG * g:TG * (g + 1), :]).then_inc(stored, 16)
            sp.wait_ge(stored, 16 * NG)

        @block.gpsimd
        def _(pool):
            gp = nc.gpsimd
            gp.iota(rank_int[:, :], pattern=[[-1, E]], base=E, channel_multiplier=0).then_inc(rank_made, 1)

            def split(i, level, count):
                pool.wait_ge(raw_in[i], level)
                apart(k, pool)
                gp.tensor_copy(w[i][0][:, :], raw[i][:, :]).then_inc(w_hi, 1)
                pool.wait_ge(w_hi, count)
                gp.tensor_tensor(w[i][1][:, :], raw[i][:, :], w[i][0][:, :].bitcast(F32), ALU.subtract).then_inc(w_split, 1)

            split(0, 32, 1)
            with pool.Fori(0, E // 2) as ep:
                for i in range(2):
                    for g in range(NG):
                        n = NG * i + g
                        for f in range(KI):
                            pool.wait_ge(fuse_done, ep * (KI * UB) + (KI * (n + 1) + f + 1))
                            apart(k, pool)
                            gp.tensor_copy(fz[n % 2][0][:, f, :], fuse[n % 2][f][:, :]).then_inc(fz_hi, 1)
                            pool.wait_ge(fz_hi, ep * (KI * UB) + (KI * n + f + 1))
                            gp.tensor_tensor(fz[n % 2][1][:, f, :], fuse[n % 2][f][:, :], fz[n % 2][0][:, f, :].bitcast(F32),
                                             ALU.subtract).then_inc(fz_split, 1)
                        if g == 1:
                            pool.wait_ge(y_made, ep * (TG * UB) + (TG * NG * i + 1))
                            split(1 - i, ep * 32 + 32 * (i + 1), ep * 2 + (i + 2))

        @block.tensor
        def _(pe):
            pe.sem_inc(y_made, 1)
            pe.wait_ge(gw_in, 16)
            for c in range(KD):
                mm = nc.tensor.transpose(b_gu[0][:, E * c:E * (c + 1)], gw[:, P * c:P * (c + 1)], k.ident[0:E, 0:E])
            mm.then_inc(gw_turned, 1)
            pe.wait_ge(gw_split, 1)
            for t in range(NT):
                i = 0
                for c in range(KD):
                    at = slice(P * t, P * (t + 1))
                    for a, b in ((k.xnT_hi, gwT[0]), (k.xnT_hi, gwT[1]), (k.xnT_lo, gwT[0])):
                        mm = nc.tensor.matmul(b_y[0][:, E * t:E * (t + 1)], a[:, c, at], b[:, c, :], start=(i == 0), stop=(i == 3 * KD - 1))
                        i += 1
            mm.then_inc(logits_made, 1)
            with pe.Fori(0, E // 2) as ep:
                def up(n):
                    i, g = n // NG, n % NG
                    if g == 0:
                        pe.wait_ge(w_split, ep * 2 + (i + 1))
                    for f in range(KI):
                        pe.wait_ge(fuse_done, ep * (KI * UB) + (KI * n + f + 1))
                        for b, first in ((f, P * f), (KI + f, I + P * f)):
                            j = 0
                            for c in range(KD):
                                cols = slice(2 * I * c + first, 2 * I * c + first + P)
                                for a, x in ((0, k.xnT_hi), (0, k.xnT_lo), (1, k.xnT_hi)):
                                    mm = nc.tensor.matmul(b_gu[b][:, :], w[i][a][:, cols], x[:, c, GT * g:GT * (g + 1)],
                                                          start=(j == 0), stop=(j == 3 * KD - 1))
                                    j += 1
                        mm.then_inc(gu_made, 1)

                def down(n):
                    i = n // NG
                    pe.wait_ge(fz_split, ep * (KI * UB) + KI * (n + 1))
                    for t in range(TG):
                        pe.wait_ge(y_added, ep * (TG * UB) + (TG * n + t + 1))
                        j = 0
                        for f in range(KI):
                            wd = slice(KD * 2 * I + D * f, KD * 2 * I + D * (f + 1))
                            for a, b in ((0, 0), (0, 1), (1, 0)):
                                mm = nc.tensor.matmul(b_y[t][:, :], fz[n % 2][a][:, f, P * t:P * (t + 1)], w[i][b][:, wd],
                                                      start=(j == 0), stop=(j == 3 * KI - 1))
                                j += 1
                        mm.then_inc(y_made, 1)

                for n in range(UB):
                    up(n)
                    if n >= 1:
                        down(n - 1)
                down(UB - 1)

        @block.scalar
        def _(act):
            act.wait_ge(gw_turned, 1)
            nc.scalar.copy(gwT[0][:, :, :].rearrange("p k e -> p (k e)"), b_gu[0][:, 0:KD * E]).then_inc(gw_hi, 1)
            act.wait_ge(logits_made, 1)
            nc.scalar.activation(prob[:, :, :].rearrange("p t e -> p (t e)"), b_y[0][:, 0:NT * E], ACT.Sigmoid).then_inc(prob_made, 1)
            with act.Fori(0, E // 2) as ep:
                for n in range(UB):
                    for f in range(KI):
                        act.wait_ge(gu_made, ep * (KI * UB) + (KI * n + f + 1))
                        nc.scalar.activation(silu[f][:, :], b_gu[f][:, :], ACT.Silu).then_inc(silu_done, 1)

        @block.vector
        def _(dve):
            v = nc.vector
            dve.wait_ge(gw_hi, 1)
            v.tensor_tensor(gwT[1][:, :, :].rearrange("p k e -> p (k e)"), b_gu[0][:, 0:KD * E],
                            gwT[0][:, :, :].rearrange("p k e -> p (k e)").bitcast(F32), ALU.subtract).then_inc(gw_split, 1)
            dve.sem_inc(fuse_done, KI)
            dve.sem_inc(y_added, TG)
            done = [0]

            def step(ins):
                ins.then_inc(route_chain, 1)
                done[0] += 1
                dve.wait_ge(route_chain, done[0])

            def over_e(a):
                return a.rearrange("p (t o) -> p t o", o=1).broadcast_to([P, NT, E])

            def pick(best, chosen):
                step(v.tensor_reduce(best[:, :], prob[:, :, :], AX.X, ALU.max))
                step(v.tensor_tensor(eq[:, :, :], prob[:, :, :], over_e(best[:, :]), ALU.is_equal))
                step(v.tensor_tensor(eq[:, :, :], eq[:, :, :], rank[:, :].rearrange("p (o e) -> p o e", o=1).broadcast_to([P, NT, E]), ALU.mult))
                step(v.tensor_reduce(key[:, :], eq[:, :, :], AX.X, ALU.max))
                step(v.tensor_tensor(chosen[:, :, :], eq[:, :, :], over_e(key[:, :]), ALU.is_equal))

            dve.wait_ge(prob_made, 1)
            dve.wait_ge(rank_made, 1)
            step(v.tensor_copy(rank[:, :], rank_int[:, :]))
            step(v.tensor_reduce(ms[:, :], prob[:, :, :], AX.X, ALU.add))
            step(v.reciprocal(ms[:, :], ms[:, :]))
            step(v.tensor_tensor(prob[:, :, :], prob[:, :, :], over_e(ms[:, :]), ALU.mult))
            pick(m1, pick1)
            step(v.scalar_tensor_tensor(prob[:, :, :], pick1[:, :, :], -4.0, prob[:, :, :], ALU.mult, ALU.add))
            pick(m2, pick2)
            step(v.tensor_tensor(ms[:, :], m1[:, :], m2[:, :], ALU.add))
            step(v.reciprocal(ms[:, :], ms[:, :]))
            step(v.tensor_tensor(m1[:, :], m1[:, :], ms[:, :], ALU.mult))
            step(v.tensor_tensor(m2[:, :], m2[:, :], ms[:, :], ALU.mult))
            step(v.tensor_tensor(pick1[:, :, :], pick1[:, :, :], over_e(m1[:, :]), ALU.mult))
            step(v.tensor_tensor(pick2[:, :, :], pick2[:, :, :], over_e(m2[:, :]), ALU.mult))
            step(v.tensor_tensor(comb[:, :, :], pick1[:, :, :], pick2[:, :, :], ALU.add))

            with dve.Fori(0, E // 2) as ep:
                def gate(n):
                    for f in range(KI):
                        dve.wait_ge(silu_done, ep * (KI * UB) + (KI * n + f + 1))
                        v.tensor_tensor(fuse[n % 2][f][:, :], b_gu[KI + f][:, :], silu[f][:, :], ALU.mult).then_inc(fuse_done, 1)

                def add(n):
                    i, g = n // NG, n % NG
                    for t in range(TG):
                        dve.wait_ge(y_made, ep * (TG * UB) + (TG * n + t + 2))
                        row = k.x_sb[:, TG * g + t, :]
                        v.scalar_tensor_tensor(row, b_y[t][:, :], comb[:, TG * g + t, bass.ds(ep * 2 + i, 1)], row,
                                               ALU.mult, ALU.add).then_inc(y_added, 1)

                for n in range(UB):
                    gate(n)
                    if n >= 1:
                        add(n - 1)
                add(UB - 1)


def decoder_layers(nc, x, ctx_1024, mask, w0, f0, w1, m1, out):
    with ExitStack() as st:
        k = Parts()
        k.nc = nc
        k.sem = lambda n: st.enter_context(nc.semaphore(n))
        k.banks = [st.enter_context(nc.psum_tensor(f"bank{i}", [P, 512], F32)) for i in range(8)]
        k.x_sb = st.enter_context(nc.sbuf_tensor("x_sb", [P, NT, D], F32))
        k.xnT_hi = st.enter_context(nc.sbuf_tensor("xnT_hi", [P, KD, T], F32R))
        k.xnT_lo = st.enter_context(nc.sbuf_tensor("xnT_lo", [P, KD, T], F32R))
        k.ident = st.enter_context(nc.sbuf_tensor("ident", [P, P], F32))
        k.ctx_split = nc.dram_tensor("ctx_split", (NG, P, 2 * KC * GT), F32, kind="Internal").ap()
        k.ln_calls = 0
        k.ident_made, k.wait_over = k.sem("ident_made"), k.sem("wait_over")
        k.ln_sems = [k.sem(f"ln_{n}") for n in ("chain", "normed", "turned", "hi_done", "lo_done")]
        load_stage(k, x, ctx_1024)
        layernorm_stage(k)
        attention_stage(k, "l0", *w0, mask=mask)
        layernorm_stage(k)
        ffn_stage(k, *f0)
        layernorm_stage(k)
        attention_stage(k, "l1", *w1[:4], gq=w1[4], gk=w1[5])
        layernorm_stage(k)
        moe_stage(k, *m1, out)


_INS = ["x", "ctx_1024", "mask_BxS2_bf1", "L0_xattn_Wq", "L0_xattn_Wk", "L0_xattn_Wv", "L0_xattn_Wo", "L0_ffn_gate_w",
        "L0_ffn_up_w", "L0_ffn_down_w", "L0_ffn_gate_scale", "L0_ffn_up_scale", "L0_ffn_down_scale", "L1_xattn_Wq",
        "L1_xattn_Wk", "L1_xattn_Wv", "L1_xattn_Wo", "L1_xattn_gq", "L1_xattn_gk", "L1_ffn_gate_w", "L1_ffn_gate_up_proj",
        "L1_ffn_down_proj"]


def kernel(**inputs):
    import concourse.bacc as bacc
    import numpy as np
    from concourse.bass_utils import run_bass_kernel_spmd as run

    nc = bacc.Bacc("TRN2", target_bir_lowering=False, num_devices=1)
    arrays, aps = {}, []
    for name in _INS:
        a = np.ascontiguousarray(inputs[name])
        if a.dtype == np.bool_:
            a = a.view(np.uint8)
        arrays[f"in_{name}"] = a
        aps.append(nc.dram_tensor(f"in_{name}", a.shape, mybir.dt.from_np(a.dtype), kind="ExternalInput").ap())
    out = nc.dram_tensor("out_x", (B, S, D), F32, kind="ExternalOutput").ap()
    decoder_layers(nc, aps[0], aps[1], aps[2], aps[3:7], aps[7:13], aps[13:19], aps[19:22], out)
    return run(nc, [arrays], core_ids=[0]).results[0]["out_x"]
```

```python
from contextlib import ExitStack

import concourse.bass as bass
from concourse import mybir

ALU = mybir.AluOpType
ACT = mybir.ActivationFunctionType
AX = mybir.AxisListType
F32 = mybir.dt.float32
F32R = mybir.dt.float32r
BF16 = mybir.dt.bfloat16
I32 = mybir.dt.int32
U32 = mybir.dt.uint32
U8 = mybir.dt.uint8

P = 128
B, S, D = 8, 256, 512
C = 256
T = B * S
NT = T // P
KD, KC = D // P, C // P
GT = 512
NG = T // GT
TG = GT // P
NH, HD = 16, 128
HB = 2
NHG = NH // HB
UN = HB * 2
F = 1536
NF = F // P
E, I = 16, 256
EPS = 1e-5
SM_SCALE = float(HD) ** -0.5
MASKED = -1e30
MAX_FLOOR = -1e29
RSQRT_SEED = float(0x5F3759DF)


def rsqrt_steps(eng, y, tmp, v, step, apart=lambda: None):
    apart()
    step(eng.tensor_scalar(y.bitcast(I32), v.bitcast(I32), -0.5, RSQRT_SEED, ALU.mult, ALU.add))
    for _ in range(3):
        step(eng.tensor_tensor(tmp, y, y, ALU.mult))
        step(eng.tensor_tensor(tmp, tmp, v, ALU.mult))
        apart()
        step(eng.tensor_scalar(tmp, tmp, -0.5, 1.5, ALU.mult, ALU.add))
        step(eng.tensor_tensor(y, y, tmp, ALU.mult))


RSQRT_STEPS = 13


def apart(k, eng):
    eng.sem_inc(k.wait_over, 1)


class Parts:
    pass


def load_stage(k, x, ctx_in):
    nc, banks = k.nc, k.banks
    with ExitStack() as st:
        c_sb = st.enter_context(nc.sbuf_tensor("c_sb", [P, NT, C], F32))
        ct = [st.enter_context(nc.sbuf_tensor(f"ct{i}", [P, 2, KC, GT], F32R)) for i in range(2)]
        zero = st.enter_context(nc.sbuf_tensor("zero", [P, P], F32))
        block = st.enter_context(nc.Block())
        ident_made = k.ident_made
        x_in, c_loaded, c_turned, c_hi, c_lo = (k.sem(n) for n in ("x_in", "c_loaded", "c_turned", "c_hi", "c_lo"))
        c_stored = [k.sem(f"c_stored{i}") for i in range(2)]

        @block.sync
        def _(sp):
            sp.dma_start(c_sb[:, :, :], ctx_in.rearrange("b (t p) d -> p (b t) d", p=P)).then_inc(c_loaded, 16)
            xv = x.rearrange("b (t p) d -> p (b t) d", p=P)
            for g in range(NG):
                sp.dma_start(k.x_sb[:, TG * g:TG * (g + 1), :], xv[:, TG * g:TG * (g + 1), :]).then_inc(x_in, 16)
            for g in range(NG):
                sp.wait_ge(c_lo, KC * (g + 1))
                sp.dma_start(k.ctx_split[g], ct[g % 2][:, :, :, :].rearrange("p a k t -> p (a k t)").bitcast(F32)).then_inc(c_stored[g % 2], 16)
            sp.wait_ge(x_in, 16 * NG)
            for stored in c_stored:
                sp.wait_ge(stored, 16 * NG // 2)

        @block.gpsimd
        def _(pool):
            nc.gpsimd.memset(zero[:, :], 0.0).then_inc(ident_made, 1)
            pool.wait_ge(ident_made, 1)
            nc.gpsimd.affine_select(out=k.ident[:, :], in_=zero[:, :], compare_op=ALU.not_equal, fill=1.0, base=0,
                                    pattern=[[-1, P]], channel_multiplier=1).then_inc(ident_made, 1)

        @block.tensor
        def _(pe):
            pe.wait_ge(ident_made, 2)
            pe.wait_ge(c_loaded, 16)
            for g in range(NG):
                for c in range(KC):
                    if g >= 2:
                        pe.wait_ge(c_lo, KC * (g - 2) + c + 1)
                    for j in range(TG):
                        mm = nc.tensor.transpose(banks[KC * (g % 2) + c][:, P * j:P * (j + 1)],
                                                 c_sb[:, TG * g + j, P * c:P * (c + 1)], k.ident[:, :])
                    mm.then_inc(c_turned, 1)

        @block.scalar
        def _(act):
            for g in range(NG):
                if g >= 2:
                    act.wait_ge(c_stored[g % 2], 16 * (g // 2))
                for c in range(KC):
                    act.wait_ge(c_turned, KC * g + c + 1)
                    nc.scalar.copy(ct[g % 2][:, 0, c, :], banks[KC * (g % 2) + c][:, :]).then_inc(c_hi, 1)

        @block.vector
        def _(dve):
            for g in range(NG):
                for c in range(KC):
                    dve.wait_ge(c_hi, KC * g + c + 1)
                    nc.vector.tensor_tensor(ct[g % 2][:, 1, c, :], banks[KC * (g % 2) + c][:, :],
                                            ct[g % 2][:, 0, c, :].bitcast(F32), ALU.subtract).then_inc(c_lo, 1)


def layernorm_stage(k, rows=None):
    nc, banks = k.nc, k.banks
    turn = k.ln_calls
    k.ln_calls += 1
    steps = 2 * TG + 1 + RSQRT_STEPS
    with ExitStack() as st:
        xn = [st.enter_context(nc.sbuf_tensor(f"xn{turn}_{j}", [P, D], F32)) for j in range(TG)]
        stats = st.enter_context(nc.sbuf_tensor(f"ln_stats{turn}", [P, TG, 6], F32))
        mv = st.enter_context(nc.sbuf_tensor(f"ln_mv{turn}", [P, TG, 2], F32))
        var = st.enter_context(nc.sbuf_tensor(f"ln_var{turn}", [P, TG], F32))
        rstd = st.enter_context(nc.sbuf_tensor(f"ln_rstd{turn}", [P, TG], F32))
        tmp = st.enter_context(nc.sbuf_tensor(f"ln_tmp{turn}", [P, TG], F32))
        block = st.enter_context(nc.Block())
        chain, normed, turned, hi_done, lo_done = k.ln_sems
        if rows is not None:
            rows_out = k.sem("ln_rows_out")
            rows_v = rows.rearrange("(t p) d -> p t d", p=P)

            @block.sync
            def _(sp):
                with sp.Fori(0, NG) as g:
                    for j in range(TG):
                        sp.wait_ge(normed, g * TG + (turn * NT + j + 1))
                        sp.dma_start(rows_v[:, bass.ds(g * TG + j, 1), :], xn[j][:, :]).then_inc(rows_out, 16)
                sp.wait_ge(rows_out, 16 * NT + 1)

        @block.vector
        def _(dve):
            if rows is not None:
                dve.sem_inc(rows_out, 1)
            with dve.Fori(0, NG) as g:
                done = [0]

                def step(ins, wait=True):
                    ins.then_inc(chain, 1)
                    done[0] += 1
                    if wait:
                        dve.wait_ge(chain, g * steps + (turn * NG * steps + done[0]))

                for j in range(TG):
                    step(nc.vector.bn_stats(stats[:, j, :], k.x_sb[:, bass.ds(g * TG + j, 1), :]), j == TG - 1)
                apart(k, dve)
                for j in range(TG):
                    step(nc.vector.bn_aggr(mv[:, j, :], stats[:, j, :]), j == TG - 1)
                step(nc.vector.tensor_scalar(var[:, :], mv[:, :, 1], EPS, None, ALU.add))
                rsqrt_steps(nc.vector, rstd[:, :], tmp[:, :], var[:, :], step)
                if rows is not None:
                    dve.wait_ge(rows_out, g * (16 * TG) + 1)
                    apart(k, dve)
                for j in range(TG):
                    nc.vector.tensor_scalar(xn[j][:, :], k.x_sb[:, bass.ds(g * TG + j, 1), :], mv[:, j, 0:1],
                                            rstd[:, j:j + 1], ALU.subtract, ALU.mult).then_inc(normed, 1)
                for j in range(TG):
                    at = bass.ds(g * GT + P * j, P)
                    dve.wait_ge(hi_done, g * TG + (turn * NT + j + 1))
                    nc.vector.tensor_tensor(k.xnT_lo[:, :, at], banks[j][:, :].rearrange("p (k t) -> p k t", k=KD),
                                            k.xnT_hi[:, :, at].bitcast(F32), ALU.subtract).then_inc(lo_done, 1)

        @block.tensor
        def _(pe):
            with pe.Fori(0, NG) as g:
                for j in range(TG):
                    pe.wait_ge(normed, g * TG + (turn * NT + j + 1))
                    for c in range(KD):
                        mm = nc.tensor.transpose(banks[j][:, P * c:P * (c + 1)], xn[j][:, P * c:P * (c + 1)], k.ident[:, :])
                    mm.then_inc(turned, 1)

        @block.scalar
        def _(act):
            with act.Fori(0, NG) as g:
                for j in range(TG):
                    act.wait_ge(turned, g * TG + (turn * NT + j + 1))
                    nc.scalar.copy(k.xnT_hi[:, :, bass.ds(g * GT + P * j, P)],
                                   banks[j][:, :].rearrange("p (k t) -> p k t", k=KD)).then_inc(hi_done, 1)


def attention_stage(k, name, Wq, Wk, Wv, Wo, mask=None, gq=None, gk=None):
    nc, banks = k.nc, k.banks
    rms = gq is not None
    nkv = HB if rms else 1
    kvw = nkv * HD
    b_q, b_kv, b_s, b_pt, b_o = banks[0:2], banks[2:4], banks[4:6], banks[6], banks[7]
    wq_v = Wq.rearrange("(k p) n -> p k n", p=P)
    wk_v = Wk.rearrange("(k p) n -> p k n", p=P)
    wv_v = Wv.rearrange("(k p) n -> p k n", p=P)
    wo_v = Wo.rearrange("(h p) n -> p h n", p=P)

    with ExitStack() as st:
        def sb(n, shape, dt=F32):
            return st.enter_context(nc.sbuf_tensor(f"{name}_{n}", shape, dt))

        def pair(n, shape):
            return [sb(f"{n}_hi", shape, F32R), sb(f"{n}_lo", shape, F32R)]

        def sem(n):
            return k.sem(f"{name}_{n}")

        wq, wkv, wo = pair("wq", [P, KD, HB * HD]), pair("wkv", [P, KC, 2 * kvw]), pair("wo", [P, HB, D])
        raw_a = sb("raw_a", [P, KD * HB * HD])
        raw_b = sb("raw_b", [P, KC, 2 * kvw])
        ctxT = sb("ctxT", [P, 2, KC, GT], F32R)
        qT = [pair(f"qT{h}", [P, GT]) for h in range(HB)]
        kT = [pair(f"kT{h}", [P, GT]) for h in range(nkv)]
        v = [pair(f"v{i}", [P, TG, kvw]) for i in range(2)]
        kn = sb("kn", [P, TG, kvw])
        probs = [sb(f"probs{i}", [P, 2, S]) for i in range(2)]
        pT = pair("pT", [P, 2, S])
        oT = [[pair(f"oT{i}_{h}", [P, GT]) for h in range(HB)] for i in range(2)]
        mx, nbias, rsum, rden = (sb(n, [P, 2 * UN]) for n in ("mx", "nbias", "rsum", "rden"))
        if rms:
            q2, k2 = sb("q2", [P, GT]), sb("k2", [P, HD])
            nk, nq = TG * nkv, TG * HB
            sums, var, rr, tmp = (sb(n, [P, nk + nq]) for n in ("sums", "var", "rr", "tmp"))
            of_k, of_q = slice(0, nk), slice(nk, nk + nq)
            gain_in = sb("gain_in", [P, 2])
            gain = sb("gain", [P, 1])
            ones = sb("ones", [P, 1])
        else:
            mask_u8 = sb("mask_u8", [P, T // 2], U8)
            mask_bias = sb("mask_bias", [P, T], BF16)
            scored = [sb(f"scored{i}", [P, 2, S]) for i in range(2)]
        block = st.enter_context(nc.Block())

        wq_in, wkv_in, wo_in, const_in = (sem(n) for n in ("wq_in", "wkv_in", "wo_in", "const_in"))
        ctx_in = sem("ctx_in")
        wq_split, wkv_split, wo_split, zeroed = (sem(n) for n in ("wq_split", "wkv_split", "wo_split", "zeroed"))
        w_hi = sem("w_hi")
        q_made, kv_made, k_turned, s_made, p_turned, pv_made, y_made, qsum_made = (
            sem(n) for n in ("q_made", "kv_made", "k_turned", "s_made", "p_turned", "pv_made", "y_made", "qsum_made"))
        q_hi, q_sq, kv_hi, kT_hi, exp_done, pT_hi, o_hi = (sem(n) for n in ("q_hi", "q_sq", "kv_hi", "kT_hi", "exp_done", "pT_hi", "o_hi"))
        q_split, kv_split, kT_split, pT_split, o_split, bias_done, rden_done, y_added, p_normed, dve_chain = (
            sem(n) for n in ("q_split", "kv_split", "kT_split", "pT_split", "o_split", "bias_done", "rden_done", "y_added",
                             "p_normed", "dve_chain"))
        den_chain = sem("den_chain")
        if rms:
            k_sq, k_chain, q_chain, k_ready, qsum_out, q_ready = (
                sem(n) for n in ("k_sq", "k_chain", "q_chain", "k_ready", "qsum_out", "q_ready"))

        def count(per_body, extra, hg, g):
            return hg * (NG * per_body) + (g * per_body + extra)

        PROLOGUE = (0, -1)

        @block.sync
        def _(sp):
            def load_wq(hg):
                sp.dma_start(raw_a[:, :].rearrange("p (k n) -> p k n", k=KD), wq_v[:, :, bass.ds(hg * (HB * HD), HB * HD)]).then_inc(wq_in, 16)

            def load_wkv(hg):
                at = bass.ds(hg * kvw, kvw)
                sp.dma_start(raw_b[:, :, 0:kvw], wk_v[:, :, at]).then_inc(wkv_in, 16)
                sp.dma_start(raw_b[:, :, kvw:2 * kvw], wv_v[:, :, at]).then_inc(wkv_in, 16)

            def load_ctx(m):
                sp.dma_start(ctxT[:, :, :, :].rearrange("p a k t -> p (a k t)").bitcast(F32), k.ctx_split[m % NG]).then_inc(ctx_in, 16)

            load_wq(0)
            load_wkv(0)
            load_ctx(0)
            if rms:
                sp.dma_start(gain_in[:, 0:1], gq.rearrange("(p a) -> p a", a=1)).then_inc(const_in, 16)
                sp.dma_start(gain_in[:, 1:2], gk.rearrange("(p a) -> p a", a=1)).then_inc(const_in, 16)
            else:
                flat = mask.rearrange("(a b) s -> a (b s)", a=2)
                sp.dma_start(mask_u8[:, :], flat[0:1, :].broadcast_to([P, T // 2])).then_inc(const_in, 16)
                sp.wait_ge(dve_chain, 1)
                sp.dma_start(mask_u8[:, :], flat[1:2, :].broadcast_to([P, T // 2])).then_inc(const_in, 16)
            sp.wait_ge(kv_made, TG)
            load_ctx(1)
            with sp.Fori(0, NHG) as hg:
                sp.wait_ge(wq_split, hg + 1)
                sp.dma_start(raw_a[:, :].rearrange("p (h n) -> p h n", h=HB), wo_v[:, bass.ds(hg * HB, HB), :]).then_inc(wo_in, 16)
                sp.wait_ge(wkv_split, hg + 1)
                load_wkv((hg + 1) % NHG)
                for g in range(NG):
                    sp.wait_ge(kv_made, count(TG, 2 * TG, hg, g))
                    load_ctx(g + 2)
                    if g == 1:
                        sp.wait_ge(wo_split, hg + 2)
                        load_wq((hg + 1) % NHG)
            sp.wait_ge(ctx_in, 16 * (NHG * NG + 2))
            sp.wait_ge(wkv_in, 32 * (NHG + 1))
            sp.wait_ge(wq_in, 16 * (NHG + 1))

        wq_flat = [w[:, :, :].rearrange("p k n -> p (k n)") for w in wq]
        wkv_flat = [w[:, :, :].rearrange("p k n -> p (k n)") for w in wkv]
        wo_flat = [w[:, :, :].rearrange("p h n -> p (h n)") for w in wo]
        raw_b_flat = raw_b[:, :, :].rearrange("p k n -> p (k n)")

        @block.gpsimd
        def _(pool):
            gp = nc.gpsimd

            def weights_lo(w, raw, level, done):
                pool.wait_ge(w_hi, level)
                gp.tensor_tensor(w[1], raw, w[0].bitcast(F32), ALU.subtract).then_inc(done, 1)

            norm_steps = 1 + RSQRT_STEPS

            def factors(cols, chain, hg, g):
                done = [0]

                def step(ins):
                    ins.then_inc(chain, 1)
                    done[0] += 1
                    pool.wait_ge(chain, count(norm_steps, norm_steps + done[0], hg, g))

                apart(k, pool)
                step(gp.tensor_scalar(var[:, cols], sums[:, cols], 1.0 / HD, EPS, ALU.mult, ALU.add))
                rsqrt_steps(gp, rr[:, cols], tmp[:, cols], var[:, cols], step, lambda: apart(k, pool))

            def norm_keys(hg, g):
                pool.wait_ge(kv_hi, count(TG, 2 * TG, hg, g))
                factors(of_k, k_chain, hg, g)
                kn3 = kn[:, :, :].rearrange("p t (h d) -> p (t h) d", d=HD)
                scale = rr[:, of_k].rearrange("p (a b) -> p a b", b=1).broadcast_to([P, nk, HD])
                gp.tensor_tensor(kn3, kn3, scale, ALU.mult).then_inc(k_ready, 1)

            def norm_queries(hg, g):
                pool.wait_ge(qsum_out, count(HB, 2 * HB, hg, g))
                factors(of_q, q_chain, hg, g)
                pool.sem_inc(q_ready, 1)

            zeros = [*wo_flat, *(oT[1][h][p][:, :] for h in range(HB) for p in range(2))]
            for w in zeros:
                gp.memset(w.bitcast(F32), 0.0).then_inc(zeroed, 1)
            pool.wait_ge(zeroed, len(zeros))
            pool.sem_inc(wo_split, 1)
            if rms:
                gp.memset(ones[:, :], 1.0).then_inc(const_in, 1)
            weights_lo(wq_flat, raw_a[:, :], 1, wq_split)
            weights_lo(wkv_flat, raw_b_flat, 2, wkv_split)
            if rms:
                norm_keys(*PROLOGUE)
                norm_queries(*PROLOGUE)
            with pool.Fori(0, NHG) as hg:
                for g in range(NG):
                    if g == 1:
                        weights_lo(wo_flat, raw_a[:, :], hg * 3 + 3, wo_split)
                    if rms:
                        norm_keys(hg, g)
                        norm_queries(hg, g)
                    if g == 2:
                        weights_lo(wkv_flat, raw_b_flat, hg * 3 + 4, wkv_split)
                        weights_lo(wq_flat, raw_a[:, :], hg * 3 + 5, wq_split)

        @block.tensor
        def _(pe):
            def products(out, terms):
                n = 3 * len(terms)
                i = 0
                for a, b in terms:
                    for x, y in ((0, 0), (0, 1), (1, 0)):
                        mm = nc.tensor.matmul(out, a[x], b[y], start=(i == 0), stop=(i == n - 1))
                        i += 1
                return mm

            def project_q(hg, g, h):
                ng = (g + 1) % NG
                if h == 0:
                    pe.wait_ge(wq_split, hg + (2 if g == NG - 1 else 1))
                    if g >= 0:
                        pe.wait_ge(y_added, count(TG, 1, hg, g))
                at = slice(GT * ng, GT * (ng + 1))
                products(b_q[h][:, :], [([w[:, c, HD * h:HD * (h + 1)] for w in wq], [k.xnT_hi[:, c, at], k.xnT_lo[:, c, at]])
                                        for c in range(KD)]).then_inc(q_made, 1)

            def project_kv(hg, g, t):
                if t == 0:
                    pe.wait_ge(wkv_split, hg + (2 if g == NG - 1 else 1))
                    pe.wait_ge(ctx_in, count(16, 32, hg, g))
                if t >= 2:
                    pe.wait_ge(kv_split, count(TG, TG + t - 1, hg, g))
                products(b_kv[t % 2][:, 0:2 * kvw], [([ctxT[:, a, c, P * t:P * (t + 1)] for a in range(2)], [w[:, c, :] for w in wkv])
                                                     for c in range(KC)]).then_inc(kv_made, 1)

            def sum_q(hg, g, h):
                pe.wait_ge(q_sq, count(HB, HB + h + 1, hg, g))
                pe.wait_ge(q_split, count(HB, HB + h + 1, hg, g))
                for t in range(TG):
                    mm = nc.tensor.matmul(b_q[h][:, t:t + 1], q2[:, P * t:P * (t + 1)], ones[:, :], start=True, stop=True)
                mm.then_inc(qsum_made, 1)

            def turn_k(hg, g):
                if rms:
                    pe.wait_ge(k_ready, count(1, 2, hg, g))
                pe.wait_ge(kv_split, count(TG, 2 * TG, hg, g))
                for h in range(nkv):
                    for t in range(TG):
                        mm = nc.tensor.transpose(b_kv[h][:, P * t:P * (t + 1)], kn[:, t, HD * h:HD * (h + 1)], k.ident[:, :])
                    mm.then_inc(k_turned, 1)

            def scores(hg, g, u):
                h, b = u // 2, u % 2
                if u == 0:
                    pe.wait_ge(q_split, count(HB, HB, hg, g))
                    pe.wait_ge(kT_split, count(nkv, nkv, hg, g))
                    if rms:
                        pe.wait_ge(q_ready, count(1, 1, hg, g))
                kk = kT[min(h, nkv - 1)]
                for t in range(2):
                    at = slice(S * b + P * t, S * b + P * (t + 1))
                    mm = products(b_s[u % 2][:, S * t:S * (t + 1)], [([w[:, at] for w in qT[h]], [w[:, S * b:S * (b + 1)] for w in kk])])
                mm.then_inc(s_made, 1)

            def turn_p(hg, g, u):
                pe.wait_ge(p_normed, count(UN, u + 1, hg, g))
                for t in range(2):
                    for s in range(2):
                        mm = nc.tensor.transpose(b_pt[:, S * s + P * t:S * s + P * (t + 1)], probs[u % 2][:, t, P * s:P * (s + 1)], k.ident[:, :])
                mm.then_inc(p_turned, 1)

            def weigh_v(hg, g, u):
                h, b = u // 2, u % 2
                if b == 0:
                    pe.wait_ge(o_split, count(HB, h + 1, hg, g))
                pe.wait_ge(pT_split, count(UN, u + 1, hg, g))
                vh = min(h, nkv - 1)
                products(b_o[:, S * b:S * (b + 1)], [([w[:, 2 * b + s, HD * vh:HD * (vh + 1)] for w in v[g % 2]], [w[:, s, :] for w in pT])
                                                     for s in range(2)]).then_inc(pv_made, 1)

            def project_out(hg, g, t, last=False):
                if t == 0:
                    pe.wait_ge(wo_split, hg + (1 if g == 0 else 2))
                if last and t == 0:
                    pe.wait_ge(y_added, count(TG, 1, hg, g))
                elif not last and not rms and t < 2:
                    pe.wait_ge(q_split, count(HB, 2 * HB, hg, g))
                elif not last and t < 2:
                    pe.wait_ge(qsum_out, count(HB, 2 * HB, hg, g))
                if t >= 2:
                    pe.wait_ge(y_added, count(TG, t, hg, g))
                o = oT[(g + 1) % 2]
                products(b_q[t % 2][:, :], [([w[:, P * t:P * (t + 1)] for w in o[h]], [w[:, h, :] for w in wo])
                                            for h in range(HB)]).then_inc(y_made, 1)

            if rms:
                pe.wait_ge(const_in, 33)
            for t in range(TG):
                project_kv(*PROLOGUE, t)
            for h in range(HB):
                project_q(*PROLOGUE, h)
                if rms:
                    sum_q(*PROLOGUE, h)
            turn_k(*PROLOGUE)
            with pe.Fori(0, NHG) as hg:
                for g in range(NG):
                    scores(hg, g, 0)
                    scores(hg, g, 1)
                    project_kv(hg, g, 0)
                    project_kv(hg, g, 1)
                    turn_p(hg, g, 0)
                    scores(hg, g, 2)
                    project_kv(hg, g, 2)
                    project_kv(hg, g, 3)
                    weigh_v(hg, g, 0)
                    turn_p(hg, g, 1)
                    scores(hg, g, 3)
                    project_q(hg, g, 0)
                    weigh_v(hg, g, 1)
                    turn_p(hg, g, 2)
                    project_q(hg, g, 1)
                    if rms:
                        sum_q(hg, g, 0)
                    weigh_v(hg, g, 2)
                    turn_p(hg, g, 3)
                    if rms:
                        sum_q(hg, g, 1)
                    project_out(hg, g, 0)
                    project_out(hg, g, 1)
                    weigh_v(hg, g, 3)
                    turn_k(hg, g)
                    project_out(hg, g, 2)
                    project_out(hg, g, 3)
            pe.wait_ge(o_split, HB * NHG * NG + 1)
            for t in range(TG):
                project_out(NHG, 0, t, last=True)

        @block.scalar
        def _(act):
            def copy_q(hg, g, h):
                act.wait_ge(q_made, count(HB, HB + h + 1, hg, g))
                nc.scalar.copy(qT[h][0][:, :], b_q[h][:, :]).then_inc(q_hi, 1)
                if rms:
                    if h >= 1:
                        act.wait_ge(qsum_made, count(HB, HB + h, hg, g))
                    nc.scalar.activation(q2[:, :], b_q[h][:, :], ACT.Square).then_inc(q_sq, 1)

            def copy_kv(hg, g, t):
                act.wait_ge(kv_made, count(TG, TG + t + 1, hg, g))
                nc.scalar.copy(kn[:, t, :], b_kv[t % 2][:, 0:kvw])
                if rms:
                    for h in range(nkv):
                        i = nkv * t + h
                        nc.scalar.activation(k2[:, :], b_kv[t % 2][:, HD * h:HD * (h + 1)], ACT.Square, accum_out=sums[:, i:i + 1]).then_inc(k_sq, 1)
                        act.wait_ge(k_sq, count(nk, nk + i + 1, hg, g))
                nc.scalar.copy(v[(g + 1) % 2][0][:, t, :], b_kv[t % 2][:, kvw:2 * kvw]).then_inc(kv_hi, 1)

            def copy_k(hg, g, h):
                act.wait_ge(k_turned, count(nkv, nkv + h + 1, hg, g))
                if rms:
                    nc.scalar.activation(kT[h][0][:, :], b_kv[h][:, :], ACT.Identity, scale=gain[:, 0:1]).then_inc(kT_hi, 1)
                else:
                    nc.scalar.copy(kT[h][0][:, :], b_kv[h][:, :]).then_inc(kT_hi, 1)

            def exponentials(hg, g, u):
                act.wait_ge(bias_done, count(UN, u + 1, hg, g))
                for t in range(2):
                    i = 2 * u + t
                    src = b_s[u % 2][:, S * t:S * (t + 1)] if rms else scored[u % 2][:, t, :]
                    scale = rr[:, nk + i:nk + i + 1] if rms else SM_SCALE
                    ins = nc.scalar.activation(probs[u % 2][:, t, :], src, ACT.Exp, bias=nbias[:, i:i + 1], scale=scale,
                                               accum_out=rsum[:, i:i + 1])
                ins.then_inc(exp_done, 1)

            def copy_p(hg, g, u):
                act.wait_ge(p_turned, count(UN, u + 1, hg, g))
                nc.scalar.copy(pT[0][:, :, :].rearrange("p s q -> p (s q)"), b_pt[:, :]).then_inc(pT_hi, 1)

            def copy_o(hg, g, h):
                act.wait_ge(pv_made, count(UN, 2 * h + 2, hg, g))
                nc.scalar.copy(oT[g % 2][h][0][:, :], b_o[:, :]).then_inc(o_hi, 1)

            def weights_hi(w, raw, *waits):
                for w_sem, level in waits:
                    act.wait_ge(w_sem, level)
                nc.scalar.copy(w[0], raw).then_inc(w_hi, 1)

            weights_hi(wq_flat, raw_a[:, :], (wq_in, 16))
            weights_hi(wkv_flat, raw_b_flat, (wkv_in, 32))
            for t in range(TG):
                copy_kv(*PROLOGUE, t)
            for h in range(HB):
                copy_q(*PROLOGUE, h)
            if rms:
                act.wait_ge(dve_chain, 1)
            for h in range(nkv):
                copy_k(*PROLOGUE, h)
            with act.Fori(0, NHG) as hg:
                for g in range(NG):
                    exponentials(hg, g, 0)
                    exponentials(hg, g, 1)
                    copy_kv(hg, g, 0)
                    copy_kv(hg, g, 1)
                    copy_p(hg, g, 0)
                    exponentials(hg, g, 2)
                    copy_kv(hg, g, 2)
                    copy_kv(hg, g, 3)
                    copy_p(hg, g, 1)
                    exponentials(hg, g, 3)
                    if g == 1:
                        weights_hi(wo_flat, raw_a[:, :], (wo_in, hg * 16 + 16), (y_made, count(TG, 0, hg, g)))
                    copy_q(hg, g, 0)
                    copy_o(hg, g, 0)
                    copy_p(hg, g, 2)
                    copy_q(hg, g, 1)
                    copy_p(hg, g, 3)
                    if g == 2:
                        weights_hi(wkv_flat, raw_b_flat, (wkv_in, hg * 32 + 64), (kv_made, count(TG, 2 * TG, hg, g)))
                        weights_hi(wq_flat, raw_a[:, :], (wq_in, hg * 16 + 32), (q_made, count(HB, 2 * HB, hg, g)))
                    copy_o(hg, g, 1)
                    for h in range(nkv):
                        copy_k(hg, g, h)

        @block.vector
        def _(dve):
            def lo(pair, src, done):
                nc.vector.tensor_tensor(pair[1], src, pair[0].bitcast(F32), ALU.subtract).then_inc(done, 1)

            def split_q(hg, g, h):
                dve.wait_ge(q_sq if rms else q_hi, count(HB, HB + h + 1, hg, g))
                lo([w[:, :] for w in qT[h]], b_q[h][:, :], q_split)

            def split_kv(hg, g, t):
                dve.wait_ge(kv_hi, count(TG, TG + t + 1, hg, g))
                lo([w[:, t, :] for w in v[(g + 1) % 2]], b_kv[t % 2][:, kvw:2 * kvw], kv_split)

            def split_k(hg, g, h):
                dve.wait_ge(kT_hi, count(nkv, nkv + h + 1, hg, g))
                if rms:
                    nc.vector.scalar_tensor_tensor(kT[h][1][:, :], b_kv[h][:, :], gain[:, 0:1], kT[h][0][:, :].bitcast(F32),
                                                   ALU.mult, ALU.subtract).then_inc(kT_split, 1)
                else:
                    lo([w[:, :] for w in kT[h]], b_kv[h][:, :], kT_split)

            def split_p(hg, g, u):
                dve.wait_ge(pT_hi, count(UN, u + 1, hg, g))
                lo([w[:, :, :].rearrange("p s q -> p (s q)") for w in pT], b_pt[:, :], pT_split)

            def split_o(hg, g, h):
                dve.wait_ge(o_hi, count(HB, h + 1, hg, g))
                lo([w[:, :] for w in oT[g % 2][h]], b_o[:, :], o_split)

            before_loop = 1 if rms else 2

            def biases(hg, g, u):
                i = slice(2 * u, 2 * u + 2)
                dve.wait_ge(s_made, count(UN, u + 1, hg, g))
                if rms:
                    nc.vector.tensor_reduce(mx[:, i], b_s[u % 2][:, :].rearrange("p (t s) -> p t s", t=2), AX.X, ALU.max).then_inc(dve_chain, 1)
                    dve.wait_ge(dve_chain, count(UN, before_loop + u + 1, hg, g))
                    nc.vector.scalar_tensor_tensor(nbias[:, i], mx[:, i], -1.0, rr[:, nk + 2 * u:nk + 2 * u + 2],
                                                   ALU.mult, ALU.mult).then_inc(bias_done, 1)
                else:
                    at = S * (2 * g + u % 2)
                    apart(k, dve)
                    for t in range(2):
                        ins = nc.vector.tensor_tensor_reduce(scored[u % 2][:, t, :], b_s[u % 2][:, S * t:S * (t + 1)], mask_bias[:, at:at + S],
                                                             1.0, MAX_FLOOR, ALU.add, ALU.max, mx[:, 2 * u + t:2 * u + t + 1])
                    ins.then_inc(dve_chain, 1)
                    dve.wait_ge(dve_chain, count(UN, before_loop + u + 1, hg, g))
                    nc.vector.tensor_scalar(nbias[:, i], mx[:, i], -SM_SCALE, None, ALU.mult).then_inc(bias_done, 1)

            def denominators(hg, g, u):
                i = slice(2 * u, 2 * u + 2)
                dve.wait_ge(exp_done, count(UN, u + 1, hg, g))
                if not rms:
                    nc.vector.tensor_scalar(rsum[:, i], rsum[:, i], 1e-30, None, ALU.max).then_inc(den_chain, 1)
                    dve.wait_ge(den_chain, count(UN, u + 1, hg, g))
                nc.vector.reciprocal(rden[:, i], rsum[:, i]).then_inc(rden_done, 1)
                dve.wait_ge(rden_done, count(UN, u + 1, hg, g))
                for t in range(2):
                    row = probs[u % 2][:, t, :]
                    ins = nc.vector.tensor_scalar(row, row, rden[:, 2 * u + t:2 * u + t + 1], None, ALU.mult)
                ins.then_inc(p_normed, 1)

            def take_sums(hg, g, h):
                i = nk + TG * h
                dve.wait_ge(qsum_made, count(HB, HB + h + 1, hg, g))
                nc.vector.tensor_copy(sums[:, i:i + TG], b_q[h][:, 0:TG]).then_inc(qsum_out, 1)

            def add_y(hg, g, t):
                dve.wait_ge(y_made, count(TG, t + 1, hg, g))
                row = k.x_sb[:, TG * ((g - 1) % NG) + t, :]
                nc.vector.tensor_tensor(row, b_q[t % 2][:, :], row, ALU.add).then_inc(y_added, 1)

            if rms:
                dve.wait_ge(const_in, 33)
                nc.vector.scalar_tensor_tensor(gain[:, :], gain_in[:, 0:1], SM_SCALE, gain_in[:, 1:2], ALU.mult, ALU.mult).then_inc(dve_chain, 1)
            else:
                half = T // 2
                for i in range(2):
                    dve.wait_ge(const_in, 16 * (i + 1))
                    nc.vector.tensor_scalar(mask_bias[:, half * i:half * (i + 1)], mask_u8[:, :], -MASKED, MASKED, ALU.mult, ALU.add).then_inc(dve_chain, 1)
                dve.wait_ge(dve_chain, 2)
            dve.sem_inc(y_added, 1)
            dve.sem_inc(o_split, 1)
            for t in range(TG):
                split_kv(*PROLOGUE, t)
            for h in range(HB):
                split_q(*PROLOGUE, h)
                if rms:
                    take_sums(*PROLOGUE, h)
            for h in range(nkv):
                split_k(*PROLOGUE, h)
            with dve.Fori(0, NHG) as hg:
                for g in range(NG):
                    biases(hg, g, 0)
                    biases(hg, g, 1)
                    denominators(hg, g, 0)
                    denominators(hg, g, 1)
                    split_kv(hg, g, 0)
                    split_kv(hg, g, 1)
                    split_p(hg, g, 0)
                    biases(hg, g, 2)
                    denominators(hg, g, 2)
                    split_kv(hg, g, 2)
                    split_kv(hg, g, 3)
                    split_p(hg, g, 1)
                    biases(hg, g, 3)
                    denominators(hg, g, 3)
                    split_q(hg, g, 0)
                    split_o(hg, g, 0)
                    split_p(hg, g, 2)
                    if rms:
                        take_sums(hg, g, 0)
                    split_q(hg, g, 1)
                    split_p(hg, g, 3)
                    if rms:
                        take_sums(hg, g, 1)
                    add_y(hg, g, 0)
                    add_y(hg, g, 1)
                    split_o(hg, g, 1)
                    for h in range(nkv):
                        split_k(hg, g, h)
                    add_y(hg, g, 2)
                    add_y(hg, g, 3)
            for t in range(TG):
                add_y(NHG, 0, t)


def ffn_stage(k, gate_w, up_w, down_w, gate_scale, up_scale, down_scale):
    nc, banks = k.nc, k.banks
    half = 3 * D // 2
    gate_v = gate_w.rearrange("(k p) f -> p k f", p=P)
    up_v = up_w.rearrange("(k p) f -> p k f", p=P)
    down_v = down_w.rearrange("(f p) n -> p f n", p=P)
    b_gate, b_up, b_y = banks[0:2], banks[2:4], banks[4:8]
    with ExitStack() as st:
        def sb(n, shape, dt=F32):
            return st.enter_context(nc.sbuf_tensor(f"ffn_{n}", shape, dt))

        def sem(n):
            return k.sem(f"ffn_{n}")

        w = sb("w", [P, NF, 3 * D], F32R)
        raw = [sb(f"raw{i}", [P, half]) for i in range(2)]
        magic = [sb(f"magic{i}", [P, half]) for i in range(2)]
        silu = [sb(f"silu{i}", [P, GT]) for i in range(2)]
        fuse = [sb(f"fuse{i}", [P, GT]) for i in range(2)]
        fz = [[sb(f"fz{i}_{p}", [P, GT], F32R) for p in ("hi", "lo")] for i in range(2)]
        scale_rows = sb("scale_rows", [2 * NF, P])
        scales, dsc = sb("scales", [P, 2 * NF]), sb("dsc", [P, D])
        ysc = [sb(f"ysc{i}", [P, D]) for i in range(2)]
        block = st.enter_context(nc.Block())
        raw_in = [sem(f"raw_in{i}") for i in range(2)]
        scales_turned, scales_ready = sem("scales_turned"), sem("scales_ready")
        scales_in, magic_chain, magic_made, round_chain, w_ready = (
            sem(n) for n in ("scales_in", "magic_chain", "magic_made", "round_chain", "w_ready"))
        gate_made, up_made, silu_done, fuse_done, fz_hi, fz_split, y_made, y_chain, y_added = (
            sem(n) for n in ("gate_made", "up_made", "silu_done", "fuse_done", "fz_hi", "fz_split", "y_made", "y_chain", "y_added"))

        @block.sync
        def _(sp):
            def load(f):
                at = bass.ds(f * P, P)
                r0 = raw[0][:, :].rearrange("p (k f) -> p k f", f=P)
                sp.dma_start(r0[:, 0:KD, :], gate_v[:, :, at]).then_inc(raw_in[0], 16)
                sp.dma_start(r0[:, KD:half // P, :], up_v[:, 0:2, at]).then_inc(raw_in[0], 16)
                yield
                r1 = raw[1][:, 0:2 * P].rearrange("p (k f) -> p k f", f=P)
                sp.dma_start(r1, up_v[:, 2:4, at]).then_inc(raw_in[1], 16)
                sp.dma_start(raw[1][:, 2 * P:half], down_v[:, bass.ds(f, 1), :]).then_inc(raw_in[1], 16)
                yield

            for _ in load(0):
                pass
            sp.dma_start(scale_rows[0:NF, :], gate_scale.rearrange("(f p) -> f p", p=P)).then_inc(scales_in, 16)
            sp.dma_start(scale_rows[NF:2 * NF, :], up_scale.rearrange("(f p) -> f p", p=P)).then_inc(scales_in, 16)
            sp.dma_start(dsc[:, :], down_scale.rearrange("(a n) -> a n", a=1).broadcast_to([P, D])).then_inc(scales_in, 16)
            with sp.Fori(0, NF - 1) as f:
                steps = load(f + 1)
                for c in range(2):
                    sp.wait_ge(w_ready, f * 2 + (c + 1))
                    next(steps)

        @block.gpsimd
        def _(pool):
            with pool.Fori(0, NF) as f:
                for c in range(2):
                    pool.wait_ge(magic_made, f * 2 + (c + 1))
                    nc.gpsimd.tensor_tensor(raw[c][:, :], raw[c][:, :], magic[c][:, :], ALU.add).then_inc(round_chain, 1)
                    pool.wait_ge(round_chain, f * 2 + (c + 1))
                    nc.gpsimd.tensor_tensor(w[:, bass.ds(f, 1), half * c:half * (c + 1)], raw[c][:, :], magic[c][:, :],
                                            ALU.subtract).then_inc(w_ready, 1)
            with pool.Fori(0, NG) as g:
                for f in range(NF):
                    pool.wait_ge(fuse_done, g * NF + (f + 1))
                    apart(k, pool)
                    nc.gpsimd.tensor_copy(fz[f % 2][0][:, :], fuse[f % 2][:, :]).then_inc(fz_hi, 1)
                    pool.wait_ge(fz_hi, g * NF + (f + 1))
                    nc.gpsimd.tensor_tensor(fz[f % 2][1][:, :], fuse[f % 2][:, :], fz[f % 2][0][:, :].bitcast(F32),
                                            ALU.subtract).then_inc(fz_split, 1)

        @block.vector
        def _(dve):
            with dve.Fori(0, NF) as f:
                for c in range(2):
                    dve.wait_ge(raw_in[c], f * 32 + 32)
                    nc.vector.tensor_scalar(magic[c][:, :].bitcast(U32), raw[c][:, :].bitcast(U32), 0x7F800000, None,
                                            ALU.bitwise_and).then_inc(magic_chain, 1)
                    dve.wait_ge(magic_chain, f * 2 + (c + 1))
                    nc.vector.tensor_scalar(magic[c][:, :], magic[c][:, :], 2.0 ** -6, 1.5 * 2.0 ** 20, ALU.max, ALU.mult).then_inc(magic_made, 1)
            dve.wait_ge(scales_turned, 1)
            nc.vector.tensor_copy(scales[:, :], b_gate[0][:, 0:2 * NF]).then_inc(scales_ready, 1)
            dve.wait_ge(scales_ready, 1)
            with dve.Fori(0, NG) as g:
                for f in range(NF):
                    dve.wait_ge(silu_done, g * NF + (f + 1))
                    dve.wait_ge(up_made, g * NF + (f + 1))
                    nc.vector.scalar_tensor_tensor(fuse[f % 2][:, :], b_up[f % 2][:, :], scales[:, NF + f:NF + f + 1], silu[f % 2][:, :],
                                                   ALU.mult, ALU.mult).then_inc(fuse_done, 1)
                for t in range(TG):
                    dve.wait_ge(y_made, g * TG + (t + 1))
                    nc.vector.tensor_tensor(ysc[t % 2][:, :], b_y[t][:, :], dsc[:, :], ALU.mult).then_inc(y_chain, 1)
                    dve.wait_ge(y_chain, g * TG + (t + 1))
                    row = k.x_sb[:, bass.ds(g * TG + t, 1), :]
                    nc.vector.tensor_tensor(row, ysc[t % 2][:, :], row, ALU.add).then_inc(y_added, 1)

        @block.scalar
        def _(act):
            act.wait_ge(scales_ready, 1)
            with act.Fori(0, NG) as g:
                for f in range(NF):
                    act.wait_ge(gate_made, g * NF + (f + 1))
                    nc.scalar.activation(silu[f % 2][:, :], b_gate[f % 2][:, :], ACT.Silu, scale=scales[:, f:f + 1]).then_inc(silu_done, 1)

        @block.tensor
        def _(pe):
            pe.wait_ge(scales_in, 48)
            nc.tensor.transpose(b_gate[0][:, 0:2 * NF], scale_rows[:, :], k.ident[0:2 * NF, 0:2 * NF]).then_inc(scales_turned, 1)
            pe.wait_ge(scales_ready, 1)
            pe.wait_ge(w_ready, 2 * NF)
            with pe.Fori(0, NG) as g:
                def down(f):
                    pe.wait_ge(fz_split, g * NF + (f + 1))
                    for t in range(TG):
                        for part in fz[f % 2]:
                            mm = nc.tensor.matmul(b_y[t][:, :], part[:, P * t:P * (t + 1)], w[:, f, 2 * D:3 * D],
                                                  start=(f == 0 and part is fz[f % 2][0]), stop=(f == NF - 1 and part is fz[f % 2][1]))
                        if f == NF - 1:
                            mm.then_inc(y_made, 1)

                at = bass.ds(g * GT, GT)
                for f in range(NF):
                    for out, first, done in ((b_gate, 0, gate_made), (b_up, D, up_made)):
                        for c in range(KD):
                            for part in (k.xnT_hi, k.xnT_lo):
                                mm = nc.tensor.matmul(out[f % 2][:, :], w[:, f, first + P * c:first + P * (c + 1)], part[:, c, at],
                                                      start=(c == 0 and part is k.xnT_hi), stop=(c == KD - 1 and part is k.xnT_lo))
                        mm.then_inc(done, 1)
                    if f >= 1:
                        down(f - 1)
                down(NF - 1)


def moe_stage(k, xn_rows, gate_w, gate_up, down_proj, out):
    nc, banks = k.nc, k.banks
    KI = I // P
    HALVES = 2
    ROWS = HALVES * P
    TILES = 2 * T // ROWS + E
    ITER = TILES // 2
    LISTED = TILES + 2
    SLOTS = LISTED * HALVES
    STEPS = 2 * HALVES
    GU, DN = KD * 2 * I, KI * D
    NOWHERE = 65536.0
    ROUND = 1.5 * 2.0 ** 23
    y_rows = nc.dram_tensor("moe_y_rows", (2 * T, D), F32, kind="Internal").ap()
    gu_v = gate_up.rearrange("e (p k) f -> (e p) (k f)", p=P)
    dn_v = down_proj.rearrange("e (p k) n -> (e p) (k n)", p=P)
    with ExitStack() as st:
        def sb(n, shape, dt=F32):
            return st.enter_context(nc.sbuf_tensor(f"moe_{n}", shape, dt))

        def sem(n):
            return k.sem(f"moe_{n}")

        def pair(n, shape):
            return [sb(f"{n}_hi", shape, F32R), sb(f"{n}_lo", shape, F32R)]

        raw_gu, raw_dn = ([sb(f"raw_{n}{i}", [P, c]) for i in range(2)] for n, c in (("gu", GU), ("dn", DN)))
        w_gu, w_dn = ([pair(f"w_{n}{i}", [P, c]) for i in range(2)] for n, c in (("gu", GU), ("dn", DN)))
        rows = [sb(f"rows{i}", [P, D]) for i in range(STEPS)]
        xT = [[x[:, :, P * i:P * (i + 1)] for x in (k.xnT_hi, k.xnT_lo)] for i in range(2)]
        fT = [[x[:, 0:KI, P * (2 + i):P * (3 + i)] for x in (k.xnT_hi, k.xnT_lo)] for i in range(2)]
        silu = [sb(f"silu{i}", [P, I]) for i in range(2)]
        fuse = [sb(f"fuse{i}", [P, I]) for i in range(2)]
        y_sb = [sb(f"y_sb{i}", [P, D]) for i in range(STEPS)]
        gather_at = [sb(f"gather_at{i}", [P, HALVES + 1], I32) for i in range(2)]
        scatter_at = [sb(f"scatter_at{i}", [P, 1], I32) for i in range(STEPS)]
        token_of, dest_of, expert_of = sb("token_of", [P, SLOTS], I32), sb("dest_of", [P, SLOTS], I32), sb("expert_of", [P, LISTED], I32)
        gw = sb("gw", [E, D])
        gwT = pair("gwT", [P, KD, E])
        prob, eq, pick1, pick2, slots = (sb(n, [P, NT, E]) for n in ("prob", "eq", "pick1", "pick2", "slots"))
        both = sb("both", [P, NT, E], F32R)
        before, ones = (sb(n, [P, P], F32R) for n in ("before", "ones"))
        before_f, ones_f, after = sb("before_f", [P, P]), sb("ones_f", [P, P]), sb("after", [P, E, E])
        cum = sb("cum", [P, NT + 1, E])
        need, first_slot, last_tile = (sb(n, [P, E]) for n in ("need", "first_slot", "last_tile"))
        passed = sb("passed", [P, LISTED, E])
        slot, half, row_of = (sb(n, [P, 2, NT]) for n in ("slot", "half", "row_of"))
        table, empty, found = sb("table", [P, SLOTS]), sb("empty", [P, SLOTS]), sb("found", [P, LISTED])
        m1, m2, ms, key = (sb(n, [P, NT]) for n in ("m1", "m2", "ms", "key"))
        counts_i = sb("counts_i", [P, E + P + 2 * NT + 1], I32)
        counts = sb("counts", [P, E + P + 2 * NT + 1])
        rank, column = counts[:, 0:E], counts[:, E:E + P]
        name_of, part = counts[:, E + P:E + P + 2 * NT], counts[:, E + P + 2 * NT:E + P + 2 * NT + 1]

        block = st.enter_context(nc.Block())
        gw_in, gw_turned, gw_hi, gw_split, logits_made, prob_made, consts_made, route_chain, picked, ranked, sorted_, tabled, listed = (
            sem(n) for n in ("gw_in", "gw_turned", "gw_hi", "gw_split", "logits_made", "prob_made", "consts_made", "route_chain",
                             "picked", "ranked", "sorted", "tabled", "listed"))
        gu_in, dn_in, rows_in = ([sem(f"{n}_in{i}") for i in range(2)] for n in ("gu", "dn", "rows"))
        y_out = [sem(f"y_out{i}") for i in range(STEPS)]
        x_turned, x_hi, x_split, wg_hi, wg_split, wd_hi, wd_split = (
            sem(n) for n in ("x_turned", "x_hi", "x_split", "wg_hi", "wg_split", "wd_hi", "wd_split"))
        gu_made, silu_done, fused, f_turned, f_hi, f_split, y_made, y_copied = (
            sem(n) for n in ("gu_made", "silu_done", "fused", "f_turned", "f_hi", "f_split", "y_made", "y_copied"))
        gather_set, scatter_set, pairs_in, summed, stored = (
            sem(n) for n in ("gather_set", "scatter_set", "pairs_in", "summed", "stored"))
        pairs_in = [pairs_in, sem("pairs_in1")]
        b_x, b_gu, b_f, b_y = banks[0:2], banks[2:4], banks[4], banks[5:7]
        FIRST = (None, 0)

        def level(it, per, extra):
            reg, add = it
            return add * per + extra if reg is None else reg * per + (add * per + extra)

        def wait(eng, s, it, per, extra):
            n = level(it, per, extra)
            if it[0] is not None or n > 0:
                eng.wait_ge(s, n)

        def iterations(eng, body):
            body(FIRST)
            with eng.Fori(0, ITER - 1) as i:
                body((i, 1))

        def step(it, s):
            return (it[0], it[1] + s // STEPS), s % STEPS

        def exists(it, s):
            return it is not FIRST or s >= 0

        def one_hots(c):
            space = w_gu[0][c]
            return (space[:, :].rearrange("p (t r) -> p t r", r=P), w_gu[1][c][:, 0:NT * SLOTS].rearrange("p (t j) -> p t j", j=SLOTS))

        @block.sync
        def _(sp):
            sp.dma_start(gw[:, :], gate_w).then_inc(gw_in, 16)
            for s in range(STEPS):
                sp.wait_ge(y_out[s], 16 * ITER)
            for b in range(2):
                sp.wait_ge(gu_in[b], 16 * (ITER + 1))
                sp.wait_ge(dn_in[b], 16 * (ITER + 1))
                sp.wait_ge(rows_in[b], 32 * (ITER + 1))
            yv = y_rows.rearrange("(t p k) d -> p t (k d)", p=P, k=2)
            ov = out.rearrange("b (t p) d -> p (b t) d", p=P)
            for n in range(NT // 2):
                if n >= 2:
                    sp.wait_ge(summed, 2 * (n - 1))
                sp.dma_start(raw_gu[n % 2][:, :].rearrange("p (t c) -> p t c", t=2), yv[:, 2 * n:2 * (n + 1), :]).then_inc(pairs_in[n % 2], 16)
                if n >= 1:
                    sp.wait_ge(summed, 2 * n)
                    sp.dma_start(ov[:, 2 * (n - 1):2 * n, :], k.x_sb[:, 2 * (n - 1):2 * n, :]).then_inc(stored, 16)
            sp.wait_ge(summed, NT)
            sp.dma_start(ov[:, NT - 2:NT, :], k.x_sb[:, NT - 2:NT, :]).then_inc(stored, 16)
            sp.wait_ge(stored, 16 * NT // 2)

        @block.gpsimd
        def _(pool):
            gp = nc.gpsimd
            gp.iota(counts_i[:, 0:E], pattern=[[-1, E]], base=E, channel_multiplier=0).then_inc(consts_made, 1)
            gp.iota(counts_i[:, E:E + P], pattern=[[1, P]], base=0, channel_multiplier=0).then_inc(consts_made, 1)
            gp.iota(counts_i[:, E + P:E + P + 2 * NT], pattern=[[1, 2], [2 * P, NT]], base=1, channel_multiplier=2).then_inc(consts_made, 1)
            gp.iota(counts_i[:, E + P + 2 * NT:], pattern=[[0, 1]], base=0, channel_multiplier=1).then_inc(consts_made, 1)
            gp.memset(ones_f[:, :], 1.0).then_inc(consts_made, 1)
            gp.memset(after[:, :, :], 1.0).then_inc(consts_made, 1)
            pool.wait_ge(consts_made, 6)
            gp.affine_select(out=before_f[:, :], in_=ones_f[:, :], compare_op=ALU.is_ge, fill=0.0, base=-1,
                             pattern=[[1, P]], channel_multiplier=-1).then_inc(consts_made, 1)
            gp.affine_select(out=after[:, :, :], in_=after[:, :, :], compare_op=ALU.is_ge, fill=0.0, base=0,
                             pattern=[[1, E], [-1, E]], channel_multiplier=0).then_inc(consts_made, 1)
            for r in rows:
                gp.memset(r[:, :], 0.0).then_inc(consts_made, 1)
            pool.wait_ge(consts_made, 8 + STEPS)

            def gather_weights(it, b):
                wait(pool, gather_set, it, 2, b + 1)
                wait(pool, wg_split, it, 4, 2 * b - 2)
                apart(k, pool)
                at = bass.IndirectOffsetOnAxis(ap=gather_at[b][:, HALVES:HALVES + 1], axis=0)
                gp.indirect_dma_start(raw_gu[b][:, :], None, gu_v, at, bounds_check=E * P - 1, oob_is_err=False).then_inc(gu_in[b], 16)

            def gather_down(it, b):
                wait(pool, wd_split, it, 2, b - 1)
                apart(k, pool)
                at = bass.IndirectOffsetOnAxis(ap=gather_at[b][:, HALVES:HALVES + 1], axis=0)
                gp.indirect_dma_start(raw_dn[b][:, :], None, dn_v, at, bounds_check=E * P - 1, oob_is_err=False).then_inc(dn_in[b], 16)

            def gather_rows(it, b):
                wait(pool, x_turned, it, STEPS, HALVES * b - 2)
                apart(k, pool)
                for h in range(HALVES):
                    at = bass.IndirectOffsetOnAxis(ap=gather_at[b][:, h:h + 1], axis=0)
                    gp.indirect_dma_start(rows[HALVES * b + h][:, :], None, xn_rows, at, bounds_check=T - 1,
                                          oob_is_err=False).then_inc(rows_in[b], 16)

            def scatter(it, s):
                wait(pool, scatter_set, it, STEPS, s + 1)
                wait(pool, y_copied, it, STEPS, s + 1)
                apart(k, pool)
                at = bass.IndirectOffsetOnAxis(ap=scatter_at[s][:, :], axis=0)
                gp.indirect_dma_start(y_rows, at, y_sb[s][:, :], None, bounds_check=2 * T - 1, oob_is_err=False).then_inc(y_out[s], 16)

            for b in range(2):
                gather_weights(FIRST, b)
                gather_rows(FIRST, b)
                gather_down(FIRST, b)

            def body(it):
                reg, add = it
                after_it, before_it = (reg, add + 1), (reg, add - 1)
                for b in range(2):
                    gather_weights(after_it, b)
                    if b == 1 or it is not FIRST:
                        for h in range(HALVES):
                            scatter(before_it if b == 0 else it, HALVES * (1 - b) + h)
                    gather_rows(after_it, b)
                    gather_down(after_it, b)

            iterations(pool, body)
            for h in range(HALVES):
                scatter((None, ITER - 1), HALVES + h)

        @block.tensor
        def _(pe):
            pe.wait_ge(gw_in, 16)
            for c in range(KD):
                mm = nc.tensor.transpose(b_gu[0][:, E * c:E * (c + 1)], gw[:, P * c:P * (c + 1)], k.ident[0:E, 0:E])
            mm.then_inc(gw_turned, 1)
            pe.wait_ge(gw_split, 1)
            for t in range(NT):
                i = 0
                for c in range(KD):
                    at = slice(P * t, P * (t + 1))
                    for a, b in ((k.xnT_hi, gwT[0]), (k.xnT_hi, gwT[1]), (k.xnT_lo, gwT[0])):
                        mm = nc.tensor.matmul(b_y[0][:, E * t:E * (t + 1)], a[:, c, at], b[:, c, :], start=(i == 0), stop=(i == 3 * KD - 1))
                        i += 1
            mm.then_inc(logits_made, 1)
            pe.wait_ge(picked, 1)
            chosen = both[:, :, :].rearrange("p t e -> p (t e)")
            nc.tensor.matmul(b_gu[1][:, 0:NT * E], before[:, :], chosen, start=True, stop=True)
            nc.tensor.matmul(b_gu[0][:, 0:NT * E], ones[:, :], chosen, start=True, stop=True).then_inc(ranked, 1)
            for c in range(2):
                pe.wait_ge(sorted_, c + 1)
                for t in range(NT):
                    mm = nc.tensor.matmul(b_y[1][:, 0:SLOTS], one_hots(c)[0][:, t, :], one_hots(c)[1][:, t, :],
                                          start=(c == 0 and t == 0), stop=(c == 1 and t == NT - 1))
            mm.then_inc(tabled, 1)

            def turn_x(it, s):
                if s % HALVES == 0:
                    wait(pe, rows_in[s // HALVES], it, 32, 32)
                wait(pe, x_split, it, STEPS, s - 1)
                by_feature = rows[s][:, :].rearrange("p (q k) -> p k q", k=KD)
                for c in range(KD):
                    mm = nc.tensor.transpose(b_x[s % 2][:, P * c:P * (c + 1)], by_feature[:, c, :], k.ident[:, :])
                mm.then_inc(x_turned, 1)

            def gate_up_products(it, s):
                b = s // HALVES
                if s % HALVES == 0:
                    wait(pe, wg_split, it, 4, 2 * (b + 1))
                wait(pe, x_split, it, STEPS, s + 1)
                wait(pe, fused, it, STEPS, s - 1)
                j = 0
                for c in range(KD):
                    for x, w in ((0, 0), (0, 1), (1, 0)):
                        mm = nc.tensor.matmul(b_gu[s % 2][:, :], xT[s % 2][x][:, c, :], w_gu[b][w][:, 2 * I * c:2 * I * (c + 1)],
                                              start=(j == 0), stop=(j == 3 * KD - 1))
                        j += 1
                mm.then_inc(gu_made, 1)

            def turn_f(it, s):
                wait(pe, fused, it, STEPS, s + 1)
                wait(pe, f_split, it, STEPS, s)
                by_feature = fuse[s % 2][:, :].rearrange("p (q k) -> p k q", k=KI)
                for c in range(KI):
                    mm = nc.tensor.transpose(b_f[:, P * c:P * (c + 1)], by_feature[:, c, :], k.ident[:, :])
                mm.then_inc(f_turned, 1)

            def down(it, s):
                b = s // HALVES
                if s % HALVES == 0:
                    wait(pe, wd_split, it, 2, b + 1)
                wait(pe, f_split, it, STEPS, s + 1)
                wait(pe, y_copied, it, STEPS, s - 1)
                j = 0
                for c in range(KI):
                    for f, w in ((0, 0), (0, 1), (1, 0)):
                        mm = nc.tensor.matmul(b_y[s % 2][:, :], fT[s % 2][f][:, c, :], w_dn[b][w][:, D * c:D * (c + 1)],
                                              start=(j == 0), stop=(j == 3 * KI - 1))
                        j += 1
                mm.then_inc(y_made, 1)

            pe.wait_ge(listed, 1)
            turn_x(FIRST, 0)

            def body(it):
                for s in range(STEPS):
                    turn_x(*step(it, s + 1))
                    gate_up_products(it, s)
                    if exists(it, s - 1):
                        turn_f(*step(it, s - 1))
                    if exists(it, s - 2):
                        down(*step(it, s - 2))

            iterations(pe, body)
            end = (None, ITER)
            turn_f(*step(end, -1))
            down(*step(end, -2))
            down(*step(end, -1))

        @block.scalar
        def _(act):
            act.wait_ge(gw_turned, 1)
            nc.scalar.copy(gwT[0][:, :, :].rearrange("p k e -> p (k e)"), b_gu[0][:, 0:KD * E]).then_inc(gw_hi, 1)
            act.wait_ge(logits_made, 1)
            nc.scalar.activation(prob[:, :, :].rearrange("p t e -> p (t e)"), b_y[0][:, 0:NT * E], ACT.Sigmoid).then_inc(prob_made, 1)

            def copy_x(it, s):
                wait(act, x_turned, it, STEPS, s + 1)
                wait(act, gu_made, it, STEPS, s - 1)
                nc.scalar.copy(xT[s % 2][0], b_x[s % 2][:, :].rearrange("p (k t) -> p k t", k=KD)).then_inc(x_hi, 1)

            def weights_gate_up(it, b, c):
                cols = slice(GU // 2 * c, GU // 2 * (c + 1))
                if c == 0:
                    wait(act, gu_in[b], it, 16, 16)
                    wait(act, gu_made, it, STEPS, HALVES * b - 2)
                nc.scalar.copy(w_gu[b][0][:, cols], raw_gu[b][:, cols]).then_inc(wg_hi, 1)

            def weights_down(it, b):
                wait(act, dn_in[b], it, 16, 16)
                wait(act, y_made, it, STEPS, HALVES * b - 2)
                nc.scalar.copy(w_dn[b][0][:, :], raw_dn[b][:, :]).then_inc(wd_hi, 1)

            def gate(it, s):
                wait(act, gu_made, it, STEPS, s + 1)
                wait(act, fused, it, STEPS, s - 1)
                nc.scalar.activation(silu[s % 2][:, :], b_gu[s % 2][:, 0:I], ACT.Silu).then_inc(silu_done, 1)

            def copy_f(it, s):
                wait(act, f_turned, it, STEPS, s + 1)
                wait(act, y_made, it, STEPS, s - 1)
                nc.scalar.copy(fT[s % 2][0], b_f[:, 0:I].rearrange("p (k t) -> p k t", k=KI)).then_inc(f_hi, 1)

            def copy_y(it, s):
                wait(act, y_made, it, STEPS, s + 1)
                wait(act, y_out[s], it, 16, 0)
                nc.scalar.copy(y_sb[s][:, :], b_y[s % 2][:, :]).then_inc(y_copied, 1)

            act.wait_ge(tabled, 1)
            for c in range(2):
                weights_gate_up(FIRST, 0, c)
            copy_x(FIRST, 0)

            def body(it):
                for s in range(STEPS):
                    b = s // HALVES
                    copy_x(*step(it, s + 1))
                    nxt = step(it, HALVES * (b + 1))
                    weights_gate_up(nxt[0], 1 - b, s % HALVES)
                    if s % HALVES == 0:
                        weights_down(it, b)
                    gate(it, s)
                    if exists(it, s - 1):
                        copy_f(*step(it, s - 1))
                    if exists(it, s - 2):
                        copy_y(*step(it, s - 2))

            iterations(act, body)
            end = (None, ITER)
            copy_f(*step(end, -1))
            copy_y(*step(end, -2))
            copy_y(*step(end, -1))

        @block.vector
        def _(dve):
            v = nc.vector
            dve.wait_ge(gw_hi, 1)
            v.tensor_tensor(gwT[1][:, :, :].rearrange("p k e -> p (k e)"), b_gu[0][:, 0:KD * E],
                            gwT[0][:, :, :].rearrange("p k e -> p (k e)").bitcast(F32), ALU.subtract).then_inc(gw_split, 1)
            done = [0]

            def chain(ins):
                ins.then_inc(route_chain, 1)
                done[0] += 1
                dve.wait_ge(route_chain, done[0])

            def over_e(a):
                return a.rearrange("p (t o) -> p t o", o=1).broadcast_to([P, NT, E])

            def over_t(a, n=NT):
                return a.rearrange("p (o e) -> p o e", o=1).broadcast_to([P, n, E])

            def pick(best, chosen):
                chain(v.tensor_reduce(best[:, :], prob[:, :, :], AX.X, ALU.max))
                chain(v.tensor_tensor(eq[:, :, :], prob[:, :, :], over_e(best[:, :]), ALU.is_equal))
                chain(v.tensor_tensor(eq[:, :, :], eq[:, :, :], over_t(rank), ALU.mult))
                chain(v.tensor_reduce(key[:, :], eq[:, :, :], AX.X, ALU.max))
                chain(v.tensor_tensor(chosen[:, :, :], eq[:, :, :], over_e(key[:, :]), ALU.is_equal))

            def rounded(out, a, scale, offset):
                chain(v.tensor_scalar(out, a, scale, offset, ALU.mult, ALU.add))
                chain(v.tensor_scalar(out, out, ROUND, None, ALU.add))
                chain(v.tensor_scalar(out, out, -ROUND, None, ALU.add))

            dve.wait_ge(consts_made, 8)
            v.tensor_copy(before[:, :], before_f[:, :])
            v.tensor_copy(ones[:, :], ones_f[:, :])
            chain(v.tensor_copy(counts[:, :], counts_i[:, :]))
            dve.wait_ge(prob_made, 1)
            chain(v.tensor_reduce(ms[:, :], prob[:, :, :], AX.X, ALU.add))
            chain(v.reciprocal(ms[:, :], ms[:, :]))
            chain(v.tensor_tensor(prob[:, :, :], prob[:, :, :], over_e(ms[:, :]), ALU.mult))
            pick(m1, pick1)
            chain(v.scalar_tensor_tensor(prob[:, :, :], pick1[:, :, :], -4.0, prob[:, :, :], ALU.mult, ALU.add))
            pick(m2, pick2)
            v.tensor_tensor(both[:, :, :], pick1[:, :, :], pick2[:, :, :], ALU.add).then_inc(picked, 1)
            chain(v.tensor_tensor(ms[:, :], m1[:, :], m2[:, :], ALU.add))
            chain(v.reciprocal(ms[:, :], ms[:, :]))
            chain(v.tensor_tensor(m1[:, :], m1[:, :], ms[:, :], ALU.mult))
            chain(v.tensor_tensor(m2[:, :], m2[:, :], ms[:, :], ALU.mult))
            chain(v.memset(cum[:, 0, :], 0.0))
            dve.wait_ge(ranked, 1)
            for t in range(NT):
                chain(v.tensor_tensor(cum[:, t + 1, :], b_gu[0][:, E * t:E * (t + 1)], cum[:, t, :], ALU.add))
            rounded(need[:, :], cum[:, NT, :], 1.0 / ROWS, (ROWS - 1) / 2 / ROWS)
            spread = eq[:, 0:E, :]
            chain(v.tensor_tensor(spread, after[:, :, :], over_t(need[:, :], E), ALU.mult))
            chain(v.tensor_reduce(last_tile[:, :], spread, AX.X, ALU.add))
            chain(v.tensor_tensor(first_slot[:, :], last_tile[:, :], need[:, :], ALU.subtract))
            chain(v.tensor_scalar(first_slot[:, :], first_slot[:, :], float(ROWS), None, ALU.mult))
            tiles = column[:, 0:LISTED].rearrange("p (j o) -> p j o", o=1).broadcast_to([P, LISTED, E])
            chain(v.tensor_tensor(passed[:, :, :], tiles, over_t(last_tile[:, :], LISTED), ALU.is_ge))
            chain(v.tensor_reduce(found[:, :], passed[:, :, :], AX.X, ALU.add))
            chain(v.tensor_scalar(found[:, :], found[:, :], float(P), part, ALU.mult, ALU.add))
            chain(v.tensor_copy(expert_of[:, :], found[:, :]))
            chain(v.tensor_tensor(slots[:, :, :], b_gu[1][:, 0:NT * E].rearrange("p (t e) -> p t e", e=E), cum[:, 0:NT, :], ALU.add))
            chain(v.tensor_tensor(slots[:, :, :], slots[:, :, :], over_t(first_slot[:, :]), ALU.add))
            for c, chosen in enumerate((pick1, pick2)):
                chain(v.tensor_tensor(eq[:, :, :], chosen[:, :, :], slots[:, :, :], ALU.mult))
                chain(v.tensor_reduce(slot[:, c, :], eq[:, :, :], AX.X, ALU.add))
            rounded(half[:, :, :], slot[:, :, :], 1.0 / P, -(P - 1) / 2 / P)
            chain(v.scalar_tensor_tensor(row_of[:, :, :], half[:, :, :], -float(P), slot[:, :, :], ALU.mult, ALU.add))
            for c in range(2):
                def wide(a, n):
                    return a.rearrange("p (t o) -> p t o", o=1).broadcast_to([P, NT, n])

                def columns(n):
                    return column[:, 0:n].rearrange("p (o j) -> p o j", o=1).broadcast_to([P, NT, n])

                by_row, by_half = one_hots(c)
                chain(v.tensor_tensor(by_row, columns(P), wide(row_of[:, c, :], P), ALU.is_equal))
                chain(v.tensor_tensor(by_half, columns(SLOTS), wide(half[:, c, :], SLOTS), ALU.is_equal))
                v.tensor_tensor(by_half, by_half.bitcast(F32), wide(name_of[:, NT * c:NT * (c + 1)], SLOTS), ALU.mult).then_inc(sorted_, 1)
            dve.wait_ge(tabled, 1)
            chain(v.tensor_scalar(empty[:, :], b_y[1][:, 0:SLOTS], 0.0, NOWHERE, ALU.is_equal, ALU.mult))
            chain(v.scalar_tensor_tensor(table[:, :], b_y[1][:, 0:SLOTS], -1.0, empty[:, :], ALU.add, ALU.add))
            chain(v.tensor_copy(dest_of[:, :], table[:, :]))
            rounded(table[:, :], table[:, :], 0.5, -0.25)
            v.tensor_copy(token_of[:, :], table[:, :]).then_inc(listed, 1)
            dve.wait_ge(listed, 1)

            def set_gather(it, b):
                wait(dve, dn_in[b], it, 16, 0)
                wait(dve, gu_in[b], it, 16, 0)
                wait(dve, rows_in[b], it, 32, 0)
                reg, add = it
                half_at = slice(HALVES * (2 * add + b), HALVES * (2 * add + b + 1)) if reg is None else bass.ds(reg * STEPS + (STEPS * add + HALVES * b), HALVES)
                tile_at = slice(2 * add + b, 2 * add + b + 1) if reg is None else bass.ds(reg * 2 + (2 * add + b), 1)
                v.tensor_copy(gather_at[b][:, 0:HALVES], token_of[:, half_at])
                v.tensor_copy(gather_at[b][:, HALVES:HALVES + 1], expert_of[:, tile_at]).then_inc(gather_set, 1)

            def set_scatter(it, s):
                wait(dve, y_out[s], it, 16, 0)
                reg, add = it
                at = slice(STEPS * add + s, STEPS * add + s + 1) if reg is None else bass.ds(reg * STEPS + (STEPS * add + s), 1)
                v.tensor_copy(scatter_at[s][:, :], dest_of[:, at]).then_inc(scatter_set, 1)

            def lo_x(it, s):
                wait(dve, x_hi, it, STEPS, s + 1)
                v.tensor_tensor(xT[s % 2][1], b_x[s % 2][:, :].rearrange("p (k t) -> p k t", k=KD),
                                xT[s % 2][0].bitcast(F32), ALU.subtract).then_inc(x_split, 1)

            def lo_gate_up(it, b, c):
                cols = slice(GU // 2 * c, GU // 2 * (c + 1))
                wait(dve, wg_hi, it, 4, 2 * b + c + 1)
                v.tensor_tensor(w_gu[b][1][:, cols], raw_gu[b][:, cols], w_gu[b][0][:, cols].bitcast(F32), ALU.subtract).then_inc(wg_split, 1)

            def lo_down(it, b):
                wait(dve, wd_hi, it, 2, b + 1)
                v.tensor_tensor(w_dn[b][1][:, :], raw_dn[b][:, :], w_dn[b][0][:, :].bitcast(F32), ALU.subtract).then_inc(wd_split, 1)

            def fuse_up(it, s):
                wait(dve, silu_done, it, STEPS, s + 1)
                wait(dve, f_turned, it, STEPS, s - 1)
                v.tensor_tensor(fuse[s % 2][:, :], b_gu[s % 2][:, I:2 * I], silu[s % 2][:, :], ALU.mult).then_inc(fused, 1)

            def lo_f(it, s):
                wait(dve, f_hi, it, STEPS, s + 1)
                v.tensor_tensor(fT[s % 2][1], b_f[:, 0:I].rearrange("p (k t) -> p k t", k=KI),
                                fT[s % 2][0].bitcast(F32), ALU.subtract).then_inc(f_split, 1)

            for b in range(2):
                set_gather(FIRST, b)
            for c in range(2):
                lo_gate_up(FIRST, 0, c)
            lo_x(FIRST, 0)

            def body(it):
                for s in range(STEPS):
                    b = s // HALVES
                    lo_x(*step(it, s + 1))
                    nxt = step(it, HALVES * (b + 1))
                    lo_gate_up(nxt[0], 1 - b, s % HALVES)
                    if s % HALVES == 0:
                        lo_down(it, b)
                        set_gather((it[0], it[1] + 1), b)
                    set_scatter(it, s)
                    fuse_up(it, s)
                    if exists(it, s - 1):
                        lo_f(*step(it, s - 1))

            iterations(dve, body)
            lo_f(*step((None, ITER), -1))

            for t in range(NT):
                n = t // 2
                if t % 2 == 0:
                    dve.wait_ge(pairs_in[n % 2], 16 * (n // 2 + 1))
                for c, weight in enumerate((m1, m2)):
                    y = raw_gu[n % 2][:, D * (2 * (t % 2) + c):D * (2 * (t % 2) + c + 1)]
                    row = k.x_sb[:, t, :]
                    ins = v.scalar_tensor_tensor(row, y, weight[:, t:t + 1], row, ALU.mult, ALU.add)
                    ins.then_inc(*((route_chain, 1) if c == 0 else (summed, 1)))
                    if c == 0:
                        done[0] += 1
                        dve.wait_ge(route_chain, done[0])


def decoder_layers(nc, x, ctx_1024, mask, w0, f0, w1, m1, out):
    with ExitStack() as st:
        k = Parts()
        k.nc = nc
        k.sem = lambda n: st.enter_context(nc.semaphore(n))
        k.banks = [st.enter_context(nc.psum_tensor(f"bank{i}", [P, 512], F32)) for i in range(8)]
        k.x_sb = st.enter_context(nc.sbuf_tensor("x_sb", [P, NT, D], F32))
        k.xnT_hi = st.enter_context(nc.sbuf_tensor("xnT_hi", [P, KD, T], F32R))
        k.xnT_lo = st.enter_context(nc.sbuf_tensor("xnT_lo", [P, KD, T], F32R))
        k.ident = st.enter_context(nc.sbuf_tensor("ident", [P, P], F32))
        k.ctx_split = nc.dram_tensor("ctx_split", (NG, P, 2 * KC * GT), F32, kind="Internal").ap()
        k.ln_calls = 0
        k.ident_made, k.wait_over = k.sem("ident_made"), k.sem("wait_over")
        k.ln_sems = [k.sem(f"ln_{n}") for n in ("chain", "normed", "turned", "hi_done", "lo_done")]
        load_stage(k, x, ctx_1024)
        layernorm_stage(k)
        attention_stage(k, "l0", *w0, mask=mask)
        layernorm_stage(k)
        ffn_stage(k, *f0)
        layernorm_stage(k)
        attention_stage(k, "l1", *w1[:4], gq=w1[4], gk=w1[5])
        xn_rows = nc.dram_tensor("xn_rows", (T, D), F32, kind="Internal").ap()
        layernorm_stage(k, xn_rows)
        moe_stage(k, xn_rows, *m1, out)


_INS = ["x", "ctx_1024", "mask_BxS2_bf1", "L0_xattn_Wq", "L0_xattn_Wk", "L0_xattn_Wv", "L0_xattn_Wo", "L0_ffn_gate_w",
        "L0_ffn_up_w", "L0_ffn_down_w", "L0_ffn_gate_scale", "L0_ffn_up_scale", "L0_ffn_down_scale", "L1_xattn_Wq",
        "L1_xattn_Wk", "L1_xattn_Wv", "L1_xattn_Wo", "L1_xattn_gq", "L1_xattn_gk", "L1_ffn_gate_w", "L1_ffn_gate_up_proj",
        "L1_ffn_down_proj"]


def kernel(**inputs):
    import concourse.bacc as bacc
    import numpy as np
    from concourse.bass_utils import run_bass_kernel_spmd as run

    nc = bacc.Bacc("TRN2", target_bir_lowering=False, num_devices=1)
    arrays, aps = {}, []
    for name in _INS:
        a = np.ascontiguousarray(inputs[name])
        if a.dtype == np.bool_:
            a = a.view(np.uint8)
        arrays[f"in_{name}"] = a
        aps.append(nc.dram_tensor(f"in_{name}", a.shape, mybir.dt.from_np(a.dtype), kind="ExternalInput").ap())
    out = nc.dram_tensor("out_x", (B, S, D), F32, kind="ExternalOutput").ap()
    decoder_layers(nc, aps[0], aps[1], aps[2], aps[3:7], aps[7:13], aps[13:19], aps[19:22], out)
    return run(nc, [arrays], core_ids=[0]).results[0]["out_x"]
```

```python
from contextlib import ExitStack

import concourse.bass as bass
from concourse import mybir

ALU = mybir.AluOpType
ACT = mybir.ActivationFunctionType
AX = mybir.AxisListType
F32 = mybir.dt.float32
F32R = mybir.dt.float32r
BF16 = mybir.dt.bfloat16
I32 = mybir.dt.int32
U32 = mybir.dt.uint32
U8 = mybir.dt.uint8

P = 128
B, S, D = 8, 256, 512
C = 256
T = B * S
NT = T // P
KD, KC = D // P, C // P
GT = 512
NG = T // GT
TG = GT // P
NH, HD = 16, 128
HB = 2
NHG = NH // HB
UN = HB * 2
F = 1536
NF = F // P
E, I = 16, 256
EPS = 1e-5
SM_SCALE = float(HD) ** -0.5
MASKED = -1e30
MAX_FLOOR = -1e29
RSQRT_SEED = float(0x5F3759DF)


def rsqrt_steps(eng, y, tmp, v, step, apart=lambda: None):
    apart()
    step(eng.tensor_scalar(y.bitcast(I32), v.bitcast(I32), -0.5, RSQRT_SEED, ALU.mult, ALU.add))
    for _ in range(3):
        step(eng.tensor_tensor(tmp, y, y, ALU.mult))
        step(eng.tensor_tensor(tmp, tmp, v, ALU.mult))
        apart()
        step(eng.tensor_scalar(tmp, tmp, -0.5, 1.5, ALU.mult, ALU.add))
        step(eng.tensor_tensor(y, y, tmp, ALU.mult))


RSQRT_STEPS = 13


def apart(k, eng):
    eng.sem_inc(k.wait_over, 1)


class Parts:
    pass


def load_stage(k, x, ctx_in):
    nc, banks = k.nc, k.banks
    with ExitStack() as st:
        c_sb = st.enter_context(nc.sbuf_tensor("c_sb", [P, NT, C], F32))
        ct = k.ct
        zero = st.enter_context(nc.sbuf_tensor("zero", [P, P], F32))
        block = st.enter_context(nc.Block())
        ident_made = k.ident_made
        c_loaded, c_turned, c_hi, c_lo = (k.sem(n) for n in ("c_loaded", "c_turned", "c_hi", "c_lo"))

        @block.sync
        def _(sp):
            sp.dma_start(c_sb[:, :, :], ctx_in.rearrange("b (t p) d -> p (b t) d", p=P)).then_inc(c_loaded, 16)
            xv = x.rearrange("b (t p) d -> p (b t) d", p=P)
            for g in range(NG):
                sp.dma_start(k.x_sb[:, TG * g:TG * (g + 1), :], xv[:, TG * g:TG * (g + 1), :]).then_inc(k.x_in[g // (NG // 2)], 16)
            for g in range(NG):
                sp.wait_ge(c_lo, KC * (g + 1))
                sp.dma_start(k.ctx_split[g], ct[g][:, :, :, :].rearrange("p a k t -> p (a k t)").bitcast(F32)).then_inc(k.ctx_stored, 16)

        @block.gpsimd
        def _(pool):
            nc.gpsimd.memset(zero[:, :], 0.0).then_inc(ident_made, 1)
            pool.wait_ge(ident_made, 1)
            nc.gpsimd.affine_select(out=k.ident[:, :], in_=zero[:, :], compare_op=ALU.not_equal, fill=1.0, base=0,
                                    pattern=[[-1, P]], channel_multiplier=1).then_inc(ident_made, 1)

        @block.tensor
        def _(pe):
            pe.wait_ge(ident_made, 2)
            pe.wait_ge(c_loaded, 16)
            for g in range(NG):
                for c in range(KC):
                    if g >= 2:
                        pe.wait_ge(c_lo, KC * (g - 2) + c + 1)
                    for j in range(TG):
                        mm = nc.tensor.transpose(banks[KC * (g % 2) + c][:, P * j:P * (j + 1)],
                                                 c_sb[:, TG * g + j, P * c:P * (c + 1)], k.ident[:, :])
                    mm.then_inc(c_turned, 1)

        @block.scalar
        def _(act):
            for g in range(NG):
                for c in range(KC):
                    act.wait_ge(c_turned, KC * g + c + 1)
                    nc.scalar.copy(ct[g][:, 0, c, :], banks[KC * (g % 2) + c][:, :]).then_inc(c_hi, 1)

        @block.vector
        def _(dve):
            for g in range(NG):
                for c in range(KC):
                    dve.wait_ge(c_hi, KC * g + c + 1)
                    nc.vector.tensor_tensor(ct[g][:, 1, c, :], banks[KC * (g % 2) + c][:, :],
                                            ct[g][:, 0, c, :].bitcast(F32), ALU.subtract).then_inc(c_lo, 1)


def layernorm_stage(k, ahead, rows=None, stats_made=False):
    nc, banks = k.nc, k.banks
    turn = k.ln_calls
    k.ln_calls += 1
    with ExitStack() as st:
        xn = [st.enter_context(nc.sbuf_tensor(f"xn{turn}_{j}", [P, D], F32)) for j in range(2 * TG)]
        mv = st.enter_context(nc.sbuf_tensor(f"ln_mv{turn}", [P, NT, 2], F32))
        var, rstd, tmp, shift = (st.enter_context(nc.sbuf_tensor(f"ln_{n}{turn}", [P, NT], F32)) for n in ("var", "rstd", "tmp", "shift"))
        block = st.enter_context(nc.Block())
        chain, normed, act_normed, turned, hi_done, lo_done = k.ln_sems
        HALF = TG // 2

        def wait_normed(eng, t):
            j, before = t % TG, (turn * NG + t // TG) * HALF
            eng.wait_ge(normed if j < HALF else act_normed, before + j % HALF + 1)

        def normalise(eng, g, tiles, one):
            if rows is not None and g >= 2:
                eng.wait_ge(rows_out[g % 2], 16 * TG * (g // 2))
            for j in tiles:
                one(TG * g + j)

        if rows is not None:
            rows_out = [k.sem(f"ln_rows_out{i}") for i in range(2)]
            rows_v = rows.rearrange("(t p) d -> p t d", p=P)

        @block.sync
        def _(sp):
            ahead.sync(sp)
            if rows is not None:
                for t in range(NT):
                    wait_normed(sp, t)
                    sp.dma_start(rows_v[:, t, :], xn[t % (2 * TG)][:, :]).then_inc(rows_out[t // TG % 2], 16)
                for r in rows_out:
                    sp.wait_ge(r, 16 * NT // 2)

        chain_end = k.ln_chain + (0 if stats_made else NT) + NT + 1 + RSQRT_STEPS + 1

        @block.gpsimd
        def _(pool):
            ahead.gpsimd(pool)

        @block.vector
        def _(dve):
            def step(ins, wait=True):
                ins.then_inc(chain, 1)
                k.ln_chain += 1
                if wait:
                    dve.wait_ge(chain, k.ln_chain)

            if not stats_made:
                for t in range(NT):
                    if turn == 0 and t % (NT // 2) == 0:
                        dve.wait_ge(k.x_in[t // (NT // 2)], 16 * NG // 2)
                    step(nc.vector.bn_stats(k.stats[:, t, :], k.x_sb[:, t, :]), t == NT - 1)
            for t in range(NT):
                step(nc.vector.bn_aggr(mv[:, t, :], k.stats[:, t, :]), t == NT - 1)
            step(nc.vector.tensor_scalar(var[:, :], mv[:, :, 1], EPS, None, ALU.add))
            rsqrt_steps(nc.vector, rstd[:, :], tmp[:, :], var[:, :], step)

            step(nc.vector.scalar_tensor_tensor(shift[:, :], mv[:, :, 0], -1.0, rstd[:, :], ALU.mult, ALU.mult), False)

            def one(t):
                nc.vector.tensor_scalar(xn[t % (2 * TG)][:, :], k.x_sb[:, t, :], mv[:, t, 0:1], rstd[:, t:t + 1],
                                        ALU.subtract, ALU.mult).then_inc(normed, 1)

            normalise(dve, 0, range(HALF), one)
            for g in range(NG):
                if g + 1 < NG:
                    normalise(dve, g + 1, range(HALF), one)
                for t in range(TG * g, TG * (g + 1)):
                    at = slice(P * t, P * (t + 1))
                    dve.wait_ge(hi_done, turn * NT + t + 1)
                    nc.vector.tensor_tensor(k.xnT_lo[:, :, at], banks[t % (2 * TG)][:, :].rearrange("p (k t) -> p k t", k=KD),
                                            k.xnT_hi[:, :, at].bitcast(F32), ALU.subtract).then_inc(lo_done, 1)

        @block.tensor
        def _(pe):
            for t in range(NT):
                wait_normed(pe, t)
                if t >= 2 * TG:
                    pe.wait_ge(lo_done, turn * NT + t - 2 * TG + 1)
                for c in range(KD):
                    mm = nc.tensor.transpose(banks[t % (2 * TG)][:, P * c:P * (c + 1)], xn[t % (2 * TG)][:, P * c:P * (c + 1)], k.ident[:, :])
                mm.then_inc(turned, 1)

        @block.scalar
        def _(act):
            def one(t):
                nc.scalar.activation(xn[t % (2 * TG)][:, :], k.x_sb[:, t, :], ACT.Identity, bias=shift[:, t:t + 1],
                                     scale=rstd[:, t:t + 1]).then_inc(act_normed, 1)

            if turn > 0:
                ahead.scalar(act)
            act.wait_ge(chain, chain_end)
            normalise(act, 0, range(HALF, TG), one)
            for t in range(NT):
                if t % TG == 0 and t + TG < NT:
                    normalise(act, t // TG + 1, range(HALF, TG), one)
                if turn == 0 and t == 2 * TG:
                    ahead.scalar(act)
                act.wait_ge(turned, turn * NT + t + 1)
                nc.scalar.copy(k.xnT_hi[:, :, P * t:P * (t + 1)], banks[t % (2 * TG)][:, :].rearrange("p (k t) -> p k t", k=KD)).then_inc(hi_done, 1)


def attention_start(k, st, name, Wq, Wk, Wv, rms):
    nc = k.nc
    a = Parts()
    a.nkv = HB if rms else 1
    a.kvw = nkv_w = a.nkv * HD

    def sb(n, shape, dt=F32):
        return st.enter_context(nc.sbuf_tensor(f"{name}_{n}", shape, dt))

    def pair(n, shape):
        return [sb(f"{n}_hi", shape, F32R), sb(f"{n}_lo", shape, F32R)]

    a.wq, a.wkv = pair("wq", [P, KD, HB * HD]), pair("wkv", [P, KC, 2 * nkv_w])
    a.raw_a = sb("raw_a", [P, KD * HB * HD])
    a.raw_b = sb("raw_b", [P, KC, 2 * nkv_w])
    a.ctxT = sb("ctxT", [P, 2, KC, GT], F32R)
    a.wq_of = [[w[:, :, HD * h:HD * (h + 1)] for w in a.wq] for h in range(HB)]
    a.raw_wq_of = [a.raw_a[:, :].rearrange("p (k n) -> p k n", k=KD)[:, :, HD * h:HD * (h + 1)] for h in range(HB)]
    a.wkv_flat = [w[:, :, :].rearrange("p k n -> p (k n)") for w in a.wkv]
    a.raw_b_flat = a.raw_b[:, :, :].rearrange("p k n -> p (k n)")
    a.wq_in, a.wkv_in, a.ctx_in, a.w_hi, a.wq_split, a.wkv_split = (
        k.sem(f"{name}_{n}") for n in ("wq_in", "wkv_in", "ctx_in", "w_hi", "wq_split", "wkv_split"))
    wq_v = Wq.rearrange("(k p) n -> p k n", p=P)
    wk_v = Wk.rearrange("(k p) n -> p k n", p=P)
    wv_v = Wv.rearrange("(k p) n -> p k n", p=P)

    def load_wq(sp, hg):
        sp.dma_start(a.raw_a[:, :].rearrange("p (k n) -> p k n", k=KD), wq_v[:, :, bass.ds(hg * (HB * HD), HB * HD)]).then_inc(a.wq_in, 16)

    def load_wkv(sp, hg):
        at = bass.ds(hg * nkv_w, nkv_w)
        sp.dma_start(a.raw_b[:, :, 0:nkv_w], wk_v[:, :, at]).then_inc(a.wkv_in, 16)
        sp.dma_start(a.raw_b[:, :, nkv_w:2 * nkv_w], wv_v[:, :, at]).then_inc(a.wkv_in, 16)

    def load_ctx(sp, m):
        sp.dma_start(a.ctxT[:, :, :, :].rearrange("p a k t -> p (a k t)").bitcast(F32), k.ctx_split[m % NG]).then_inc(a.ctx_in, 16)

    def weights_hi(act, w, raw, *waits):
        for w_sem, level in waits:
            act.wait_ge(w_sem, level)
        nc.scalar.copy(w[0], raw).then_inc(a.w_hi, 1)

    def weights_lo(pool, w, raw, level, done):
        pool.wait_ge(a.w_hi, level)
        nc.gpsimd.tensor_tensor(w[1], raw, w[0].bitcast(F32), ALU.subtract).then_inc(done, 1)

    def sync(sp):
        load_wkv(sp, 0)
        load_wq(sp, 0)
        sp.wait_ge(k.ctx_stored, 16 * NG)
        load_ctx(sp, 0)

    def scalar(act):
        weights_hi(act, a.wkv_flat, a.raw_b_flat, (a.wkv_in, 32))
        for h in range(HB):
            weights_hi(act, a.wq_of[h], a.raw_wq_of[h], (a.wq_in, 16))

    def gpsimd(pool):
        weights_lo(pool, a.wkv_flat, a.raw_b_flat, 1, a.wkv_split)
        for h in range(HB):
            weights_lo(pool, a.wq_of[h], a.raw_wq_of[h], h + 2, a.wq_split)

    a.load_wq, a.load_wkv, a.load_ctx, a.weights_hi, a.weights_lo = load_wq, load_wkv, load_ctx, weights_hi, weights_lo
    a.sync, a.scalar, a.gpsimd = sync, scalar, gpsimd
    return a


def attention_stage(k, name, start, Wo, mask=None, gq=None, gk=None):
    nc, banks = k.nc, k.banks
    rms = gq is not None
    nkv, kvw = start.nkv, start.kvw
    wq, wkv, raw_a, raw_b, ctxT = start.wq, start.wkv, start.raw_a, start.raw_b, start.ctxT
    wq_of, raw_wq_of, wkv_flat, raw_b_flat = start.wq_of, start.raw_wq_of, start.wkv_flat, start.raw_b_flat
    load_wq, load_wkv, load_ctx = start.load_wq, start.load_wkv, start.load_ctx
    wq_in, wkv_in, ctx_in, w_hi, wq_split, wkv_split = start.wq_in, start.wkv_in, start.ctx_in, start.w_hi, start.wq_split, start.wkv_split
    b_q, b_kv, b_s, b_pt, b_o = banks[0:2], banks[2:4], banks[4:6], banks[6], banks[7]
    wo_v = Wo.rearrange("(h p) n -> p h n", p=P)

    with ExitStack() as st:
        def sb(n, shape, dt=F32):
            return st.enter_context(nc.sbuf_tensor(f"{name}_{n}", shape, dt))

        def pair(n, shape):
            return [sb(f"{n}_hi", shape, F32R), sb(f"{n}_lo", shape, F32R)]

        def sem(n):
            return k.sem(f"{name}_{n}")

        wo = pair("wo", [P, HB, D])
        qT = [pair(f"qT{h}", [P, GT]) for h in range(HB)]
        kT = [pair(f"kT{h}", [P, GT]) for h in range(nkv)]
        v = [pair(f"v{i}", [P, TG, kvw]) for i in range(2)]
        kn = sb("kn", [P, TG, kvw])
        probs = [sb(f"probs{i}", [P, 2, S]) for i in range(2)]
        pT = pair("pT", [P, 2, S])
        oT = [[pair(f"oT{i}_{h}", [P, GT]) for h in range(HB)] for i in range(2)]
        mx, nbias, rsum, rden = (sb(n, [P, 2 * UN]) for n in ("mx", "nbias", "rsum", "rden"))
        if rms:
            q2, k2 = sb("q2", [P, GT]), sb("k2", [P, HD])
            nk, nq = TG * nkv, TG * HB
            sums, var, rr, tmp = (sb(n, [P, nk + nq]) for n in ("sums", "var", "rr", "tmp"))
            gain_in = sb("gain_in", [P, 2])
            gain = sb("gain", [P, 1])
            ones = sb("ones", [P, 1])
        else:
            den_chain = sem("den_chain")
            mask_u8 = sb("mask_u8", [P, T], U8)
            mask_bias = sb("mask_bias", [P, T], BF16)
            scored = [sb(f"scored{i}", [P, 2, S]) for i in range(2)]
        block = st.enter_context(nc.Block())

        wo_in, const_in = sem("wo_in"), sem("const_in")
        wo_split, zeroed = sem("wo_split"), sem("zeroed")
        q_made, kv_made, k_turned, s_made, p_turned, pv_made, y_made, qsum_made = (
            sem(n) for n in ("q_made", "kv_made", "k_turned", "s_made", "p_turned", "pv_made", "y_made", "qsum_made"))
        q_hi, q_sq, kv_hi, kT_hi, exp_done, pT_hi, o_hi = (sem(n) for n in ("q_hi", "q_sq", "kv_hi", "kT_hi", "exp_done", "pT_hi", "o_hi"))
        q_split, kv_split, kT_split, pT_split, o_split, bias_done, rden_done, y_added, p_normed, dve_chain = (
            sem(n) for n in ("q_split", "kv_split", "kT_split", "pT_split", "o_split", "bias_done", "rden_done", "y_added",
                             "p_normed", "dve_chain"))
        if rms:
            k_sq, k_chain, q_chain, k_ready, qsum_out, q_ready = (
                sem(n) for n in ("k_sq", "k_chain", "q_chain", "k_ready", "qsum_out", "q_ready"))

        def count(per_body, extra, hg, g):
            return hg * (NG * per_body) + (g * per_body + extra)

        def over(hg, g):
            return isinstance(hg, int) and hg * NG + g >= NHG * NG

        def iterations(eng, iteration):
            with eng.Fori(0, NHG - 1) as hg:
                iteration(hg)
            iteration(NHG - 1)

        stats_chain = k.ln_sems[0]
        PROLOGUE = (0, -1)

        @block.sync
        def _(sp):
            if rms:
                sp.dma_start(gain_in[:, 0:1], gq.rearrange("(p a) -> p a", a=1)).then_inc(const_in, 16)
                sp.dma_start(gain_in[:, 1:2], gk.rearrange("(p a) -> p a", a=1)).then_inc(const_in, 16)
            else:
                sp.dma_start(mask_u8[:, :], mask.rearrange("(a b) s -> a (b s)", a=1).broadcast_to([P, T])).then_inc(const_in, 16)
            sp.wait_ge(kv_made, TG)
            load_ctx(sp, 1)

            def iteration(hg):
                sp.wait_ge(wq_split, hg * HB + HB)
                sp.dma_start(raw_a[:, :].rearrange("p (h n) -> p h n", h=HB), wo_v[:, bass.ds(hg * HB, HB), :]).then_inc(wo_in, 16)
                if not over(hg + 1, 0):
                    sp.wait_ge(wkv_split, hg + 1)
                    load_wkv(sp, hg + 1)
                for g in range(NG):
                    if not over(hg, g + 2):
                        sp.wait_ge(kv_made, count(TG, 2 * TG, hg, g))
                        load_ctx(sp, g + 2)
                    if g == 1 and not over(hg + 1, 0):
                        sp.wait_ge(wo_split, hg + 2)
                        load_wq(sp, hg + 1)

            iterations(sp, iteration)

        wo_flat = [w[:, :, :].rearrange("p h n -> p (h n)") for w in wo]

        @block.gpsimd
        def _(pool):
            gp = nc.gpsimd

            def weights_lo(w, raw, level, done):
                start.weights_lo(pool, w, raw, level, done)

            norm_steps = 1 + RSQRT_STEPS

            def factors(cols, chain, hg, g):
                done = [0]

                def step(ins):
                    ins.then_inc(chain, 1)
                    done[0] += 1
                    pool.wait_ge(chain, count(norm_steps, norm_steps + done[0], hg, g))

                apart(k, pool)
                step(gp.tensor_scalar(var[:, cols], sums[:, cols], 1.0 / HD, EPS, ALU.mult, ALU.add))
                rsqrt_steps(gp, rr[:, cols], tmp[:, cols], var[:, cols], step, lambda: apart(k, pool))

            def norm_keys(hg, g, first=False):
                if over(hg, g + 1):
                    return
                pool.wait_ge(kv_hi, count(TG, 2 * TG, hg, g))
                pool.wait_ge(qsum_out, count(HB, HB + 1, hg, g))
                if not first:
                    pool.wait_ge(exp_done, count(UN, 2, hg, g))
                factors(slice(0, nk + TG), k_chain, hg, g)
                pool.sem_inc(q_ready, 1)
                kn3 = kn[:, :, :].rearrange("p t (h d) -> p (t h) d", d=HD)
                scale = rr[:, 0:nk].rearrange("p (a b) -> p a b", b=1).broadcast_to([P, nk, HD])
                gp.tensor_tensor(kn3, kn3, scale, ALU.mult).then_inc(k_ready, 1)

            def norm_queries(hg, g):
                pool.wait_ge(qsum_out, count(HB, 2, hg, g))
                pool.wait_ge(exp_done, count(UN, 1, hg, g))
                factors(slice(nk + TG, nk + nq), q_chain, hg, g - 1)
                pool.sem_inc(q_ready, 1)

            if rms:
                gp.memset(ones[:, :], 1.0).then_inc(const_in, 1)
            zeros = [*wo_flat, *(oT[1][0][p][:, :] for p in range(2)), *(w[:, :, :].rearrange("p t d -> p (t d)") for w in v[1]),
                     *(w[:, :, :].rearrange("p s q -> p (s q)") for w in pT)]
            for w in zeros:
                gp.memset(w.bitcast(F32), 0.0).then_inc(zeroed, 1)
            pool.wait_ge(zeroed, len(zeros))
            pool.sem_inc(wo_split, 1)
            if rms:
                norm_keys(*PROLOGUE, first=True)

            def iteration(hg):
                for g in range(NG):
                    if rms:
                        norm_queries(hg, g)
                    if g == 3 and not over(hg + 1, 0):
                        weights_lo(wq_of[1], raw_wq_of[1], hg * 4 + 7, wq_split)
                    if rms:
                        norm_keys(hg, g)
                    if g == 0:
                        weights_lo(wo_flat, raw_a[:, :], hg * 4 + 4, wo_split)
                    if g == 2 and not over(hg + 1, 0):
                        weights_lo(wq_of[0], raw_wq_of[0], hg * 4 + 5, wq_split)
                        weights_lo(wkv_flat, raw_b_flat, hg * 4 + 6, wkv_split)

            iterations(pool, iteration)

        @block.tensor
        def _(pe):
            def products(out, terms):
                n = 3 * len(terms)
                i = 0
                for a, b in terms:
                    for x, y in ((0, 0), (0, 1), (1, 0)):
                        mm = nc.tensor.matmul(out, a[x], b[y], start=(i == 0), stop=(i == n - 1))
                        i += 1
                return mm

            def project_q(hg, g, h):
                if over(hg, g + 1):
                    return
                ng = (g + 1) % NG
                pe.wait_ge(wq_split, hg * HB + (h + 1 + (HB if g == NG - 1 else 0)))
                if g >= 0:
                    pe.wait_ge(y_added, count(TG, 1, hg, g) if h == 0 else count(TG, TG + 1, hg, g))
                at = slice(GT * ng, GT * (ng + 1))
                products(b_q[h][:, :], [([w[:, c, HD * h:HD * (h + 1)] for w in wq], [k.xnT_hi[:, c, at], k.xnT_lo[:, c, at]])
                                        for c in range(KD)]).then_inc(q_made, 1)

            def project_kv(hg, g, t):
                if over(hg, g + 1):
                    return
                if t == 0:
                    pe.wait_ge(wkv_split, hg + (2 if g == NG - 1 else 1))
                    pe.wait_ge(ctx_in, count(16, 32, hg, g))
                if t >= 2:
                    pe.wait_ge(kv_split, count(TG, TG + t - 1, hg, g))
                products(b_kv[t % 2][:, 0:2 * kvw], [([ctxT[:, a, c, P * t:P * (t + 1)] for a in range(2)], [w[:, c, :] for w in wkv])
                                                     for c in range(KC)]).then_inc(kv_made, 1)

            def sum_q(hg, g, h):
                if over(hg, g):
                    return
                pe.wait_ge(q_sq, count(HB, h + 1, hg, g))
                pe.wait_ge(q_split, count(HB, h + 1, hg, g))
                for t in range(TG):
                    mm = nc.tensor.matmul(b_q[h][:, t:t + 1], q2[:, P * t:P * (t + 1)], ones[:, :], start=True, stop=True)
                mm.then_inc(qsum_made, 1)

            def turn_k(hg, g):
                if over(hg, g + 1):
                    return
                if rms:
                    pe.wait_ge(k_ready, count(1, 2, hg, g))
                pe.wait_ge(kv_split, count(TG, 2 * TG, hg, g))
                for h in range(nkv):
                    for t in range(TG):
                        mm = nc.tensor.transpose(b_kv[h][:, P * t:P * (t + 1)], kn[:, t, HD * h:HD * (h + 1)], k.ident[:, :])
                    mm.then_inc(k_turned, 1)

            def scores(hg, g, u):
                if over(hg, g):
                    return
                h, b = u // 2, u % 2
                if b == 0:
                    pe.wait_ge(q_split, count(HB, h + 1, hg, g))
                    if rms:
                        pe.wait_ge(q_ready, count(HB, h + 1, hg, g))
                if u == 0:
                    pe.wait_ge(kT_split, count(nkv, nkv, hg, g))
                kk = kT[min(h, nkv - 1)]
                for t in range(2):
                    at = slice(S * b + P * t, S * b + P * (t + 1))
                    mm = products(b_s[u % 2][:, S * t:S * (t + 1)], [([w[:, at] for w in qT[h]], [w[:, S * b:S * (b + 1)] for w in kk])])
                mm.then_inc(s_made, 1)

            def turn_p(hg, g, u):
                pe.wait_ge(p_normed, count(UN, u + 1, hg, g))
                for t in range(2):
                    for s in range(2):
                        mm = nc.tensor.transpose(b_pt[:, S * s + P * t:S * s + P * (t + 1)], probs[u % 2][:, t, P * s:P * (s + 1)], k.ident[:, :])
                mm.then_inc(p_turned, 1)

            def weigh_v(hg, g, u, first=False):
                h, b = u // 2, u % 2
                if not first:
                    if b == 0:
                        pe.wait_ge(o_split, count(HB, h + 1, hg, g))
                    pe.wait_ge(pT_split, count(UN, u + 2, hg, g))
                vh = min(h, nkv - 1)
                products(b_o[:, S * b:S * (b + 1)], [([w[:, 2 * b + s, HD * vh:HD * (vh + 1)] for w in v[g % 2]], [w[:, s, :] for w in pT])
                                                     for s in range(2)]).then_inc(pv_made, 1)

            def project_out(hg, g, t, last=False):
                if t == 0:
                    pe.wait_ge(wo_split, hg + (1 if g == 0 else 2))
                if last and t == 0:
                    pe.wait_ge(y_added, count(TG, 1, hg, g))
                elif t == 0:
                    pe.wait_ge(qsum_out if rms else q_split, count(HB, HB if over(hg, g + 1) else HB + 1, hg, g))
                    if over(hg, g + 1):
                        pe.wait_ge(y_added, count(TG, 1, hg, g))
                if t >= 2:
                    pe.wait_ge(y_added, count(TG, t, hg, g))
                o = oT[(g + 1) % 2]
                products(b_q[t % 2][:, :], [([w[:, P * t:P * (t + 1)] for w in o[h]], [w[:, h, :] for w in wo])
                                            for h in range(HB)]).then_inc(y_made, 1)

            for t in range(TG):
                project_kv(*PROLOGUE, t)
            project_q(*PROLOGUE, 0)
            if not rms:
                project_q(*PROLOGUE, 1)
            else:
                pe.wait_ge(const_in, 33)
                sum_q(0, 0, 0)
                project_q(*PROLOGUE, 1)
            turn_k(*PROLOGUE)
            pe.wait_ge(zeroed, 8)
            weigh_v(0, -1, 2, first=True)
            scores(0, 0, 0)

            def iteration(hg):
                for g in range(NG):
                    scores(hg, g, 1)
                    weigh_v(hg, g - 1, 3)
                    if rms:
                        project_q(hg, g, 0)
                        sum_q(hg, g, 1)
                        turn_p(hg, g, 0)
                    project_kv(hg, g, 0)
                    project_kv(hg, g, 1)
                    if not rms:
                        turn_p(hg, g, 0)
                        project_q(hg, g, 0)

                    if rms:
                        sum_q(hg, g + 1, 0)
                    else:
                        scores(hg, g, 2)
                    if rms:
                        weigh_v(hg, g, 0)
                    project_kv(hg, g, 2)
                    project_kv(hg, g, 3)
                    if not rms:
                        weigh_v(hg, g, 0)
                    turn_p(hg, g, 1)
                    if rms:
                        scores(hg, g, 2)
                    project_out(hg, g, 0)
                    project_out(hg, g, 1)

                    scores(hg, g, 3)
                    if not rms:
                        turn_k(hg, g)
                    weigh_v(hg, g, 1)
                    turn_p(hg, g, 2)
                    project_out(hg, g, 2)
                    project_out(hg, g, 3)

                    if not rms:
                        scores(hg, g + 1, 0)
                    weigh_v(hg, g, 2)
                    turn_p(hg, g, 3)
                    if rms:
                        turn_k(hg, g)
                    project_q(hg, g, 1)
                    if rms:
                        scores(hg, g + 1, 0)

            iterations(pe, iteration)
            weigh_v(NHG, -1, 3)
            pe.wait_ge(o_split, HB * NHG * NG + 1)
            for t in range(TG):
                project_out(NHG, 0, t, last=True)

        @block.scalar
        def _(act):
            def copy_q(hg, g, h):
                if over(hg, g + 1):
                    return
                act.wait_ge(q_made, count(HB, HB + h + 1, hg, g))
                nc.scalar.copy(qT[h][0][:, :], b_q[h][:, :]).then_inc(q_hi, 1)
                if rms:
                    if h >= 1 or g >= 0:
                        act.wait_ge(qsum_made, count(HB, HB + h, hg, g))
                    nc.scalar.activation(q2[:, :], b_q[h][:, :], ACT.Square).then_inc(q_sq, 1)

            def copy_kv(hg, g, t):
                if over(hg, g + 1):
                    return
                act.wait_ge(kv_made, count(TG, TG + t + 1, hg, g))
                nc.scalar.copy(kn[:, t, :], b_kv[t % 2][:, 0:kvw])
                if rms:
                    for h in range(nkv):
                        i = nkv * t + h
                        nc.scalar.activation(k2[:, :], b_kv[t % 2][:, HD * h:HD * (h + 1)], ACT.Square, accum_out=sums[:, i:i + 1]).then_inc(k_sq, 1)
                        act.wait_ge(k_sq, count(nk, nk + i + 1, hg, g))
                nc.scalar.copy(v[(g + 1) % 2][0][:, t, :], b_kv[t % 2][:, kvw:2 * kvw]).then_inc(kv_hi, 1)

            def copy_k(hg, g, h):
                if over(hg, g + 1):
                    return
                act.wait_ge(k_turned, count(nkv, nkv + h + 1, hg, g))
                if rms:
                    nc.scalar.activation(kT[h][0][:, :], b_kv[h][:, :], ACT.Identity, scale=gain[:, 0:1]).then_inc(kT_hi, 1)
                else:
                    nc.scalar.copy(kT[h][0][:, :], b_kv[h][:, :]).then_inc(kT_hi, 1)

            def exponentials(hg, g, u):
                if over(hg, g):
                    return
                act.wait_ge(bias_done, count(UN, u + 1, hg, g))
                for t in range(2):
                    i = 2 * u + t
                    src = b_s[u % 2][:, S * t:S * (t + 1)] if rms else scored[u % 2][:, t, :]
                    scale = rr[:, nk + i:nk + i + 1] if rms else SM_SCALE
                    ins = nc.scalar.activation(probs[u % 2][:, t, :], src, ACT.Exp, bias=nbias[:, i:i + 1], scale=scale,
                                               accum_out=rsum[:, i:i + 1])
                ins.then_inc(exp_done, 1)

            def copy_p(hg, g, u):
                act.wait_ge(p_turned, count(UN, u + 1, hg, g))
                nc.scalar.copy(pT[0][:, :, :].rearrange("p s q -> p (s q)"), b_pt[:, :]).then_inc(pT_hi, 1)

            def copy_o(hg, g, h):
                act.wait_ge(pv_made, count(UN, 2 * h + 4, hg, g))
                nc.scalar.copy(oT[g % 2][h][0][:, :], b_o[:, :]).then_inc(o_hi, 1)

            def weights_hi(w, raw, *waits):
                start.weights_hi(act, w, raw, *waits)

            for t in range(TG):
                copy_kv(*PROLOGUE, t)
            for h in range(HB):
                copy_q(*PROLOGUE, h)
            if rms:
                act.wait_ge(dve_chain, 1)
            for h in range(nkv):
                copy_k(*PROLOGUE, h)
            exponentials(0, 0, 0)

            def iteration(hg):
                def next_wq(g, h):
                    weights_hi(wq_of[h], raw_wq_of[h], (wq_in, hg * 16 + 32), (q_made, count(HB, HB + h + 1, hg, 2)))

                for g in range(NG):
                    copy_o(hg, g - 1, 1)
                    if rms:
                        copy_q(hg, g, 0)
                    exponentials(hg, g, 1)
                    if g == 3 and not over(hg + 1, 0):
                        next_wq(g, 1)
                    if rms:
                        copy_p(hg, g, 0)
                    copy_kv(hg, g, 0)
                    copy_kv(hg, g, 1)
                    if not rms:
                        copy_p(hg, g, 0)
                        copy_q(hg, g, 0)

                    copy_kv(hg, g, 2)
                    if not rms:
                        exponentials(hg, g, 2)
                    copy_kv(hg, g, 3)
                    copy_p(hg, g, 1)
                    if rms:
                        exponentials(hg, g, 2)
                    if g == 2 and not over(hg + 1, 0):
                        next_wq(g, 0)

                    if not rms:
                        copy_k(hg, g, 0)
                    if not rms:
                        exponentials(hg, g, 3)
                    copy_o(hg, g, 0)
                    copy_p(hg, g, 2)
                    if rms:
                        exponentials(hg, g, 3)
                    if g == 2 and not over(hg + 1, 0):
                        weights_hi(wkv_flat, raw_b_flat, (wkv_in, hg * 32 + 64), (kv_made, count(TG, 2 * TG, hg, g)))

                    if not rms:
                        exponentials(hg, g + 1, 0)
                    copy_p(hg, g, 3)
                    if rms:
                        for h in range(nkv):
                            copy_k(hg, g, h)
                    copy_q(hg, g, 1)
                    if rms:
                        exponentials(hg, g + 1, 0)
                    if g == 0:
                        weights_hi(wo_flat, raw_a[:, :], (wo_in, hg * 16 + 16), (y_made, count(TG, TG, hg, g)))

            iterations(act, iteration)
            copy_o(NHG, -1, 1)

        @block.vector
        def _(dve):
            def lo(pair, src, done):
                nc.vector.tensor_tensor(pair[1], src, pair[0].bitcast(F32), ALU.subtract).then_inc(done, 1)

            def split_q(hg, g, h):
                if over(hg, g + 1):
                    return
                dve.wait_ge(q_sq if rms else q_hi, count(HB, HB + h + 1, hg, g))
                lo([w[:, :] for w in qT[h]], b_q[h][:, :], q_split)

            def split_kv(hg, g, t):
                if over(hg, g + 1):
                    return
                dve.wait_ge(kv_hi, count(TG, TG + t + 1, hg, g))
                lo([w[:, t, :] for w in v[(g + 1) % 2]], b_kv[t % 2][:, kvw:2 * kvw], kv_split)

            def split_k(hg, g, h):
                if over(hg, g + 1):
                    return
                dve.wait_ge(kT_hi, count(nkv, nkv + h + 1, hg, g))
                if rms:
                    nc.vector.scalar_tensor_tensor(kT[h][1][:, :], b_kv[h][:, :], gain[:, 0:1], kT[h][0][:, :].bitcast(F32),
                                                   ALU.mult, ALU.subtract).then_inc(kT_split, 1)
                else:
                    lo([w[:, :] for w in kT[h]], b_kv[h][:, :], kT_split)

            def split_p(hg, g, u):
                dve.wait_ge(pT_hi, count(UN, u + 1, hg, g))
                lo([w[:, :, :].rearrange("p s q -> p (s q)") for w in pT], b_pt[:, :], pT_split)

            def split_o(hg, g, h):
                dve.wait_ge(o_hi, count(HB, h + 2, hg, g))
                lo([w[:, :] for w in oT[g % 2][h]], b_o[:, :], o_split)

            before_loop = 1

            def biases(hg, g, u):
                if over(hg, g):
                    return
                i = slice(2 * u, 2 * u + 2)
                dve.wait_ge(s_made, count(UN, u + 1, hg, g))
                if rms:
                    nc.vector.tensor_reduce(mx[:, i], b_s[u % 2][:, :].rearrange("p (t s) -> p t s", t=2), AX.X, ALU.max).then_inc(dve_chain, 1)
                    dve.wait_ge(dve_chain, count(UN, before_loop + u + 1, hg, g))
                    nc.vector.scalar_tensor_tensor(nbias[:, i], mx[:, i], -1.0, rr[:, nk + 2 * u:nk + 2 * u + 2],
                                                   ALU.mult, ALU.mult).then_inc(bias_done, 1)
                else:
                    at = S * (2 * (g % NG) + u % 2)
                    apart(k, dve)
                    for t in range(2):
                        ins = nc.vector.tensor_tensor_reduce(scored[u % 2][:, t, :], b_s[u % 2][:, S * t:S * (t + 1)], mask_bias[:, at:at + S],
                                                             1.0, MAX_FLOOR, ALU.add, ALU.max, mx[:, 2 * u + t:2 * u + t + 1])
                    ins.then_inc(dve_chain, 1)
                    dve.wait_ge(dve_chain, count(UN, before_loop + u + 1, hg, g))
                    nc.vector.tensor_scalar(nbias[:, i], mx[:, i], -SM_SCALE, None, ALU.mult).then_inc(bias_done, 1)

            def denominators(hg, g, u):
                if over(hg, g):
                    return
                i = slice(2 * u, 2 * u + 2)
                dve.wait_ge(exp_done, count(UN, u + 1, hg, g))
                if not rms:
                    nc.vector.tensor_scalar(rsum[:, i], rsum[:, i], 1e-30, None, ALU.max).then_inc(den_chain, 1)
                    dve.wait_ge(den_chain, count(UN, u + 1, hg, g))
                nc.vector.reciprocal(rden[:, i], rsum[:, i]).then_inc(rden_done, 1)
                dve.wait_ge(rden_done, count(UN, u + 1, hg, g))
                for t in range(2):
                    row = probs[u % 2][:, t, :]
                    ins = nc.vector.tensor_scalar(row, row, rden[:, 2 * u + t:2 * u + t + 1], None, ALU.mult)
                ins.then_inc(p_normed, 1)

            def take_sums(hg, g, h):
                if over(hg, g):
                    return
                i = nk + TG * h
                dve.wait_ge(qsum_made, count(HB, h + 1, hg, g))
                nc.vector.tensor_copy(sums[:, i:i + TG], b_q[h][:, 0:TG]).then_inc(qsum_out, 1)

            def add_y(hg, g, t):
                dve.wait_ge(y_made, count(TG, t + 1, hg, g))
                row = k.x_sb[:, TG * ((g - 1) % NG) + t, :]
                nc.vector.tensor_tensor(row, b_q[t % 2][:, :], row, ALU.add).then_inc(y_added, 1)

            dve.sem_inc(y_added, 1)
            dve.sem_inc(pT_split, 1)
            for t in range(TG):
                split_kv(*PROLOGUE, t)
            split_q(*PROLOGUE, 0)
            if rms:
                take_sums(0, 0, 0)
            split_q(*PROLOGUE, 1)
            if rms:
                dve.wait_ge(const_in, 33)
                nc.vector.scalar_tensor_tensor(gain[:, :], gain_in[:, 0:1], SM_SCALE, gain_in[:, 1:2], ALU.mult, ALU.mult).then_inc(dve_chain, 1)
            else:
                dve.wait_ge(const_in, 16)
                nc.vector.tensor_scalar(mask_bias[:, :], mask_u8[:, :], -MASKED, MASKED, ALU.mult, ALU.add).then_inc(dve_chain, 1)
                dve.wait_ge(dve_chain, 1)
            for h in range(nkv):
                split_k(*PROLOGUE, h)
            biases(0, 0, 0)
            if not rms:
                denominators(0, 0, 0)

            def iteration(hg):
                for g in range(NG):
                    if rms:
                        denominators(hg, g, 0)
                    biases(hg, g, 1)
                    split_o(hg, g - 1, 1)
                    if rms:
                        take_sums(hg, g, 1)
                        split_q(hg, g, 0)
                        denominators(hg, g, 1)
                        split_p(hg, g, 0)
                    split_kv(hg, g, 0)
                    split_kv(hg, g, 1)
                    if not rms:
                        denominators(hg, g, 1)
                        split_p(hg, g, 0)
                        split_q(hg, g, 0)

                    if rms:
                        take_sums(hg, g + 1, 0)
                    else:
                        biases(hg, g, 2)
                    split_kv(hg, g, 2)
                    split_kv(hg, g, 3)
                    if rms:
                        biases(hg, g, 2)
                        split_p(hg, g, 1)
                        add_y(hg, g, 0)
                    denominators(hg, g, 2)
                    if not rms:
                        split_p(hg, g, 1)
                        add_y(hg, g, 0)
                    add_y(hg, g, 1)

                    biases(hg, g, 3)
                    if not rms:
                        split_k(hg, g, 0)
                        denominators(hg, g, 3)
                    split_o(hg, g, 0)
                    split_p(hg, g, 2)
                    add_y(hg, g, 2)
                    if rms:
                        denominators(hg, g, 3)
                    add_y(hg, g, 3)

                    if not rms:
                        biases(hg, g + 1, 0)
                    split_p(hg, g, 3)
                    if rms:
                        for h in range(nkv):
                            split_k(hg, g, h)
                    else:
                        denominators(hg, g + 1, 0)
                    split_q(hg, g, 1)
                    if rms:
                        biases(hg, g + 1, 0)

            iterations(dve, iteration)
            split_o(NHG, -1, 1)

            def statistics(tiles):
                for t in tiles:
                    nc.vector.bn_stats(k.stats[:, t, :], k.x_sb[:, t, :]).then_inc(stats_chain, 1)

            done = NG - 1
            dve.wait_ge(y_added, count(TG, 1, NHG, 0))
            for t in range(TG):
                statistics(range(done * t, done * (t + 1)))
                add_y(NHG, 0, t)
            dve.wait_ge(y_added, count(TG, TG + 1, NHG, 0))
            statistics(range(done * TG, NT))
            k.ln_chain += NT
            dve.wait_ge(stats_chain, k.ln_chain)


def ffn_start(k, st, gate_w, up_w, down_w, gate_scale, up_scale, down_scale):
    nc = k.nc
    a = Parts()
    half = 3 * D // 2
    gate_v = gate_w.rearrange("(k p) f -> p k f", p=P)
    up_v = up_w.rearrange("(k p) f -> p k f", p=P)
    down_v = down_w.rearrange("(f p) n -> p f n", p=P)
    a.raw = [st.enter_context(nc.sbuf_tensor(f"ffn_raw{i}", [P, half], F32)) for i in range(2)]
    a.scale_rows = st.enter_context(nc.sbuf_tensor("ffn_scale_rows", [2 * NF, P], F32))
    a.dsc = st.enter_context(nc.sbuf_tensor("ffn_dsc", [P, D], F32))
    a.raw_in = [k.sem(f"ffn_raw_in{i}") for i in range(2)]
    a.scales_in = k.sem("ffn_scales_in")

    def load(sp, f):
        at = bass.ds(f * P, P)
        r0 = a.raw[0][:, :].rearrange("p (k f) -> p k f", f=P)
        sp.dma_start(r0[:, 0:KD, :], gate_v[:, :, at]).then_inc(a.raw_in[0], 16)
        sp.dma_start(r0[:, KD:half // P, :], up_v[:, 0:2, at]).then_inc(a.raw_in[0], 16)
        yield
        r1 = a.raw[1][:, 0:2 * P].rearrange("p (k f) -> p k f", f=P)
        sp.dma_start(r1, up_v[:, 2:4, at]).then_inc(a.raw_in[1], 16)
        sp.dma_start(a.raw[1][:, 2 * P:half], down_v[:, bass.ds(f, 1), :]).then_inc(a.raw_in[1], 16)
        yield

    def sync(sp):
        for _ in load(sp, 0):
            pass
        sp.dma_start(a.scale_rows[0:NF, :], gate_scale.rearrange("(f p) -> f p", p=P)).then_inc(a.scales_in, 16)
        sp.dma_start(a.scale_rows[NF:2 * NF, :], up_scale.rearrange("(f p) -> f p", p=P)).then_inc(a.scales_in, 16)
        sp.dma_start(a.dsc[:, :], down_scale.rearrange("(a n) -> a n", a=1).broadcast_to([P, D])).then_inc(a.scales_in, 16)

    a.load, a.sync, a.scalar, a.gpsimd = load, sync, lambda act: None, lambda pool: None
    return a


def ffn_stage(k, start):
    nc, banks = k.nc, k.banks
    half = 3 * D // 2
    raw, scale_rows, dsc, raw_in, scales_in = start.raw, start.scale_rows, start.dsc, start.raw_in, start.scales_in
    b_gate, b_up, b_y = banks[0:2], banks[2:4], banks[4:8]
    with ExitStack() as st:
        def sb(n, shape, dt=F32):
            return st.enter_context(nc.sbuf_tensor(f"ffn_{n}", shape, dt))

        def sem(n):
            return k.sem(f"ffn_{n}")

        w = sb("w", [P, NF, 3 * D], F32R)
        magic = [sb(f"magic{i}", [P, half]) for i in range(2)]
        raised = [sb(f"raised{i}", [P, half]) for i in range(2)]
        silu = [sb(f"silu{i}", [P, GT]) for i in range(2)]
        fuse = [sb(f"fuse{i}", [P, GT]) for i in range(2)]
        fz = [[sb(f"fz{i}_{p}", [P, GT], F32R) for p in ("hi", "lo")] for i in range(2)]
        scales = sb("scales", [P, 2 * NF])
        ysc = [r[:, 0:D] for r in raised]
        block = st.enter_context(nc.Block())
        scales_turned, scales_ready = sem("scales_turned"), sem("scales_ready")
        magic_chain, magic_made, w_ready = (sem(n) for n in ("magic_chain", "magic_made", "w_ready"))
        gate_made, up_made, silu_done, fuse_done, fz_hi, fz_split, y_made, y_chain, y_added = (
            sem(n) for n in ("gate_made", "up_made", "silu_done", "fuse_done", "fz_hi", "fz_split", "y_made", "y_chain", "y_added"))

        @block.sync
        def _(sp):
            with sp.Fori(0, NF - 1) as f:
                steps = start.load(sp, f + 1)
                for c in range(2):
                    sp.wait_ge(magic_made, f * 2 + (c + 1))
                    next(steps)

        def groups(eng, body):
            body(None, 0)
            with eng.Fori(0, NG - 1) as i:
                body(i, 1)

        def level(i, add, per, extra):
            return add * per + extra if i is None else i * per + (add * per + extra)

        @block.gpsimd
        def _(pool):
            def round_off(f):
                for c in range(2):
                    pool.wait_ge(magic_made, 2 * f + c + 1)
                    nc.gpsimd.tensor_tensor(w[:, f, half * c:half * (c + 1)], raised[c][:, :], magic[c][:, :], ALU.subtract).then_inc(w_ready, 1)

            def body(i, add):
                for f in range(NF):
                    if i is None and f + 1 < NF:
                        round_off(f + 1)
                    pool.wait_ge(fz_hi, level(i, add, NF, f + 1))
                    nc.gpsimd.tensor_tensor(fz[f % 2][1][:, :], fuse[f % 2][:, :], fz[f % 2][0][:, :].bitcast(F32),
                                            ALU.subtract).then_inc(fz_split, 1)

            round_off(0)
            groups(pool, body)

        stats_chain = k.ln_sems[0]

        @block.vector
        def _(dve):
            def round_up(f):
                for c in range(2):
                    dve.wait_ge(raw_in[c], 32 * (f + 1))
                    if f >= 1:
                        dve.wait_ge(w_ready, 2 * (f - 1) + c + 1)
                    nc.vector.tensor_scalar(magic[c][:, :].bitcast(U32), raw[c][:, :].bitcast(U32), 0x7F800000, None,
                                            ALU.bitwise_and).then_inc(magic_chain, 1)
                    dve.wait_ge(magic_chain, 4 * f + 2 * c + 1)
                    nc.vector.tensor_scalar(magic[c][:, :], magic[c][:, :], 2.0 ** -6, 1.5 * 2.0 ** 20, ALU.max, ALU.mult).then_inc(magic_chain, 1)
                    dve.wait_ge(magic_chain, 4 * f + 2 * c + 2)
                    nc.vector.tensor_tensor(raised[c][:, :], raw[c][:, :], magic[c][:, :], ALU.add).then_inc(magic_made, 1)

            def add_y(i, add):
                for t in range(TG):
                    dve.wait_ge(y_made, level(i, add, TG, t + 1))
                    nc.vector.tensor_tensor(ysc[t % 2], b_y[t][:, :], dsc[:, :], ALU.mult).then_inc(y_chain, 1)
                    dve.wait_ge(y_chain, level(i, add, TG, t + 1))
                    row = k.x_sb[:, TG * add + t, :] if i is None else k.x_sb[:, bass.ds(i * TG + (TG * add + t), 1), :]
                    nc.vector.tensor_tensor(row, ysc[t % 2], row, ALU.add).then_inc(y_added, 1)

            def statistics(i, add):
                dve.wait_ge(y_added, level(i, add, TG, TG))
                apart(k, dve)
                for t in range(TG):
                    n = slice(TG * add + t, TG * add + t + 1) if i is None else bass.ds(i * TG + (TG * add + t), 1)
                    nc.vector.bn_stats(k.stats[:, n, :], k.x_sb[:, n, :]).then_inc(stats_chain, 1)

            def body(i, add):
                for f in range(NF):
                    if i is None and f + 1 < NF:
                        round_up(f + 1)
                    dve.wait_ge(up_made, level(i, add, NF, f + 1))
                    dve.wait_ge(silu_done, level(i, add, NF, f + 1))
                    nc.vector.scalar_tensor_tensor(fuse[f % 2][:, :], b_up[f % 2][:, :], scales[:, NF + f:NF + f + 1], silu[f % 2][:, :],
                                                   ALU.mult, ALU.mult).then_inc(fuse_done, 1)
                    if i is not None and f == 0:
                        add_y(i, add - 1)
                    if i is not None and f == 2:
                        statistics(i, add - 1)

            round_up(0)
            dve.wait_ge(scales_turned, 1)
            nc.vector.tensor_copy(scales[:, :], b_gate[0][:, 0:2 * NF]).then_inc(scales_ready, 1)
            groups(dve, body)
            add_y(None, NG - 1)
            statistics(None, NG - 1)
            k.ln_chain += NT
            dve.wait_ge(stats_chain, k.ln_chain)

        @block.scalar
        def _(act):
            def body(i, add):
                for f in range(NF):
                    act.wait_ge(gate_made, level(i, add, NF, f + 1))
                    nc.scalar.activation(silu[f % 2][:, :], b_gate[f % 2][:, :], ACT.Silu, scale=scales[:, f:f + 1]).then_inc(silu_done, 1)
                    act.wait_ge(fuse_done, level(i, add, NF, f + 1))
                    nc.scalar.copy(fz[f % 2][0][:, :], fuse[f % 2][:, :]).then_inc(fz_hi, 1)

            act.wait_ge(scales_ready, 1)
            groups(act, body)

        @block.tensor
        def _(pe):
            def down(i, add, f):
                pe.wait_ge(fz_split, level(i, add, NF, f + 1))
                for t in range(TG):
                    if f == 0 and (i is not None or add > 0):
                        pe.wait_ge(y_added, level(i, add, TG, t - TG + 1))
                    for part in fz[f % 2]:
                        mm = nc.tensor.matmul(b_y[t][:, :], part[:, P * t:P * (t + 1)], w[:, f, 2 * D:3 * D],
                                              start=(f == 0 and part is fz[f % 2][0]), stop=(f == NF - 1 and part is fz[f % 2][1]))
                    if f == NF - 1:
                        mm.then_inc(y_made, 1)

            def body(i, add):
                at = slice(0, GT) if i is None else bass.ds(i * GT + add * GT, GT)
                for f in range(NF):
                    if i is not None or f >= 2:
                        pe.wait_ge(fuse_done, level(i, add, NF, f - 1))
                    for n, (out, first, done) in enumerate(((b_gate, 0, gate_made), (b_up, D, up_made))):
                        if i is None:
                            pe.wait_ge(w_ready, 2 * f + n + 1)
                        for c in range(KD):
                            for part in (k.xnT_hi, k.xnT_lo):
                                mm = nc.tensor.matmul(out[f % 2][:, :], w[:, f, first + P * c:first + P * (c + 1)], part[:, c, at],
                                                      start=(c == 0 and part is k.xnT_hi), stop=(c == KD - 1 and part is k.xnT_lo))
                        mm.then_inc(done, 1)
                    if f >= 1:
                        down(i, add, f - 1)
                    elif i is not None:
                        down(i, add - 1, NF - 1)

            pe.wait_ge(scales_in, 48)
            nc.tensor.transpose(b_gate[0][:, 0:2 * NF], scale_rows[:, :], k.ident[0:2 * NF, 0:2 * NF]).then_inc(scales_turned, 1)
            pe.wait_ge(scales_ready, 1)
            groups(pe, body)
            down(None, NG - 1, NF - 1)


def moe_start(k, st, gate_w):
    a = Parts()
    a.gw = st.enter_context(k.nc.sbuf_tensor("moe_gw", [E, D], F32))
    a.gw_in = k.sem("moe_gw_in")
    a.sync = lambda sp: sp.dma_start(a.gw[:, :], gate_w).then_inc(a.gw_in, 16)
    a.scalar, a.gpsimd = lambda act: None, lambda pool: None
    return a


def moe_stage(k, start, xn_rows, gate_up, down_proj, out):
    nc, banks = k.nc, k.banks
    KI = I // P
    HALVES = 2
    ROWS = HALVES * P
    TILES = 2 * T // ROWS + E
    ITER = TILES // 2
    LISTED = TILES + 2
    SLOTS = LISTED * HALVES
    STEPS = 2 * HALVES
    GU, DN = KD * 2 * I, KI * D
    NOWHERE = 65536.0
    ROUND = 1.5 * 2.0 ** 23
    y_rows = nc.dram_tensor("moe_y_rows", (2 * T, D), F32, kind="Internal").ap()
    gu_v = gate_up.rearrange("e (p k) f -> (e p) (k f)", p=P)
    dn_v = down_proj.rearrange("e (p k) n -> (e p) (k n)", p=P)
    with ExitStack() as st:
        def sb(n, shape, dt=F32):
            return st.enter_context(nc.sbuf_tensor(f"moe_{n}", shape, dt))

        def sem(n):
            return k.sem(f"moe_{n}")

        def pair(n, shape):
            return [sb(f"{n}_hi", shape, F32R), sb(f"{n}_lo", shape, F32R)]

        raw_gu, raw_dn = ([sb(f"raw_{n}{i}", [P, c]) for i in range(2)] for n, c in (("gu", GU), ("dn", DN)))
        w_gu, w_dn = ([pair(f"w_{n}{i}", [P, c]) for i in range(2)] for n, c in (("gu", GU), ("dn", DN)))
        rows = [sb(f"rows{i}", [P, D]) for i in range(STEPS)]
        xT = [[x[:, :, P * i:P * (i + 1)] for x in (k.xnT_hi, k.xnT_lo)] for i in range(2)]
        fT = [[x[:, 0:KI, P * (2 + i):P * (3 + i)] for x in (k.xnT_hi, k.xnT_lo)] for i in range(2)]
        silu = [sb(f"silu{i}", [P, I]) for i in range(2)]
        fuse = [sb(f"fuse{i}", [P, I]) for i in range(2)]
        y_sb = [sb(f"y_sb{i}", [P, D]) for i in range(STEPS)]
        gather_at = [sb(f"gather_at{i}", [P, HALVES + 1], I32) for i in range(2)]
        scatter_at = [sb(f"scatter_at{i}", [P, 1], I32) for i in range(STEPS)]
        token_of, dest_of, expert_of = sb("token_of", [P, SLOTS], I32), sb("dest_of", [P, SLOTS], I32), sb("expert_of", [P, LISTED], I32)
        gw, gw_in = start.gw, start.gw_in
        probT = raw_gu[0][0:E, :]
        gwT = pair("gwT", [P, KD, E])
        prob, eq, pick1, pick2, slots = (sb(n, [P, NT, E]) for n in ("prob", "eq", "pick1", "pick2", "slots"))
        both = sb("both", [P, NT, E], F32R)
        before, ones = (sb(n, [P, P], F32R) for n in ("before", "ones"))
        before_f, ones_f, after = sb("before_f", [P, P]), sb("ones_f", [P, P]), sb("after", [P, E, E])
        cum = sb("cum", [P, NT + 1, E])
        need, first_slot, last_tile = (sb(n, [P, E]) for n in ("need", "first_slot", "last_tile"))
        passed = sb("passed", [P, LISTED, E])
        slot, half, row_of = (sb(n, [P, 2, NT]) for n in ("slot", "half", "row_of"))
        table, empty, found = sb("table", [P, SLOTS]), sb("empty", [P, SLOTS]), sb("found", [P, LISTED])
        m1, m2, ms, key = (sb(n, [P, NT]) for n in ("m1", "m2", "ms", "key"))
        counts_i = sb("counts_i", [P, E + P + 2 * NT + 1], I32)
        counts = sb("counts", [P, E + P + 2 * NT + 1])
        rank, column = counts[:, 0:E], counts[:, E:E + P]
        name_of, part = counts[:, E + P:E + P + 2 * NT], counts[:, E + P + 2 * NT:E + P + 2 * NT + 1]

        block = st.enter_context(nc.Block())
        (gw_turned, gw_hi, gw_split, logits_made, sigmoids_made, prob_made, consts_made, route_chain, picked, ranked,
         experts_set, sorted_, tabled, listed) = (
            sem(n) for n in ("gw_turned", "gw_hi", "gw_split", "logits_made", "sigmoids_made", "prob_made", "consts_made", "route_chain",
                             "picked", "ranked", "experts_set", "sorted", "tabled", "listed"))
        gu_in, dn_in, rows_in = ([sem(f"{n}_in{i}") for i in range(2)] for n in ("gu", "dn", "rows"))
        y_out = [sem(f"y_out{i}") for i in range(STEPS)]
        x_turned, x_hi, x_split, wg_hi, wg_split, wd_hi, wd_split = (
            sem(n) for n in ("x_turned", "x_hi", "x_split", "wg_hi", "wg_split", "wd_hi", "wd_split"))
        gu_made, silu_done, fused, f_turned, f_hi, f_split, y_made, y_copied = (
            sem(n) for n in ("gu_made", "silu_done", "fused", "f_turned", "f_hi", "f_split", "y_made", "y_copied"))
        gather_set, scatter_set, pairs_in, summed, stored = (
            sem(n) for n in ("gather_set", "scatter_set", "pairs_in", "summed", "stored"))
        pairs_in = [pairs_in, sem("pairs_in1")]
        b_x, b_gu, b_f, b_y = banks[0:2], banks[2:4], banks[4], banks[5:7]
        FIRST = (None, 0)

        def level(it, per, extra):
            reg, add = it
            return add * per + extra if reg is None else reg * per + (add * per + extra)

        def wait(eng, s, it, per, extra):
            n = level(it, per, extra)
            if it[0] is not None or n > 0:
                eng.wait_ge(s, n)

        def iterations(eng, body):
            body(FIRST)
            with eng.Fori(0, ITER - 1) as i:
                body((i, 1))

        def step(it, s):
            return (it[0], it[1] + s // STEPS), s % STEPS

        def exists(it, s):
            return it is not FIRST or s >= 0

        def one_hots(c):
            space = w_gu[0][c]
            return (space[:, :].rearrange("p (t r) -> p t r", r=P), w_gu[1][c][:, 0:NT * SLOTS].rearrange("p (t j) -> p t j", j=SLOTS))

        @block.sync
        def _(sp):
            for s in range(STEPS):
                sp.wait_ge(y_out[s], 16 * ITER)
            for b in range(2):
                sp.wait_ge(gu_in[b], 16 * (ITER + 1))
                sp.wait_ge(dn_in[b], 16 * (ITER + 1))
                sp.wait_ge(rows_in[b], 32 * (ITER + 1))
            yv = y_rows.rearrange("(t p k) d -> p t (k d)", p=P, k=2)
            ov = out.rearrange("b (t p) d -> p (b t) d", p=P)
            for n in range(NT // 2):
                if n >= 2:
                    sp.wait_ge(summed, 2 * (n - 1))
                sp.dma_start(raw_gu[n % 2][:, :].rearrange("p (t c) -> p t c", t=2), yv[:, 2 * n:2 * (n + 1), :]).then_inc(pairs_in[n % 2], 16)
                if n >= 1:
                    sp.wait_ge(summed, 2 * n)
                    sp.dma_start(ov[:, 2 * (n - 1):2 * n, :], k.x_sb[:, 2 * (n - 1):2 * n, :]).then_inc(stored, 16)
            sp.wait_ge(summed, NT)
            sp.dma_start(ov[:, NT - 2:NT, :], k.x_sb[:, NT - 2:NT, :]).then_inc(stored, 16)
            sp.wait_ge(stored, 16 * NT // 2)

        @block.gpsimd
        def _(pool):
            gp = nc.gpsimd
            gp.iota(counts_i[:, 0:E], pattern=[[-1, E]], base=E, channel_multiplier=0).then_inc(consts_made, 1)
            gp.iota(counts_i[:, E:E + P], pattern=[[1, P]], base=0, channel_multiplier=0).then_inc(consts_made, 1)
            gp.iota(counts_i[:, E + P:E + P + 2 * NT], pattern=[[1, 2], [2 * P, NT]], base=1, channel_multiplier=2).then_inc(consts_made, 1)
            gp.iota(counts_i[:, E + P + 2 * NT:], pattern=[[0, 1]], base=0, channel_multiplier=1).then_inc(consts_made, 1)
            gp.memset(ones_f[:, :], 1.0).then_inc(consts_made, 1)
            gp.memset(after[:, :, :], 1.0).then_inc(consts_made, 1)
            pool.wait_ge(consts_made, 6)
            gp.affine_select(out=before_f[:, :], in_=ones_f[:, :], compare_op=ALU.is_ge, fill=0.0, base=-1,
                             pattern=[[1, P]], channel_multiplier=-1).then_inc(consts_made, 1)
            gp.affine_select(out=after[:, :, :], in_=after[:, :, :], compare_op=ALU.is_ge, fill=0.0, base=0,
                             pattern=[[1, E], [-1, E]], channel_multiplier=0).then_inc(consts_made, 1)
            for r in rows:
                gp.memset(r[:, :], 0.0).then_inc(consts_made, 1)
            pool.wait_ge(consts_made, 8 + STEPS)

            def gather_weights(it, b):
                if it is FIRST:
                    pool.wait_ge(experts_set, b + 1)
                else:
                    wait(pool, gather_set, it, 2, b + 1)
                wait(pool, wg_split, it, 4, 2 * b - 2)
                apart(k, pool)
                at = bass.IndirectOffsetOnAxis(ap=gather_at[b][:, HALVES:HALVES + 1], axis=0)
                gp.indirect_dma_start(raw_gu[b][:, :], None, gu_v, at, bounds_check=E * P - 1, oob_is_err=False).then_inc(gu_in[b], 16)

            def gather_down(it, b):
                wait(pool, wd_split, it, 2, b - 1)
                apart(k, pool)
                at = bass.IndirectOffsetOnAxis(ap=gather_at[b][:, HALVES:HALVES + 1], axis=0)
                gp.indirect_dma_start(raw_dn[b][:, :], None, dn_v, at, bounds_check=E * P - 1, oob_is_err=False).then_inc(dn_in[b], 16)

            def gather_rows(it, b):
                wait(pool, gather_set, it, 2, b + 1)
                wait(pool, x_turned, it, STEPS, HALVES * b - 2)
                apart(k, pool)
                for h in range(HALVES):
                    at = bass.IndirectOffsetOnAxis(ap=gather_at[b][:, h:h + 1], axis=0)
                    gp.indirect_dma_start(rows[HALVES * b + h][:, :], None, xn_rows, at, bounds_check=T - 1,
                                          oob_is_err=False).then_inc(rows_in[b], 16)

            def scatter(it, s):
                wait(pool, scatter_set, it, STEPS, s + 1)
                wait(pool, y_copied, it, STEPS, s + 1)
                apart(k, pool)
                at = bass.IndirectOffsetOnAxis(ap=scatter_at[s][:, :], axis=0)
                gp.indirect_dma_start(y_rows, at, y_sb[s][:, :], None, bounds_check=2 * T - 1, oob_is_err=False).then_inc(y_out[s], 16)

            for b in range(2):
                gather_weights(FIRST, b)
                gather_down(FIRST, b)
            for b in range(2):
                gather_rows(FIRST, b)

            def body(it):
                reg, add = it
                after_it, before_it = (reg, add + 1), (reg, add - 1)
                for b in range(2):
                    gather_weights(after_it, b)
                    gather_rows(after_it, b)
                    gather_down(after_it, b)
                    if b == 1 or it is not FIRST:
                        for h in range(HALVES):
                            scatter(before_it if b == 0 else it, HALVES * (1 - b) + h)

            iterations(pool, body)
            for h in range(HALVES):
                scatter((None, ITER - 1), HALVES + h)

        @block.tensor
        def _(pe):
            pe.wait_ge(gw_in, 16)
            for c in range(KD):
                mm = nc.tensor.transpose(b_y[1][:, E * c:E * (c + 1)], gw[:, P * c:P * (c + 1)], k.ident[0:E, 0:E])
            mm.then_inc(gw_turned, 1)
            pe.wait_ge(gw_split, 1)
            for g in range(NG):
                i = 0
                for c in range(KD):
                    at = slice(GT * g, GT * (g + 1))
                    for a, b in ((gwT[0], k.xnT_hi), (gwT[1], k.xnT_hi), (gwT[0], k.xnT_lo)):
                        mm = nc.tensor.matmul(banks[g][0:E, :], a[:, c, :], b[:, c, at], start=(i == 0), stop=(i == 3 * KD - 1))
                        i += 1
                mm.then_inc(logits_made, 1)
            for t in range(NT):
                if t % TG == 0:
                    pe.wait_ge(sigmoids_made, t // TG + 1)
                mm = nc.tensor.transpose(b_y[0][:, E * t:E * (t + 1)], probT[:, P * t:P * (t + 1)], k.ident[0:E, 0:E])
            mm.then_inc(prob_made, 1)
            pe.wait_ge(picked, 1)
            chosen = both[:, :, :].rearrange("p t e -> p (t e)")
            nc.tensor.matmul(b_gu[1][:, 0:NT * E], before[:, :], chosen, start=True, stop=True)
            nc.tensor.matmul(b_gu[0][:, 0:NT * E], ones[:, :], chosen, start=True, stop=True).then_inc(ranked, 1)
            for c in range(2):
                pe.wait_ge(sorted_, c + 1)
                for t in range(NT):
                    mm = nc.tensor.matmul(b_y[1][:, 0:SLOTS], one_hots(c)[0][:, t, :], one_hots(c)[1][:, t, :],
                                          start=(c == 0 and t == 0), stop=(c == 1 and t == NT - 1))
            mm.then_inc(tabled, 1)

            def turn_x(it, s):
                if s % HALVES == 0:
                    wait(pe, rows_in[s // HALVES], it, 32, 32)
                wait(pe, x_split, it, STEPS, s - 1)
                by_feature = rows[s][:, :].rearrange("p (q k) -> p k q", k=KD)
                for c in range(KD):
                    mm = nc.tensor.transpose(b_x[s % 2][:, P * c:P * (c + 1)], by_feature[:, c, :], k.ident[:, :])
                mm.then_inc(x_turned, 1)

            def gate_up_products(it, s):
                b = s // HALVES
                if s % HALVES == 0:
                    wait(pe, wg_split, it, 4, 2 * (b + 1))
                wait(pe, x_split, it, STEPS, s + 1)
                wait(pe, fused, it, STEPS, s - 1)
                j = 0
                for c in range(KD):
                    for x, w in ((0, 0), (0, 1), (1, 0)):
                        mm = nc.tensor.matmul(b_gu[s % 2][:, :], xT[s % 2][x][:, c, :], w_gu[b][w][:, 2 * I * c:2 * I * (c + 1)],
                                              start=(j == 0), stop=(j == 3 * KD - 1))
                        j += 1
                mm.then_inc(gu_made, 1)

            def turn_f(it, s):
                wait(pe, fused, it, STEPS, s + 1)
                wait(pe, f_split, it, STEPS, s)
                by_feature = fuse[s % 2][:, :].rearrange("p (q k) -> p k q", k=KI)
                for c in range(KI):
                    mm = nc.tensor.transpose(b_f[:, P * c:P * (c + 1)], by_feature[:, c, :], k.ident[:, :])
                mm.then_inc(f_turned, 1)

            def down(it, s):
                b = s // HALVES
                if s % HALVES == 0:
                    wait(pe, wd_split, it, 2, b + 1)
                wait(pe, f_split, it, STEPS, s + 1)
                wait(pe, y_copied, it, STEPS, s - 1)
                j = 0
                for c in range(KI):
                    for f, w in ((0, 0), (0, 1), (1, 0)):
                        mm = nc.tensor.matmul(b_y[s % 2][:, :], fT[s % 2][f][:, c, :], w_dn[b][w][:, D * c:D * (c + 1)],
                                              start=(j == 0), stop=(j == 3 * KI - 1))
                        j += 1
                mm.then_inc(y_made, 1)

            pe.wait_ge(listed, 1)
            turn_x(FIRST, 0)

            def body(it):
                for s in range(STEPS):
                    turn_x(*step(it, s + 1))
                    gate_up_products(it, s)
                    if exists(it, s - 1):
                        turn_f(*step(it, s - 1))
                    if exists(it, s - 2):
                        down(*step(it, s - 2))

            iterations(pe, body)
            end = (None, ITER)
            turn_f(*step(end, -1))
            down(*step(end, -2))
            down(*step(end, -1))

        @block.scalar
        def _(act):
            act.wait_ge(gw_turned, 1)
            nc.scalar.copy(gwT[0][:, :, :].rearrange("p k e -> p (k e)"), b_y[1][:, 0:KD * E]).then_inc(gw_hi, 1)
            for g in range(NG):
                act.wait_ge(logits_made, g + 1)
                nc.scalar.activation(probT[:, GT * g:GT * (g + 1)], banks[g][0:E, :], ACT.Sigmoid).then_inc(sigmoids_made, 1)

            def copy_x(it, s):
                wait(act, x_turned, it, STEPS, s + 1)
                wait(act, gu_made, it, STEPS, s - 1)
                nc.scalar.copy(xT[s % 2][0], b_x[s % 2][:, :].rearrange("p (k t) -> p k t", k=KD)).then_inc(x_hi, 1)

            def weights_gate_up(it, b, c):
                cols = slice(GU // 2 * c, GU // 2 * (c + 1))
                if c == 0:
                    wait(act, gu_in[b], it, 16, 16)
                    wait(act, gu_made, it, STEPS, HALVES * b - 2)
                nc.scalar.copy(w_gu[b][0][:, cols], raw_gu[b][:, cols]).then_inc(wg_hi, 1)

            def weights_down(it, b):
                wait(act, dn_in[b], it, 16, 16)
                wait(act, y_made, it, STEPS, HALVES * b - 2)
                nc.scalar.copy(w_dn[b][0][:, :], raw_dn[b][:, :]).then_inc(wd_hi, 1)

            def gate(it, s):
                wait(act, gu_made, it, STEPS, s + 1)
                wait(act, fused, it, STEPS, s - 1)
                nc.scalar.activation(silu[s % 2][:, :], b_gu[s % 2][:, 0:I], ACT.Silu).then_inc(silu_done, 1)

            def copy_f(it, s):
                wait(act, f_turned, it, STEPS, s + 1)
                wait(act, y_made, it, STEPS, s - 1)
                nc.scalar.copy(fT[s % 2][0], b_f[:, 0:I].rearrange("p (k t) -> p k t", k=KI)).then_inc(f_hi, 1)

            def copy_y(it, s):
                wait(act, y_made, it, STEPS, s + 1)
                wait(act, y_out[s], it, 16, 0)
                nc.scalar.copy(y_sb[s][:, :], b_y[s % 2][:, :]).then_inc(y_copied, 1)

            act.wait_ge(tabled, 1)
            for c in range(2):
                weights_gate_up(FIRST, 0, c)
            copy_x(FIRST, 0)

            def body(it):
                for s in range(STEPS):
                    b = s // HALVES
                    copy_x(*step(it, s + 1))
                    nxt = step(it, HALVES * (b + 1))
                    weights_gate_up(nxt[0], 1 - b, s % HALVES)
                    if s % HALVES == 0:
                        weights_down(it, b)
                    gate(it, s)
                    if exists(it, s - 1):
                        copy_f(*step(it, s - 1))
                    if exists(it, s - 2):
                        copy_y(*step(it, s - 2))

            iterations(act, body)
            end = (None, ITER)
            copy_f(*step(end, -1))
            copy_y(*step(end, -2))
            copy_y(*step(end, -1))

        @block.vector
        def _(dve):
            v = nc.vector
            dve.wait_ge(gw_hi, 1)
            v.tensor_tensor(gwT[1][:, :, :].rearrange("p k e -> p (k e)"), b_y[1][:, 0:KD * E],
                            gwT[0][:, :, :].rearrange("p k e -> p (k e)").bitcast(F32), ALU.subtract).then_inc(gw_split, 1)
            done = [0]

            def chain(ins):
                ins.then_inc(route_chain, 1)
                done[0] += 1
                dve.wait_ge(route_chain, done[0])

            def over_e(a):
                return a.rearrange("p (t o) -> p t o", o=1).broadcast_to([P, NT, E])

            def over_t(a, n=NT):
                return a.rearrange("p (o e) -> p o e", o=1).broadcast_to([P, n, E])

            def pick(best, chosen):
                chain(v.tensor_reduce(best[:, :], prob[:, :, :], AX.X, ALU.max))
                chain(v.tensor_tensor(eq[:, :, :], prob[:, :, :], over_e(best[:, :]), ALU.is_equal))
                chain(v.tensor_tensor(eq[:, :, :], eq[:, :, :], over_t(rank), ALU.mult))
                chain(v.tensor_reduce(key[:, :], eq[:, :, :], AX.X, ALU.max))
                chain(v.tensor_tensor(chosen[:, :, :], eq[:, :, :], over_e(key[:, :]), ALU.is_equal))

            def rounded(out, a, scale, offset):
                chain(v.tensor_scalar(out, a, scale, offset, ALU.mult, ALU.add))
                chain(v.tensor_scalar(out, out, ROUND, None, ALU.add))
                chain(v.tensor_scalar(out, out, -ROUND, None, ALU.add))

            dve.wait_ge(consts_made, 8)
            v.tensor_copy(before[:, :], before_f[:, :])
            v.tensor_copy(ones[:, :], ones_f[:, :])
            chain(v.tensor_copy(counts[:, :], counts_i[:, :]))
            dve.wait_ge(prob_made, 1)
            chain(v.tensor_copy(prob[:, :, :].rearrange("p t e -> p (t e)"), b_y[0][:, 0:NT * E]))
            chain(v.tensor_reduce(ms[:, :], prob[:, :, :], AX.X, ALU.add))
            chain(v.reciprocal(ms[:, :], ms[:, :]))
            chain(v.tensor_tensor(prob[:, :, :], prob[:, :, :], over_e(ms[:, :]), ALU.mult))
            pick(m1, pick1)
            chain(v.scalar_tensor_tensor(prob[:, :, :], pick1[:, :, :], -4.0, prob[:, :, :], ALU.mult, ALU.add))
            pick(m2, pick2)
            v.tensor_tensor(both[:, :, :], pick1[:, :, :], pick2[:, :, :], ALU.add).then_inc(picked, 1)
            chain(v.tensor_tensor(ms[:, :], m1[:, :], m2[:, :], ALU.add))
            chain(v.reciprocal(ms[:, :], ms[:, :]))
            chain(v.tensor_tensor(m1[:, :], m1[:, :], ms[:, :], ALU.mult))
            chain(v.tensor_tensor(m2[:, :], m2[:, :], ms[:, :], ALU.mult))
            chain(v.memset(cum[:, 0, :], 0.0))
            dve.wait_ge(ranked, 1)
            for t in range(NT):
                chain(v.tensor_tensor(cum[:, t + 1, :], b_gu[0][:, E * t:E * (t + 1)], cum[:, t, :], ALU.add))
            rounded(need[:, :], cum[:, NT, :], 1.0 / ROWS, (ROWS - 1) / 2 / ROWS)
            spread = eq[:, 0:E, :]
            chain(v.tensor_tensor(spread, after[:, :, :], over_t(need[:, :], E), ALU.mult))
            chain(v.tensor_reduce(last_tile[:, :], spread, AX.X, ALU.add))
            chain(v.tensor_tensor(first_slot[:, :], last_tile[:, :], need[:, :], ALU.subtract))
            chain(v.tensor_scalar(first_slot[:, :], first_slot[:, :], float(ROWS), None, ALU.mult))
            tiles = column[:, 0:LISTED].rearrange("p (j o) -> p j o", o=1).broadcast_to([P, LISTED, E])
            chain(v.tensor_tensor(passed[:, :, :], tiles, over_t(last_tile[:, :], LISTED), ALU.is_ge))
            chain(v.tensor_reduce(found[:, :], passed[:, :, :], AX.X, ALU.add))
            chain(v.tensor_scalar(found[:, :], found[:, :], float(P), part, ALU.mult, ALU.add))
            chain(v.tensor_copy(expert_of[:, :], found[:, :]))
            for b in range(2):
                v.tensor_copy(gather_at[b][:, HALVES:HALVES + 1], expert_of[:, b:b + 1]).then_inc(experts_set, 1)
            chain(v.tensor_tensor(slots[:, :, :], b_gu[1][:, 0:NT * E].rearrange("p (t e) -> p t e", e=E), cum[:, 0:NT, :], ALU.add))
            chain(v.tensor_tensor(slots[:, :, :], slots[:, :, :], over_t(first_slot[:, :]), ALU.add))
            for c, chosen in enumerate((pick1, pick2)):
                chain(v.tensor_tensor(eq[:, :, :], chosen[:, :, :], slots[:, :, :], ALU.mult))
                chain(v.tensor_reduce(slot[:, c, :], eq[:, :, :], AX.X, ALU.add))
            rounded(half[:, :, :], slot[:, :, :], 1.0 / P, -(P - 1) / 2 / P)
            chain(v.scalar_tensor_tensor(row_of[:, :, :], half[:, :, :], -float(P), slot[:, :, :], ALU.mult, ALU.add))
            for c in range(2):
                def wide(a, n):
                    return a.rearrange("p (t o) -> p t o", o=1).broadcast_to([P, NT, n])

                def columns(n):
                    return column[:, 0:n].rearrange("p (o j) -> p o j", o=1).broadcast_to([P, NT, n])

                by_row, by_half = one_hots(c)
                chain(v.tensor_tensor(by_row, columns(P), wide(row_of[:, c, :], P), ALU.is_equal))
                chain(v.tensor_tensor(by_half, columns(SLOTS), wide(half[:, c, :], SLOTS), ALU.is_equal))
                v.tensor_tensor(by_half, by_half.bitcast(F32), wide(name_of[:, NT * c:NT * (c + 1)], SLOTS), ALU.mult).then_inc(sorted_, 1)
            dve.wait_ge(tabled, 1)
            chain(v.tensor_scalar(empty[:, :], b_y[1][:, 0:SLOTS], 0.0, NOWHERE, ALU.is_equal, ALU.mult))
            chain(v.scalar_tensor_tensor(table[:, :], b_y[1][:, 0:SLOTS], -1.0, empty[:, :], ALU.add, ALU.add))
            chain(v.tensor_copy(dest_of[:, :], table[:, :]))
            rounded(table[:, :], table[:, :], 0.5, -0.25)
            v.tensor_copy(token_of[:, :], table[:, :]).then_inc(listed, 1)
            dve.wait_ge(listed, 1)

            def set_gather(it, b):
                wait(dve, dn_in[b], it, 16, 0)
                wait(dve, gu_in[b], it, 16, 0)
                wait(dve, rows_in[b], it, 32, 0)
                reg, add = it
                tile = 2 * add + b
                half_at = slice(HALVES * tile, HALVES * (tile + 1)) if reg is None else bass.ds(reg * STEPS + HALVES * tile, HALVES)
                tile_at = slice(tile, tile + 1) if reg is None else bass.ds(reg * 2 + tile, 1)
                if it is not FIRST:
                    v.tensor_copy(gather_at[b][:, HALVES:HALVES + 1], expert_of[:, tile_at])
                v.tensor_copy(gather_at[b][:, 0:HALVES], token_of[:, half_at]).then_inc(gather_set, 1)

            def set_scatter(it, s):
                wait(dve, y_out[s], it, 16, 0)
                reg, add = it
                at = slice(STEPS * add + s, STEPS * add + s + 1) if reg is None else bass.ds(reg * STEPS + (STEPS * add + s), 1)
                v.tensor_copy(scatter_at[s][:, :], dest_of[:, at]).then_inc(scatter_set, 1)

            def lo_x(it, s):
                wait(dve, x_hi, it, STEPS, s + 1)
                v.tensor_tensor(xT[s % 2][1], b_x[s % 2][:, :].rearrange("p (k t) -> p k t", k=KD),
                                xT[s % 2][0].bitcast(F32), ALU.subtract).then_inc(x_split, 1)

            def lo_gate_up(it, b, c):
                cols = slice(GU // 2 * c, GU // 2 * (c + 1))
                wait(dve, wg_hi, it, 4, 2 * b + c + 1)
                v.tensor_tensor(w_gu[b][1][:, cols], raw_gu[b][:, cols], w_gu[b][0][:, cols].bitcast(F32), ALU.subtract).then_inc(wg_split, 1)

            def lo_down(it, b):
                wait(dve, wd_hi, it, 2, b + 1)
                v.tensor_tensor(w_dn[b][1][:, :], raw_dn[b][:, :], w_dn[b][0][:, :].bitcast(F32), ALU.subtract).then_inc(wd_split, 1)

            def fuse_up(it, s):
                wait(dve, silu_done, it, STEPS, s + 1)
                wait(dve, f_turned, it, STEPS, s - 1)
                v.tensor_tensor(fuse[s % 2][:, :], b_gu[s % 2][:, I:2 * I], silu[s % 2][:, :], ALU.mult).then_inc(fused, 1)

            def lo_f(it, s):
                wait(dve, f_hi, it, STEPS, s + 1)
                v.tensor_tensor(fT[s % 2][1], b_f[:, 0:I].rearrange("p (k t) -> p k t", k=KI),
                                fT[s % 2][0].bitcast(F32), ALU.subtract).then_inc(f_split, 1)

            for b in range(2):
                set_gather(FIRST, b)
            for c in range(2):
                lo_gate_up(FIRST, 0, c)
            lo_x(FIRST, 0)

            def body(it):
                for s in range(STEPS):
                    b = s // HALVES
                    lo_x(*step(it, s + 1))
                    nxt = step(it, HALVES * (b + 1))
                    lo_gate_up(nxt[0], 1 - b, s % HALVES)
                    if s % HALVES == 0:
                        lo_down(it, b)
                        set_gather((it[0], it[1] + 1), b)
                    set_scatter(it, s)
                    fuse_up(it, s)
                    if exists(it, s - 1):
                        lo_f(*step(it, s - 1))

            iterations(dve, body)
            lo_f(*step((None, ITER), -1))

            for t in range(NT):
                n = t // 2
                if t % 2 == 0:
                    dve.wait_ge(pairs_in[n % 2], 16 * (n // 2 + 1))
                for c, weight in enumerate((m1, m2)):
                    y = raw_gu[n % 2][:, D * (2 * (t % 2) + c):D * (2 * (t % 2) + c + 1)]
                    row = k.x_sb[:, t, :]
                    ins = v.scalar_tensor_tensor(row, y, weight[:, t:t + 1], row, ALU.mult, ALU.add)
                    ins.then_inc(*((route_chain, 1) if c == 0 else (summed, 1)))
                    if c == 0:
                        done[0] += 1
                        dve.wait_ge(route_chain, done[0])


def decoder_layers(nc, x, ctx_1024, mask, w0, f0, w1, m1, out):
    with ExitStack() as st:
        k = Parts()
        k.nc = nc
        k.sem = lambda n: st.enter_context(nc.semaphore(n))
        k.banks = [st.enter_context(nc.psum_tensor(f"bank{i}", [P, 512], F32)) for i in range(8)]
        k.x_sb = st.enter_context(nc.sbuf_tensor("x_sb", [P, NT, D], F32))
        k.xnT_hi = st.enter_context(nc.sbuf_tensor("xnT_hi", [P, KD, T], F32R))
        k.xnT_lo = st.enter_context(nc.sbuf_tensor("xnT_lo", [P, KD, T], F32R))
        k.ident = st.enter_context(nc.sbuf_tensor("ident", [P, P], F32))
        k.ctx_split = nc.dram_tensor("ctx_split", (NG, P, 2 * KC * GT), F32, kind="Internal").ap()
        k.ln_calls, k.ln_chain = 0, 0
        k.x_in, k.ctx_stored = [k.sem(f"x_in{i}") for i in range(2)], k.sem("ctx_stored")
        k.stats = st.enter_context(nc.sbuf_tensor("ln_stats", [P, NT, 6], F32))
        k.ident_made, k.wait_over = k.sem("ident_made"), k.sem("wait_over")
        k.ln_sems = [k.sem(f"ln_{n}") for n in ("chain", "normed", "act_normed", "turned", "hi_done", "lo_done")]
        with ExitStack() as ahead:
            start = attention_start(k, ahead, "l0", *w0[:3], rms=False)
            with ExitStack() as early:
                k.ct = [early.enter_context(nc.sbuf_tensor(f"ct{g}", [P, 2, KC, GT], F32R)) for g in range(NG)]
                load_stage(k, x, ctx_1024)
                layernorm_stage(k, start)
            attention_stage(k, "l0", start, w0[3], mask=mask)
        with ExitStack() as ahead:
            start = ffn_start(k, ahead, *f0)
            layernorm_stage(k, start, stats_made=True)
            ffn_stage(k, start)
        with ExitStack() as ahead:
            start = attention_start(k, ahead, "l1", *w1[:3], rms=True)
            layernorm_stage(k, start, stats_made=True)
            attention_stage(k, "l1", start, w1[3], gq=w1[4], gk=w1[5])
        with ExitStack() as ahead:
            xn_rows = nc.dram_tensor("xn_rows", (T, D), F32, kind="Internal").ap()
            start = moe_start(k, ahead, m1[0])
            layernorm_stage(k, start, rows=xn_rows, stats_made=True)
            moe_stage(k, start, xn_rows, *m1[1:], out)


_INS = ["x", "ctx_1024", "mask_BxS2_bf1", "L0_xattn_Wq", "L0_xattn_Wk", "L0_xattn_Wv", "L0_xattn_Wo", "L0_ffn_gate_w",
        "L0_ffn_up_w", "L0_ffn_down_w", "L0_ffn_gate_scale", "L0_ffn_up_scale", "L0_ffn_down_scale", "L1_xattn_Wq",
        "L1_xattn_Wk", "L1_xattn_Wv", "L1_xattn_Wo", "L1_xattn_gq", "L1_xattn_gk", "L1_ffn_gate_w", "L1_ffn_gate_up_proj",
        "L1_ffn_down_proj"]


def kernel(**inputs):
    import concourse.bacc as bacc
    import numpy as np
    from concourse.bass_utils import run_bass_kernel_spmd as run

    nc = bacc.Bacc("TRN2", target_bir_lowering=False, num_devices=1)
    arrays, aps = {}, []
    for name in _INS:
        a = np.ascontiguousarray(inputs[name])
        if a.dtype == np.bool_:
            a = a.view(np.uint8)
        arrays[f"in_{name}"] = a
        aps.append(nc.dram_tensor(f"in_{name}", a.shape, mybir.dt.from_np(a.dtype), kind="ExternalInput").ap())
    out = nc.dram_tensor("out_x", (B, S, D), F32, kind="ExternalOutput").ap()
    decoder_layers(nc, aps[0], aps[1], aps[2], aps[3:7], aps[7:13], aps[13:19], aps[19:22], out)
    return run(nc, [arrays], core_ids=[0]).results[0]["out_x"]
```
